# Optimizing a Trainium2 kernel written in Bass

```python
import numpy as np
import jax
import jax.numpy as jnp

def _softmax(x, axis=-1):
    return jax.nn.softmax(x, axis=axis)

def _gelu(x):
    return jax.nn.gelu(x, approximate=True)

def _silu(x):
    return jax.nn.silu(x)

def _sigmoid(x):
    return jax.nn.sigmoid(x)

def _layernorm(x, axis=-1, eps=1e-05):
    m = jnp.mean(x, axis=axis, keepdims=True)
    v = jnp.var(x, axis=axis, keepdims=True)
    return (x - m) / jnp.sqrt(v + eps)

def _scatter_add(tgt, idx, src, axis=0):
    return tgt.at[idx].add(src)

def _segment_sum(src, seg, n):
    return jax.ops.segment_sum(src, seg, n)
kernel_name = 'mk_seq_preln_d2_jaxref_r8_526a00'

def setup_inputs(seed: int=0):
    np.random.seed(seed)
    _w = jnp.asarray

    def _L0_attn_setup():
        import jax, jax.numpy as jnp
        import numpy as np
        B, S, HID = (1, 512, 256)
        NH, NKV, D = (16, 4, 128)
        QPG = NH // NKV
        GROUP = (QPG + 2) * D
        TOTAL = NKV * GROUP
        key = jax.random.key(seed)
        k0, k1, k2 = jax.random.split(key, 3)
        x = jax.random.normal(k0, (B, S, HID), dtype=jnp.float32)
        weight_qkv = jax.random.normal(k1, (TOTAL, HID), dtype=jnp.float32) * 0.02
        weight_proj = jax.random.normal(k2, (HID, NH * D), dtype=jnp.float32) * 0.02
        return {'x': x, 'weight_qkv': weight_qkv, 'weight_proj': weight_proj}
    _L0_attn_in = _L0_attn_setup()

    def _L0_ffn_setup():
        import jax, jax.numpy as jnp
        import numpy as np
        LN_EPS = 1e-05
        Q_EPS = 1e-05

        def ternary_quantize(w):
            scale = jnp.mean(jnp.abs(w))
            return jnp.clip(jnp.round(w / (scale + Q_EPS)), -1.0, 1.0)

        def layernorm(x, gamma, beta):
            mu = jnp.mean(x, axis=-1, keepdims=True)
            var = jnp.mean(jnp.square(x - mu), axis=-1, keepdims=True)
            return (x - mu) * jax.lax.rsqrt(var + LN_EPS) * gamma + beta
        key = jax.random.key(seed)
        k_x, k_w = jax.random.split(key)
        B, S, D_IN, D_OUT = (4, 256, 256, 256)
        x = jax.random.normal(k_x, (B, S, D_IN), dtype=jnp.float32)
        std = np.sqrt(2.0 / D_OUT).astype(np.float32)
        weight = jax.random.normal(k_w, (D_OUT, D_IN), dtype=jnp.float32) * std
        bias = jnp.zeros((D_OUT,), dtype=jnp.float32)
        ln_gamma = jnp.ones((D_IN,), dtype=jnp.float32)
        ln_beta = jnp.zeros((D_IN,), dtype=jnp.float32)
        return {'x': x, 'weight': weight, 'bias': bias, 'ln_gamma': ln_gamma, 'ln_beta': ln_beta}
    _L0_ffn_in = _L0_ffn_setup()

    def _L1_attn_setup():
        import jax, jax.numpy as jnp
        import numpy as np
        ROPE_THETA = 10000.0

        def rope(t, rot_dim):
            S = t.shape[-2]
            half = rot_dim // 2
            inv_freq = 1.0 / ROPE_THETA ** (jnp.arange(0, rot_dim, 2, dtype=jnp.float32) / rot_dim)
            freqs = jnp.arange(S, dtype=jnp.float32)[:, None] * inv_freq[None, :]
            freqs = jnp.repeat(freqs, 2, axis=-1)
            cos, sin = (jnp.cos(freqs), jnp.sin(freqs))
            t_rot, t_pass = (t[..., :rot_dim], t[..., rot_dim:])
            x = t_rot.reshape(*t_rot.shape[:-1], half, 2)
            rh = jnp.stack([-x[..., 1], x[..., 0]], axis=-1).reshape(t_rot.shape)
            t_rot = t_rot * cos + rh * sin
            return jnp.concatenate([t_rot, t_pass], axis=-1)

        def feature_map(x):
            norm = jnp.sqrt(jnp.sum(x * x, axis=-1, keepdims=True))
            return x / jnp.maximum(norm, 1e-12)
        key = jax.random.key(seed)
        kx, kwi, kwo = jax.random.split(key, 3)
        B, S, D = (8, 512, 256)
        scale = 0.02
        return {'X': jax.random.normal(kx, (B, S, D), dtype=jnp.float32), 'W_in': jax.random.normal(kwi, (3 * D, D), dtype=jnp.float32) * scale, 'b_in': jnp.zeros((3 * D,), dtype=jnp.float32), 'W_out': jax.random.normal(kwo, (D, D), dtype=jnp.float32) * scale, 'b_out': jnp.zeros((D,), dtype=jnp.float32)}
    _L1_attn_in = _L1_attn_setup()

    def _L1_ffn_setup():
        import jax, jax.numpy as jnp
        import numpy as np
        DIM = 256
        HID = 704
        ZERO_POINT = 128.0

        def _qlinear(x, wq, scale):
            W = (wq.astype(jnp.float32) - ZERO_POINT) * scale[:, None]
            return jnp.einsum('bsd,hd->bsh', x, W)
        key = jax.random.key(seed)
        ks = jax.random.split(key, 7)
        B, S = (4, 256)
        sg = jax.random.uniform(ks[1], (HID,)) * (0.02 / np.sqrt(DIM)) + 0.0001
        su = jax.random.uniform(ks[3], (HID,)) * (0.02 / np.sqrt(DIM)) + 0.0001
        sd = jax.random.uniform(ks[5], (DIM,)) * (0.02 / np.sqrt(HID)) + 0.0001
        return {'x': jax.random.normal(ks[0], (B, S, DIM), dtype=jnp.float32), 'wq_gate': jax.random.randint(ks[2], (HID, DIM), 0, 32, dtype=jnp.int32), 's_gate': sg, 'wq_up': jax.random.randint(ks[4], (HID, DIM), 0, 32, dtype=jnp.int32), 's_up': su, 'wq_down': jax.random.randint(ks[6], (DIM, HID), 0, 32, dtype=jnp.int32), 's_down': sd}
    _L1_ffn_in = _L1_ffn_setup()
    _d = {'L0_attn_x': _L0_attn_in['x'], 'L0_attn_weight_qkv': _L0_attn_in['weight_qkv'], 'L0_attn_weight_proj': _L0_attn_in['weight_proj'], 'L0_ffn_weight': _L0_ffn_in['weight'], 'L0_ffn_bias': _L0_ffn_in['bias'], 'L0_ffn_ln_gamma': _L0_ffn_in['ln_gamma'], 'L0_ffn_ln_beta': _L0_ffn_in['ln_beta'], 'L1_attn_W_in': _L1_attn_in['W_in'], 'L1_attn_b_in': _L1_attn_in['b_in'], 'L1_attn_W_out': _L1_attn_in['W_out'], 'L1_attn_b_out': _L1_attn_in['b_out'], 'L1_ffn_wq_gate': _L1_ffn_in['wq_gate'], 'L1_ffn_s_gate': _L1_ffn_in['s_gate'], 'L1_ffn_wq_up': _L1_ffn_in['wq_up'], 'L1_ffn_s_up': _L1_ffn_in['s_up'], 'L1_ffn_wq_down': _L1_ffn_in['wq_down'], 'L1_ffn_s_down': _L1_ffn_in['s_down']}
    _x0 = _d['L0_attn_x']
    _d['L0_attn_x'] = jax.random.normal(jax.random.fold_in(jax.random.key(seed), 1), (8, 256, 256), dtype=_x0.dtype)
    del _x0
    return _d

def reference(L0_attn_x, L0_attn_weight_qkv, L0_attn_weight_proj, L0_ffn_weight, L0_ffn_bias, L0_ffn_ln_gamma, L0_ffn_ln_beta, L1_attn_W_in, L1_attn_b_in, L1_attn_W_out, L1_attn_b_out, L1_ffn_wq_gate, L1_ffn_s_gate, L1_ffn_wq_up, L1_ffn_s_up, L1_ffn_wq_down, L1_ffn_s_down):

    def _L0_attn_ref(x, weight_qkv, weight_proj):
        import jax, jax.numpy as jnp
        import numpy as np
        B, S, HID = (1, 512, 256)
        NH, NKV, D = (16, 4, 128)
        QPG = NH // NKV
        GROUP = (QPG + 2) * D
        TOTAL = NKV * GROUP
        b, s, _ = x.shape
        qkv = jnp.einsum('bsh,ph->bsp', x, weight_qkv).reshape(b, s, NKV, GROUP)
        q = qkv[..., :QPG * D].reshape(b, s, NKV, QPG, D)
        k = qkv[..., QPG * D:(QPG + 1) * D]
        v = qkv[..., (QPG + 1) * D:]
        scale = 1.0 / jnp.sqrt(jnp.float32(D))
        scores = jnp.einsum('bsgqd,btgd->bgqst', q, k) * scale
        causal = jnp.tril(jnp.ones((s, s), dtype=bool))
        scores = jnp.where(causal, scores, jnp.finfo(scores.dtype).min)
        attn = jax.nn.softmax(scores, axis=-1)
        out = jnp.einsum('bgqst,btgd->bsgqd', attn, v)
        out = out.reshape(b, s, NH * D)
        return jnp.einsum('bse,he->bsh', out, weight_proj)

    def _L0_ffn_ref(x, weight, bias, ln_gamma, ln_beta):
        import jax, jax.numpy as jnp
        import numpy as np
        LN_EPS = 1e-05
        Q_EPS = 1e-05

        def ternary_quantize(w):
            scale = jnp.mean(jnp.abs(w))
            return jnp.clip(jnp.round(w / (scale + Q_EPS)), -1.0, 1.0)

        def layernorm(x, gamma, beta):
            mu = jnp.mean(x, axis=-1, keepdims=True)
            var = jnp.mean(jnp.square(x - mu), axis=-1, keepdims=True)
            return (x - mu) * jax.lax.rsqrt(var + LN_EPS) * gamma + beta
        xn = layernorm(x, ln_gamma, ln_beta)
        w_q = ternary_quantize(weight)
        return jnp.einsum('bsi,oi->bso', xn, w_q) + bias

    def _L1_attn_ref(X, W_in, b_in, W_out, b_out):
        import jax, jax.numpy as jnp
        import numpy as np
        ROPE_THETA = 10000.0

        def rope(t, rot_dim):
            S = t.shape[-2]
            half = rot_dim // 2
            inv_freq = 1.0 / ROPE_THETA ** (jnp.arange(0, rot_dim, 2, dtype=jnp.float32) / rot_dim)
            freqs = jnp.arange(S, dtype=jnp.float32)[:, None] * inv_freq[None, :]
            freqs = jnp.repeat(freqs, 2, axis=-1)
            cos, sin = (jnp.cos(freqs), jnp.sin(freqs))
            t_rot, t_pass = (t[..., :rot_dim], t[..., rot_dim:])
            x = t_rot.reshape(*t_rot.shape[:-1], half, 2)
            rh = jnp.stack([-x[..., 1], x[..., 0]], axis=-1).reshape(t_rot.shape)
            t_rot = t_rot * cos + rh * sin
            return jnp.concatenate([t_rot, t_pass], axis=-1)

        def feature_map(x):
            norm = jnp.sqrt(jnp.sum(x * x, axis=-1, keepdims=True))
            return x / jnp.maximum(norm, 1e-12)
        D = X.shape[-1]
        QKV = jnp.einsum('bsd,ed->bse', X, W_in) + b_in
        Q, K, V = jnp.split(QKV, 3, axis=-1)
        rot_dim = D // 2
        Q = rope(Q, rot_dim)
        K = rope(K, rot_dim)
        A = jnp.sum(feature_map(K) * V, axis=-2)
        Y = A[:, None, :] * Q
        Y = jnp.einsum('bsd,ed->bse', Y, W_out) + b_out
        return Y + X

    def _L1_ffn_ref(x, wq_gate, s_gate, wq_up, s_up, wq_down, s_down):
        import jax, jax.numpy as jnp
        import numpy as np
        DIM = 256
        HID = 704
        ZERO_POINT = 128.0

        def _qlinear(x, wq, scale):
            W = (wq.astype(jnp.float32) - ZERO_POINT) * scale[:, None]
            return jnp.einsum('bsd,hd->bsh', x, W)
        gate = _qlinear(x, wq_gate, s_gate)
        gate = jax.nn.silu(gate)
        up = _qlinear(x, wq_up, s_up)
        return _qlinear(gate * up, wq_down, s_down)
    x = L0_attn_x
    x = x + _L0_attn_ref(_layernorm(x, axis=-1), L0_attn_weight_qkv, L0_attn_weight_proj)
    x = x + _L0_ffn_ref(_layernorm(x, axis=-1), L0_ffn_weight, L0_ffn_bias, L0_ffn_ln_gamma, L0_ffn_ln_beta)
    x = x + _L1_attn_ref(_layernorm(x, axis=-1), L1_attn_W_in, L1_attn_b_in, L1_attn_W_out, L1_attn_b_out)
    x = x + _L1_ffn_ref(_layernorm(x, axis=-1), L1_ffn_wq_gate, L1_ffn_s_gate, L1_ffn_wq_up, L1_ffn_s_up, L1_ffn_wq_down, L1_ffn_s_down)
    return x

_drawn_inputs = setup_inputs


def setup_inputs(seed=0):
    import zlib

    import numpy as np

    out = dict(_drawn_inputs(seed))
    spreads = {'L0_ffn_bias': (0.0, 0.8),
     'L0_ffn_ln_gamma': (1.0, 0.2),
     'L0_ffn_ln_beta': (0.0, 0.1),
     'L1_attn_b_in': (0.0, 0.8),
     'L1_attn_b_out': (0.0, 2.0)}
    factors = {'L1_attn_W_in': 8.0,
     'L1_attn_W_out': 8.0,
     'L1_ffn_s_gate': 8.0,
     'L1_ffn_s_up': 8.0,
     'L1_ffn_s_down': 8.0}
    for name, (base, spread) in spreads.items():
        noise = np.random.default_rng([zlib.crc32(name.encode()), seed]).standard_normal(out[name].shape)
        drawn = base * np.exp(spread * noise) if base else spread * noise
        out[name] = jnp.asarray(drawn.astype(out[name].dtype))
    for name, factor in factors.items():
        out[name] = (out[name] * factor).astype(out[name].dtype)
    return out
```

```python
from contextlib import ExitStack

import numpy as np

import concourse.bass as bass
from concourse import mybir

F32 = mybir.dt.float32
F32R = mybir.dt.float32r
I32 = mybir.dt.int32
ALU = mybir.AluOpType
ACT = mybir.ActivationFunctionType
AX = mybir.AxisListType

P = 128
NB = 8
S = 256
D = 256
KT = D // P
ST = S // P
NH = 16
NG = 4
DH = 128
J = NH // 2
HEADS_PER_GROUP = NH // NG
SCALE = float(1.0 / np.sqrt(np.float32(DH)))
EPS = 1e-5
MASKED = -3.0e38
HID = 704
ZERO_POINT = 128.0
HT = -(-HID // P)
HLAST = HID - (HT - 1) * P
CH = 1024
NRAW = 7
PASSES = ((0, 0), (0, 1), (1, 0))


def build(nc, x_in, wk_in, wv_in, wq_in, wp_in, wt_in, gb_in, bias_in, bin_in, win_in, wout_in, wgu_in, sgu_in,
          wd_in, rope_in, out):
    with ExitStack() as ctx:
        def sb(name, shape, dt=F32):
            return ctx.enter_context(nc.sbuf_tensor(name, shape, dt))

        def sem(name):
            return ctx.enter_context(nc.semaphore(name))

        x = sb("x", [P, NB * ST, D])
        xn = sb("xn", [P, ST, D])
        xT = sb("xT", [P, 2, KT, S], F32R)
        big = sb("big", [P, 12 * CH], F32R)
        wk = big[:, 0:2 * CH].rearrange("p (a k n) -> p a k n", a=2, k=KT)
        wv = big[:, 2 * CH:4 * CH].rearrange("p (a k n) -> p a k n", a=2, k=KT)
        wq = big[:, 4 * CH:12 * CH].rearrange("p (c a k n) -> p c a k n", c=4, a=2, k=KT)
        wp = sb("wp", [P, 4, 2, 4, D], F32R)
        raw = sb("raw", [P, NRAW, CH])
        kT = sb("kT", [P, 2, NG, S], F32R)
        v = sb("v", [P, 2, ST, NG * DH], F32R)
        qT = sb("qT", [P, 2, 2, S], F32R)
        prob = sb("prob", [P, 2, 2, 3 * P])
        pT0 = sb("pT0", [P, 2, 2 * S], F32R)
        pT1 = sb("pT1", [P, 2, 2 * P], F32R)
        oT = sb("oT", [P, 2, 2, 2 * S], F32R)
        rowmax = sb("rowmax", [P, 4])
        negmax = sb("negmax", [P, 4])
        rowsum = sb("rowsum", [P, 4])
        rowinv = sb("rowinv", [P, 2, 4])
        stats = sb("stats", [P, ST, 6])
        moments = sb("moments", [P, ST, 2])
        rstd = sb("rstd", [P, ST])
        exponent = sb("exponent", [P, 4])
        ident = sb("ident", [P, P])
        lin_w = big[:, 0:6 * 512].rearrange("p (a k n) -> p a k n", a=2, k=KT)
        gate_up = big[:, 3072:3072 + 8 * HID].rearrange("p (a g k n) -> p a g k n", a=2, g=2, k=KT)
        down = big[:, 3072 + 8 * HID:3072 + 8 * HID + 2 * HT * D].rearrange("p (a i n) -> p a i n", a=2, i=HT)
        w1 = sb("w1", [P, 6 * D], F32R)
        tern = w1[:, 0:2 * D].rearrange("p (k n) -> p k n", k=KT)
        lin_out = w1[:, 2 * D:6 * D].rearrange("p (a k n) -> p a k n", a=2, k=KT)
        wide = wp[:, :, :, :, :].rearrange("p c a h n -> p (c a h n)")
        xT4 = wide[:, 0:2048].rearrange("p (a k s) -> p a k s", a=2, k=KT)
        hT = wide[:, 2048:4096].rearrange("p (b a s) -> p b a s", b=2, a=2)
        yT = wide[:, 4096:5120].rearrange("p (a k s) -> p a k s", a=2, k=KT)
        rawf = raw[:, :, :].rearrange("p c n -> p (c n)")
        raw_t, raw_in, raw_out = rawf[:, 0:512], rawf[:, 512:2048], rawf[:, 2048:2560]
        raw_gu, raw_d = rawf[:, 2560:2560 + 4 * HID], rawf[:, 2560 + 4 * HID:2560 + 4 * HID + HT * D]
        qkv = sb("qkv", [P, 2, ST, 3 * D])
        kv = sb("kv", [P, ST, D])
        y = sb("y", [P, ST, D])
        rot1 = sb("rot1", [P, 2, P])
        rot2 = sb("rot2", [P, 2, P])
        k_norm = sb("k_norm", [P, ST])
        k_inv = sb("k_inv", [P, ST])
        z = y[:, :, :].rearrange("p t d -> p (t d)")
        flat_prob = prob[:, :, :, :].rearrange("p b h n -> p (b h n)")
        gate = flat_prob[:, 0:512]
        k_square = gate.rearrange("p (t d) -> p t d", t=ST)
        hidden = [flat_prob[:, 512 * (i + 1):512 * (i + 2)] for i in range(2)]
        scaled = y
        biases = sb("biases", [P, 3, D])
        b_in = sb("b_in", [P, 3 * D])
        rope = sb("rope", [P, 2, ST, 2, P])
        gamma_beta = sb("gamma_beta", [P, 2, KT])
        s_gu = sb("s_gu", [P, 2, HT])
        ones = sb("ones", [P, P])
        abs_w = qkv[:, 1, 0, 0:2 * D]
        abs_sum = sb("abs_sum", [P, 1])
        scale_eps = sb("scale_eps", [P, 1])
        half_scale = sb("half_scale", [P, 2])
        ternary_pos = qkv[:, 0, 0, 0:2 * D]
        ternary_neg = qkv[:, 0, 1, 0:2 * D]
        variance = sb("variance", [P, ST])
        k_bound = sb("k_bound", [P, ST])
        mask = sb("mask", [P, 2 * P])

        bank = [ctx.enter_context(nc.psum_tensor(f"bank{i}", [P, 512], F32)) for i in range(8)]
        bM, bQ, bS0, bS1, bT0, bT1, bO, bY = bank
        bS = (bS0, bS1)

        s_x = [sem(f"x_landed{b}") for b in range(NB)]
        s_raw = [sem(f"raw_landed{c}") for c in range(10)]
        s_const = sem("constants_made")
        s_wsplit = sem("early_weights_split")
        s_whi = sem("early_weights_hi")
        s_wpool = sem("late_weights_split")
        s_wph = sem("late_weights_hi")
        s_st = sem("ln_stats")
        s_mo = sem("ln_moments")
        s_var = sem("ln_variance_plus_eps")
        s_rs = sem("ln_rstd")
        s_xn = sem("xn_ready")
        s_xTp = sem("xT_in_psum")
        s_xhi = sem("xT_hi")
        s_xlo = sem("xT_lo")
        s_kp = sem("k_in_psum")
        s_khi = sem("k_hi")
        s_klo = sem("k_lo")
        s_vp = sem("v_in_psum")
        s_vhi = sem("v_hi")
        s_vlo = sem("v_lo")
        s_qp = sem("q_in_psum")
        s_qhi = sem("q_hi")
        s_qlo = sem("q_lo")
        s_sp = sem("scores_in_psum")
        s_mx = sem("rowmax_taken")
        s_nm = sem("negmax_ready")
        s_ex = sem("exp_done")
        s_ri = sem("rowinv_ready")
        s_pn0 = sem("probs_ready_head0")
        s_pn1 = sem("probs_ready_head1")
        s_pTp = sem("pT_in_psum")
        s_pThi = sem("pT_hi")
        s_pTlo = sem("pT_lo")
        s_op = sem("o_in_psum")
        s_ohi = sem("o_hi")
        s_olo = sem("o_lo")
        s_yp = sem("y_in_psum")
        s_ya = sem("y_added")
        s_tab = sem("tables_landed")
        s_rawt = sem("raw_ternary_landed")
        s_rawl = [sem(f"raw_late_landed{i}") for i in range(4)]
        s_lwhi = sem("late_layers_weights_hi")
        s_lwlo = sem("late_layers_weights_split")
        s_abs = sem("abs_weights_summed")
        s_absp = sem("abs_sum_in_psum")
        s_half = sem("half_scale_ready")
        s_tpos = sem("ternary_positive")
        s_tern = sem("ternary_ready")
        s_fn = sem("ternary_xn_ready")
        s_fb = sem("ternary_bias_added")
        s_fT = sem("ternary_xT_in_psum")
        s_fz = sem("ternary_z_ready")
        s_fhi = sem("ternary_z_hi")
        s_flo = sem("ternary_z_lo")
        s_fp = sem("ternary_out_in_psum")
        s_fa = sem("ternary_added")
        s_ln = sem("linear_xn_ready")
        s_lres = sem("linear_residual_ready")
        s_lres1 = sem("linear_residual_half")
        s_lT = sem("linear_xT_in_psum")
        s_lhi = sem("linear_xT_hi")
        s_llo = sem("linear_xT_lo")
        s_lp = sem("linear_qkv_in_psum")
        s_le = sem("linear_qkv_ready")
        s_lr1 = sem("rope_products")
        s_lr = sem("rope_done")
        s_lsq = sem("k_norm_squared")
        s_lkb = sem("k_norm_bounded")
        s_lki = sem("k_inv_ready")
        s_lkv = sem("kv_ready")
        s_lA = sem("A_in_psum")
        s_lY = sem("linear_y_ready")
        s_lyT = sem("linear_yT_in_psum")
        s_lyhi = sem("linear_yT_hi")
        s_lylo = sem("linear_yT_lo")
        s_lo = sem("linear_out_in_psum")
        s_la = sem("linear_added")
        s_gn = sem("gated_xn_ready")
        s_gT = sem("gated_xT_in_psum")
        s_ghi = sem("gated_xT_hi")
        s_glo = sem("gated_xT_lo")
        s_gg = sem("gate_in_psum")
        s_gu_ = sem("up_in_psum")
        s_gs = sem("gate_ready")
        s_gh = sem("hidden_ready")
        s_ghh = sem("hidden_hi")
        s_ghl = sem("hidden_lo")
        s_gd = sem("down_in_psum")
        s_gsc = sem("down_scaled")
        s_ga = sem("gated_added")
        s_carrier = sem("wait_carrier")
        s_out = sem("out_stored")

        x_v = x_in.rearrange("b (t p) d -> b p t d", p=P)
        out_v = out.rearrange("b (t p) d -> b p t d", p=P)

        EARLY = ["k", ("q", 0), "v", ("q", 1)]
        LATE = [("p", 0), ("q", 2), ("p", 1), ("q", 3), ("p", 2), ("p", 3)]
        CHUNKS = EARLY[:3] + LATE[:1] + EARLY[3:] + LATE[1:]

        def chunk_parts(c):
            if c == "k":
                return wk_in, [big[:, a * CH:(a + 1) * CH] for a in range(2)]
            if c == "v":
                return wv_in, [big[:, (2 + a) * CH:(3 + a) * CH] for a in range(2)]
            if c[0] == "q":
                at = 4 + 2 * c[1]
                return wq_in[c[1]], [big[:, (at + a) * CH:(at + 1 + a) * CH] for a in range(2)]
            return wp_in[c[1]], [wp[:, c[1], a].rearrange("p h n -> p (h n)") for a in range(2)]

        LAYER_WEIGHTS = [
            (raw_in, [big[:, a * 1536:(a + 1) * 1536] for a in range(2)], 0.0, P),
            (raw_out, [w1[:, (2 + 2 * a) * D:(4 + 2 * a) * D] for a in range(2)], 0.0, P),
            (raw_gu.bitcast(I32), [big[:, 3072 + a * 4 * HID:3072 + (a + 1) * 4 * HID] for a in range(2)], -ZERO_POINT, P),
            (raw_d[:, 0:(HT - 1) * D].bitcast(I32),
             [down[:, a, 0:HT - 1].rearrange("p i n -> p (i n)") for a in range(2)], -ZERO_POINT, P),
            (raw_d[0:HLAST, (HT - 1) * D:HT * D].bitcast(I32), [down[0:HLAST, a, HT - 1] for a in range(2)],
             -ZERO_POINT, HLAST),
        ]

        def wait_apart(eng, semaphore, value):
            eng.wait_ge(semaphore, value)
            if not isinstance(value, int):
                eng.sem_inc(s_carrier, 1)

        def ahead(n, j, steps):
            return (n, j + steps) if j + steps < J else (n + 1, j + steps - J)

        def f32(ap):
            return ap.bitcast(F32)

        block = ctx.enter_context(nc.Block())

        @block.sync
        def _(sp):
            sp.dma_start(x[:, 0:ST, :], x_v[0]).then_inc(s_x[0], 16)
            for n, c in enumerate(CHUNKS):
                if n >= NRAW:
                    old = CHUNKS[n - NRAW]
                    sp.wait_ge(*((s_wsplit, EARLY.index(old) + 1) if old in EARLY else (s_wpool, LATE.index(old) + 1)))
                sp.dma_start(raw[:, n % NRAW, :], chunk_parts(c)[0]).then_inc(s_raw[n], 16)
                if n == 3:
                    sp.dma_start(x[:, ST:2 * ST, :], x_v[1]).then_inc(s_x[1], 16)
            for b in range(2, NB):
                sp.dma_start(x[:, ST * b:ST * (b + 1), :], x_v[b]).then_inc(s_x[b], 16)
            for dst, src in ((biases, bias_in), (b_in, bin_in), (gamma_beta, gb_in), (s_gu, sgu_in), (rope, rope_in)):
                sp.dma_start(dst[:], src).then_inc(s_tab, 16)
            sp.wait_ge(s_wsplit, len(EARLY))
            sp.wait_ge(s_wpool, len(LATE))
            sp.dma_start(raw_t, wt_in).then_inc(s_rawt, 16)
            sp.dma_start(raw_in, win_in).then_inc(s_rawl[0], 16)
            sp.dma_start(raw_out, wout_in).then_inc(s_rawl[1], 16)
            sp.dma_start(raw_gu.bitcast(I32), wgu_in).then_inc(s_rawl[2], 16)
            wd = raw_d.bitcast(I32).rearrange("p (i n) -> p i n", i=HT)
            sp.dma_start(wd[:, 0:HT - 1, :], wd_in[0:(HT - 1) * P, :].rearrange("(i p) n -> p i n", p=P)).then_inc(s_rawl[3], 16)
            sp.dma_start(wd[0:HLAST, HT - 1, :], wd_in[(HT - 1) * P:HID, :]).then_inc(s_rawl[3], 16)
            for b in range(NB):
                sp.wait_ge(s_ga, b + 2)
                sp.dma_start(out_v[b], x[:, ST * b:ST * (b + 1), :]).then_inc(s_out, 16)
            sp.wait_ge(s_out, 16 * NB)

        @block.gpsimd
        def _(pool):
            pool.memset(ident[:], 0.0).then_inc(s_const, 1)
            pool.memset(mask[:], 0.0).then_inc(s_const, 1)
            pool.memset(exponent[:, :], -0.5)
            pool.memset(ones[:, :], 1.0)
            pool.wait_ge(s_const, 2)
            pool.affine_select(out=ident[:], in_=ident[:], compare_op=ALU.not_equal, fill=1.0, base=0,
                               pattern=[[-1, P]], channel_multiplier=1).then_inc(s_const, 1)
            pool.affine_select(out=mask[:, P:2 * P], in_=mask[:, P:2 * P], compare_op=ALU.is_ge, fill=MASKED,
                               base=0, pattern=[[-1, P]], channel_multiplier=1).then_inc(s_const, 1)
            def inv_std(call):
                wait_apart(pool, s_mo, call + 1)
                pool.tensor_scalar(variance[:, :], moments[:, :, 1], EPS, None, ALU.add).then_inc(s_var, 1)
                pool.wait_ge(s_var, call + 1)
                pool.tensor_tensor(rstd[:, :], variance[:, :], exponent[:, 0:ST], ALU.pow).then_inc(s_rs, 1)

            def inv_std_twice(n):
                pool.wait_ge(s_var, NB + n + 1)
                pool.tensor_tensor(rstd[:, :], variance[:, :], exponent[:, 0:ST], ALU.pow).then_inc(s_rs, 1)

            def add_row(n, row):
                xs = x[:, bass.ds(ST * n, ST), :]
                return pool.tensor_tensor(xs, xs, biases[:, row:row + 1, :].to_broadcast([P, ST, D]), ALU.add)

            def ternary_bias(n):
                wait_apart(pool, s_fn, n + 1)
                add_row(n, 0).then_inc(s_fb, 1)

            def rotate(n, q, t):
                u = ST * n + t
                qk = qkv[:, q, t, 0:2 * D].rearrange("p (c d) -> p c d", c=2)[:, :, 0:P]
                pairs = qk.rearrange("p c (i e) -> p c i e", e=2)
                sin = rope[:, 1, t].rearrange("p c (i e) -> p c i e", e=2)
                turned = rot2[:, :, :].rearrange("p c (i e) -> p c i e", e=2)
                wait_apart(pool, s_le, u + 1)
                if t > 0:
                    pool.wait_ge(s_lr, u)
                pool.tensor_tensor(rot1[:, :, :], qk, rope[:, 0, t], ALU.mult)
                for e in range(2):
                    m = pool.tensor_tensor(turned[:, :, :, e], pairs[:, :, :, 1 - e], sin[:, :, :, e], ALU.mult)
                m.then_inc(s_lr1, 1)
                pool.wait_ge(s_lr1, u + 1)
                pool.tensor_tensor(qk, rot1[:, :, :], rot2[:, :, :], ALU.add).then_inc(s_lr, 1)

            def k_inverse(n):
                wait_apart(pool, s_lsq, n + 1)
                pool.tensor_scalar(k_bound[:, :], k_norm[:, :], 1e-24, None, ALU.max).then_inc(s_lkb, 1)
                pool.wait_ge(s_lkb, n + 1)
                pool.tensor_tensor(k_inv[:, :], k_bound[:, :], exponent[:, 0:ST], ALU.pow).then_inc(s_lki, 1)

            def linear_residual(n):
                wait_apart(pool, s_ln, n + 1)
                xs = x[:, bass.ds(ST * n, ST), :]
                pool.tensor_tensor(xs, xs, xn[:, :, :], ALU.add).then_inc(s_lres1, 1)
                wait_apart(pool, s_lres1, n + 1)
                add_row(n, 1).then_inc(s_lres, 1)

            def normalise(n, j):
                wait_apart(pool, s_ri, J * n + j + 1)
                for r, (a, b) in enumerate(((0, P), (P, 3 * P))):
                    m = pool.tensor_scalar(prob[:, j % 2, 0, a:b], prob[:, j % 2, 0, a:b], rowinv[:, j % 2, r:r + 1], None, ALU.mult)
                m.then_inc(s_pn0, 1)

            def late(i):
                n = CHUNKS.index(LATE[i])
                src, (hi, lo) = raw[:, n % NRAW, :], chunk_parts(LATE[i])[1]
                pool.wait_ge(s_raw[n], 16)
                pool.tensor_copy(hi, src).then_inc(s_wph, 1)
                pool.wait_ge(s_wph, i + 1)
                pool.tensor_tensor(lo, src, f32(hi), ALU.subtract).then_inc(s_wpool, 1)

            def batch(n, last):
                for j in range(J):
                    if isinstance(n, int) and n == 0 and j + 1 < len(LATE):
                        late(j + 1)
                    if j < J - 2 or not last:
                        normalise(*ahead(n, j, 2))
                    if j == 2 and not last:
                        inv_std(n + 1)

            inv_std(0)
            normalise(0, 0)
            normalise(0, 1)
            late(0)
            batch(0, False)
            with pool.Fori(1, NB - 1) as n:
                batch(n, False)
            batch(NB - 1, True)

            pool.wait_ge(s_tab, 16 * 5)
            inv_std_twice(0)
            ternary_bias(0)
            inv_std_twice(1)
            ternary_bias(1)
            with pool.Fori(2, NB) as n:
                inv_std_twice(n)
                ternary_bias(n)

            inv_std(2 * NB)
            linear_residual(0)
            inv_std(2 * NB + 1)
            linear_residual(1)

            def linear(n, q, last):
                rotate(n, q, 0)
                if not last:
                    inv_std(2 * NB + 2 + n)
                rotate(n, q, 1)
                k_inverse(n)
                if not last:
                    linear_residual(n + 2)

            with pool.Fori(0, NB // 2 - 1) as m:
                for q in range(2):
                    linear(2 * m + q, q, False)
            for q in range(2):
                linear(NB - 2 + q, q, True)

            def finish(b):
                xs = x[:, bass.ds(ST * b, ST), :]
                wait_apart(pool, s_gsc, b + 1)
                pool.tensor_tensor(xs, xs, scaled[:, :, :], ALU.add).then_inc(s_ga, 1)

            pool.sem_inc(s_ga, 1)
            inv_std(3 * NB)
            inv_std(3 * NB + 1)

            def gated(m, first, last):
                if not first:
                    for q in range(2):
                        finish(2 * m - 2 + q)
                if not last:
                    for q in range(2):
                        inv_std(3 * NB + 2 * m + 2 + q)

            gated(0, True, False)
            with pool.Fori(1, NB // 2 - 1) as m:
                gated(m, False, False)
            gated(NB // 2 - 1, False, True)
            for q in range(2):
                finish(NB - 2 + q)

        def mm3(pe, out, lhs, rhs, first, last):
            for i, (a, b) in enumerate(PASSES):
                m = pe.matmul(out, lhs(a), rhs(b), start=first and i == 0, stop=last and i == 2,
                              skip_group_check=True)
            return m

        @block.tensor
        def _(pe):
            def x_transpose(n):
                pe.wait_ge(s_xn, n + 1)
                if not (isinstance(n, int) and n == 0):
                    pe.wait_ge(s_vlo, 2 * n)
                for k in range(KT):
                    for t in range(ST):
                        m = pe.transpose(bM[:, k * S + t * P:k * S + (t + 1) * P], xn[:, t, k * P:(k + 1) * P], ident[:])
                m.then_inc(s_xTp, 1)

            def k_project(n, half):
                if half == 0:
                    pe.wait_ge(s_xlo, n + 1)
                else:
                    pe.wait_ge(s_klo, 2 * n + 1)
                for i in range(2):
                    g = 2 * half + i
                    for k in range(KT):
                        m = mm3(pe, bM[:, i * S:(i + 1) * S], lambda a: wk[:, a, k, g * DH:(g + 1) * DH],
                                lambda a: xT[:, a, k, :], k == 0, k == KT - 1)
                m.then_inc(s_kp, 1)

            def v_project(n, t):
                if t == 0:
                    pe.wait_ge(s_klo, 2 * n + 2)
                else:
                    pe.wait_ge(s_vlo, 2 * n + 1)
                for k in range(KT):
                    m = mm3(pe, bM[:, :], lambda a: xT[:, a, k, t * P:(t + 1) * P], lambda a: wv[:, a, k, :],
                            k == 0, k == KT - 1)
                m.then_inc(s_vp, 1)

            def q_project(n, j):
                if not (isinstance(n, int) and n == 0 and j == 0):
                    pe.wait_ge(s_qlo, J * n + j)
                for i in range(2):
                    h = 2 * j + i
                    for k in range(KT):
                        m = mm3(pe, bQ[:, i * S:(i + 1) * S],
                                lambda a: wq[:, h // 4, a, k, (h % 4) * DH:(h % 4 + 1) * DH],
                                lambda a: xT[:, a, k, :], k == 0, k == KT - 1)
                m.then_inc(s_qp, 1)

            def scores(n, j):
                t, g = J * n + j, 2 * j // HEADS_PER_GROUP
                pe.wait_ge(s_qlo, t + 1)
                pe.wait_ge(s_klo, 2 * n + 1 + g // 2)
                for i in range(2):
                    if not (isinstance(n, int) and n == 0 and j == 0):
                        pe.wait_ge(s_mx, 2 * t - 1 + i)
                    for r in range(ST):
                        m = mm3(pe, bS[i][:, r * S:(r + 1) * S], lambda a: qT[:, a, i, r * P:(r + 1) * P],
                                lambda a: kT[:, a, g, :], True, True)
                    m.then_inc(s_sp, 1)

            def p_transpose(n, j):
                t = J * n + j
                if not (isinstance(n, int) and n == 0 and j == 0):
                    pe.wait_ge(s_pTlo, 2 * t)
                for i in range(2):
                    pe.wait_ge((s_pn0, s_pn1)[i], t + 1)
                    for r in range(ST):
                        m = pe.transpose(bT0[:, i * S + r * P:i * S + (r + 1) * P], prob[:, j % 2, i, r * P:(r + 1) * P], ident[:])
                m.then_inc(s_pTp, 1)
                for i in range(2):
                    m = pe.transpose(bT1[:, i * P:(i + 1) * P], prob[:, j % 2, i, 2 * P:3 * P], ident[:])
                m.then_inc(s_pTp, 1)

            def attend(n, j):
                t, g = J * n + j, 2 * j // HEADS_PER_GROUP
                if not (isinstance(n, int) and n == 0 and j == 0):
                    pe.wait_ge(s_olo, t)
                pe.wait_ge(s_vlo, 2 * n + 1)
                pe.wait_ge(s_pTlo, 2 * t + 1)
                mm3(pe, bO[:, :], lambda a: v[:, a, 0, g * DH:(g + 1) * DH], lambda a: pT0[:, a, :], True, False)
                pe.wait_ge(s_vlo, 2 * n + 2)
                pe.wait_ge(s_pTlo, 2 * t + 2)
                late = bO[:, :].rearrange("p (h s) -> p h s", h=2)[:, :, P:2 * P]
                m = mm3(pe, late, lambda a: v[:, a, 1, g * DH:(g + 1) * DH],
                        lambda a: pT1[:, a, :].rearrange("p (h s) -> p h s", h=2), False, True)
                m.then_inc(s_op, 1)

            def out_project(n, j):
                pe.wait_ge(s_olo, J * n + j + 1)
                if j == 0 and not (isinstance(n, int) and n == 0):
                    pe.wait_ge(s_ya, n)
                for i in range(2):
                    h = 2 * j + i
                    for t in range(ST):
                        m = mm3(pe, bY[:, t * D:(t + 1) * D],
                                lambda a: oT[:, j % 2, a, i * S + t * P:i * S + (t + 1) * P],
                                lambda a: wp[:, h // 4, a, h % 4, :], h == 0 and t == 0, h == NH - 1)
                if j == J - 1:
                    m.then_inc(s_yp, 1)

            def weights(n, early=0, late=0):
                if isinstance(n, int) and n == 0:
                    if early:
                        pe.wait_ge(s_wsplit, early)
                    if late:
                        pe.wait_ge(s_wpool, late)

            def batch(n, last):
                for j in range(J):
                    p_transpose(n, j)
                    if j < J - 2 or not last:
                        scores(*ahead(n, j, 2))
                    if j == 0:
                        v_project(n, 1)
                    if j == 4 and last:
                        pe.wait_ge(s_vlo, 2 * NB)
                        pe.wait_ge(s_abs, 1)
                        pe.matmul(bM[:, 0:1], ones[:, :], abs_sum[:, 0:1], start=True, stop=True).then_inc(s_absp, 1)
                    if j in (5, 6) and not last:
                        k_project(n + 1, j - 5)
                    if j < J - 3 or not last:
                        weights(n, late={1: 2, 3: 4}.get(j, 0))
                        q_project(*ahead(n, j, 3))
                    if j == 4 and not last:
                        x_transpose(n + 1)
                    attend(n, j)
                    if j > 0:
                        weights(n, late={1: 1, 3: 3, 5: 5, 7: 6}.get(j, 0))
                        out_project(n, j - 1)
                if not last:
                    v_project(n + 1, 0)
                out_project(n, J - 1)

            def transposes(out, src):
                for k in range(KT):
                    for t in range(ST):
                        m = pe.transpose(out[:, k * S + t * P:k * S + (t + 1) * P], src[:, t, k * P:(k + 1) * P], ident[:])
                return m

            def ternary_transpose(n):
                pe.wait_ge(s_fn, n + 1)
                if isinstance(n, int) and n == 0:
                    pe.wait_ge(s_half, 1)
                else:
                    pe.wait_ge(s_flo, n)
                transposes(bM, xn).then_inc(s_fT, 1)

            def ternary(n):
                pe.wait_ge(s_flo, n + 1)
                if isinstance(n, int) and n == 0:
                    pe.wait_ge(s_ya, NB)
                    pe.wait_ge(s_tern, 1)
                else:
                    pe.wait_ge(s_fa, n)
                for t in range(ST):
                    for k in range(KT):
                        for a in range(2):
                            m = pe.matmul(bY[:, t * D:(t + 1) * D], xT[:, a, k, t * P:(t + 1) * P], tern[:, k, :],
                                          start=k + a == 0, stop=k + a == 2, skip_group_check=True)
                m.then_inc(s_fp, 1)

            bQK, bV = (bS0, bS1), (bT0, bT1)

            def linear_transpose(n):
                pe.wait_ge(s_ln, n + 1)
                if not (isinstance(n, int) and n == 0):
                    pe.wait_ge(s_llo, n)
                transposes(bM, xn).then_inc(s_lT, 1)

            def linear_qkv(n, t):
                pe.wait_ge(s_llo, n + 1)
                if isinstance(n, int) and n == 0:
                    pe.wait_ge(s_lwlo, 1)
                else:
                    pe.wait_ge(s_le, ST * n - ST + t + 1)
                for out, a0, a1 in ((bQK[t][:, :], 0, 2 * D), (bV[t][:, 0:D], 2 * D, 3 * D)):
                    for k in range(KT):
                        m = mm3(pe, out, lambda a: xT[:, a, k, t * P:(t + 1) * P], lambda a: lin_w[:, a, k, a0:a1],
                                k == 0, k == KT - 1)
                m.then_inc(s_lp, 1)

            def linear_sum(n):
                pe.wait_ge(s_lkv, n + 1)
                if not (isinstance(n, int) and n == 0):
                    pe.wait_ge(s_lY, n)
                for t in range(ST):
                    m = pe.matmul(bQ[:, 0:D], ones[:, :], kv[:, t, :], start=t == 0, stop=t == ST - 1)
                m.then_inc(s_lA, 1)

            def linear_y_transpose(n):
                pe.wait_ge(s_lY, n + 1)
                if not (isinstance(n, int) and n == 0):
                    pe.wait_ge(s_lylo, n)
                transposes(bO, y).then_inc(s_lyT, 1)

            def linear_out(n):
                pe.wait_ge(s_lylo, n + 1)
                if isinstance(n, int) and n == 0:
                    pe.wait_ge(s_lwlo, 2)
                else:
                    pe.wait_ge(s_la, n)
                for t in range(ST):
                    for k in range(KT):
                        m = mm3(pe, bY[:, t * D:(t + 1) * D], lambda a: yT[:, a, k, t * P:(t + 1) * P],
                                lambda a: lin_out[:, a, k, :], k == 0, k == KT - 1)
                m.then_inc(s_lo, 1)

            def linear(n, qkv_on=True, sum_on=True, out_on=True, next_on=True):
                if qkv_on:
                    linear_qkv(n, 0)
                if out_on:
                    linear_y_transpose(n - 2)
                if qkv_on:
                    linear_qkv(n, 1)
                if next_on:
                    linear_transpose(n + 1)
                if sum_on:
                    linear_sum(n - 1)
                if out_on:
                    linear_out(n - 2)

            bG, bU, bD = (bQ, bS0), (bS1, bT0), (bT1, bO)

            def gated_transpose(b):
                pe.wait_ge(s_gn, b + 1)
                if not (isinstance(b, int) and b == 0):
                    pe.wait_ge(s_glo, b)
                transposes(bM, xn).then_inc(s_gT, 1)

            def gate_and_up(m, i):
                u = HT * m + i
                rows = P if i < HT - 1 else HLAST
                if i == 0:
                    pe.wait_ge(s_glo, 2 * m + 2)
                if isinstance(m, int) and m == 0 and i == 0:
                    pe.wait_ge(s_lwlo, 3)
                for g, (bank_of, done) in enumerate(((bG, s_gg), (bU, s_gu_))):
                    if not (isinstance(m, int) and m == 0 and i < 2):
                        pe.wait_ge(s_gh, u - 1)
                    for k in range(KT):
                        mm = mm3(pe, bank_of[i % 2][0:rows, :], lambda a: gate_up[:, a, g, k, i * P:i * P + rows],
                                 lambda a: xT4[:, a, k, :], k == 0, k == KT - 1)
                    mm.then_inc(done, 1)

            def down_project(m, i):
                u = HT * m + i
                rows = P if i < HT - 1 else HLAST
                pe.wait_ge(s_ghl, u + 1)
                if i == 0:
                    if isinstance(m, int) and m == 0:
                        pe.wait_ge(s_lwlo, 4)
                    else:
                        pe.wait_ge(s_gsc, 2 * m)
                for b in range(2):
                    for t in range(ST):
                        at = b * S + t * P
                        mm = mm3(pe, bD[b][:, t * D:(t + 1) * D], lambda a: hT[0:rows, i % 2, a, at:at + P],
                                 lambda a: down[0:rows, a, i, :], i == 0 and t == 0, i == HT - 1)
                    if i == HT - 1:
                        mm.then_inc(s_gd, 1)

            def gated(m, first, last):
                for i in range(HT):
                    gate_and_up(m, i)
                    if i > 0:
                        down_project(m, i - 1)
                    elif not first:
                        down_project(m - 1, HT - 1)
                if not last:
                    for q in range(2):
                        gated_transpose(2 * m + 2 + q)

            pe.wait_ge(s_const, 4)
            x_transpose(0)
            weights(0, early=1)
            k_project(0, 0)
            weights(0, early=2)
            q_project(0, 0)
            k_project(0, 1)
            scores(0, 0)
            q_project(0, 1)
            scores(0, 1)
            weights(0, early=4)
            q_project(0, 2)
            weights(0, early=3)
            v_project(0, 0)
            batch(0, False)
            with pe.Fori(1, NB - 1) as n:
                batch(n, False)
            batch(NB - 1, True)

            ternary_transpose(0)
            ternary(0)
            ternary_transpose(1)
            with pe.Fori(1, NB - 1) as n:
                ternary(n)
                ternary_transpose(n + 1)
            ternary(NB - 1)

            pe.wait_ge(s_fa, NB)
            linear_transpose(0)
            linear(0, sum_on=False, out_on=False)
            linear(1, out_on=False)
            linear(2)
            with pe.Fori(3, NB - 1) as n:
                linear(n)
            linear(NB - 1, next_on=False)
            linear(NB, qkv_on=False, next_on=False)
            linear(NB + 1, qkv_on=False, sum_on=False, next_on=False)

            pe.wait_ge(s_la, NB)
            gated_transpose(0)
            gated_transpose(1)
            gated(0, True, False)
            with pe.Fori(1, NB // 2 - 1) as m:
                gated(m, False, False)
            gated(NB // 2 - 1, False, True)
            down_project(NB // 2 - 1, HT - 1)

        @block.scalar
        def _(act):
            def hi(out, src, waits, done):
                act.wait_ge(*waits)
                act.activation(out, src, ACT.Copy).then_inc(done, 1)

            def early(i):
                n = CHUNKS.index(EARLY[i])
                act.wait_ge(s_raw[n], 16)
                act.activation(chunk_parts(EARLY[i])[1][0], raw[:, n % NRAW, :], ACT.Copy).then_inc(s_whi, 1)

            def x_hi(n):
                hi(xT[:, 0].rearrange("p k s -> p (k s)"), bM[:, :], (s_xTp, n + 1), s_xhi)

            def k_hi(n, half):
                hi(kT[:, 0, 2 * half:2 * half + 2].rearrange("p g s -> p (g s)"), bM[:, :], (s_kp, 2 * n + half + 1), s_khi)

            def v_hi(n, t):
                hi(v[:, 0, t], bM[:, :], (s_vp, 2 * n + t + 1), s_vhi)

            def q_hi(n, j):
                hi(qT[:, 0].rearrange("p h s -> p (h s)"), bQ[:, :], (s_qp, J * n + j + 1), s_qhi)

            def pT_hi(n, j):
                t = J * n + j
                hi(pT0[:, 0], bT0[:, :], (s_pTp, 2 * t + 1), s_pThi)
                hi(pT1[:, 0], bT1[:, 0:2 * P], (s_pTp, 2 * t + 2), s_pThi)

            def o_hi(n, j):
                hi(oT[:, j % 2, 0], bO[:, :], (s_op, J * n + j + 1), s_ohi)

            def exps(n, j):
                t = J * n + j
                act.wait_ge(s_nm, t + 1)
                for i in range(2):
                    for r, (a, b) in enumerate(((0, P), (P, 3 * P))):
                        m = act.activation(prob[:, j % 2, i, a:b], prob[:, j % 2, i, a:b], ACT.Exp, scale=SCALE,
                                           bias=negmax[:, 2 * i + r:2 * i + r + 1],
                                           accum_out=rowsum[:, 2 * i + r:2 * i + r + 1])
                m.then_inc(s_ex, 1)

            def batch(n, last):
                for j in range(J):
                    pT_hi(n, j)
                    if j == 2 and last:
                        act.wait_ge(s_rawt, 16)
                        act.activation(abs_w, raw_t, ACT.Abs, accum_out=abs_sum[:, 0:1]).then_inc(s_abs, 1)
                    if j >= 6 and last:
                        late_layer_hi(j - 6)
                    if j == 0:
                        v_hi(n, 1)
                    if j in (5, 6) and not last:
                        k_hi(n + 1, j - 5)
                    if j < J - 3 or not last:
                        q_hi(*ahead(n, j, 3))
                    if j == 4 and not last:
                        x_hi(n + 1)
                    if j < J - 2 or not last:
                        exps(*ahead(n, j, 2))
                    o_hi(n, j)
                if not last:
                    v_hi(n + 1, 0)

            def late_layer_hi(i):
                src, (high, _), bias, _ = LAYER_WEIGHTS[i]
                act.wait_ge(s_rawl[i], 16 if i < 3 else 32)
                if i == 0:
                    act.wait_ge(s_qp, J * NB)
                act.activation(high, src, ACT.Copy, bias=bias).then_inc(s_lwhi, 1)
                if i == 3:
                    src, (high, _), bias, _ = LAYER_WEIGHTS[4]
                    act.activation(high, src, ACT.Copy, bias=bias).then_inc(s_lwhi, 1)

            def ternary_hi(n):
                act.wait_ge(s_fT, n + 1)
                for k in range(KT):
                    m = act.activation(z[:, k * S:(k + 1) * S], bM[:, k * S:(k + 1) * S], ACT.Identity,
                                       bias=gamma_beta[:, 1, k:k + 1], scale=gamma_beta[:, 0, k:k + 1])
                m.then_inc(s_fz, 1)
                act.wait_ge(s_fz, n + 1)
                act.activation(xT[:, 0].rearrange("p k s -> p (k s)"), z, ACT.Copy).then_inc(s_fhi, 1)

            def linear_x_hi(n):
                hi(xT[:, 0].rearrange("p k s -> p (k s)"), bM[:, :], (s_lT, n + 1), s_lhi)

            def linear(n, q, qkv_on=True, out_on=True, next_on=True):
                if out_on:
                    hi(yT[:, 0].rearrange("p k s -> p (k s)"), bO[:, :], (s_lyT, n - 1), s_lyhi)
                if next_on:
                    linear_x_hi(n + 1)
                if qkv_on:
                    act.wait_ge(s_lr, ST * n + ST)
                    for t in range(ST):
                        m = act.activation(k_square[:, t, :], qkv[:, q, t, D:2 * D], ACT.Square, accum_out=k_norm[:, t:t + 1])
                    m.then_inc(s_lsq, 1)

            def gated_x_hi(b, q):
                act.wait_ge(s_gT, b + 1)
                act.activation(xT4[:, 0, :, q * S:(q + 1) * S], bM[:, :].rearrange("p (k s) -> p k s", k=KT),
                               ACT.Copy).then_inc(s_ghi, 1)

            def gated(m, last):
                for i in range(HT):
                    u = HT * m + i
                    rows = P if i < HT - 1 else HLAST
                    act.wait_ge(s_gg, u + 1)
                    if not (isinstance(m, int) and m == 0 and i == 0):
                        act.wait_ge(s_gh, u)
                    act.activation(gate[0:rows, :], bG[i % 2][0:rows, :], ACT.Silu, scale=s_gu[0:rows, 0, i:i + 1]).then_inc(s_gs, 1)
                    act.wait_ge(s_gh, u + 1)
                    act.activation(hT[0:rows, i % 2, 0], hidden[i % 2][0:rows, :], ACT.Copy).then_inc(s_ghh, 1)
                if not last:
                    for q in range(2):
                        gated_x_hi(2 * m + 2 + q, q)

            bG = (bQ, bS0)
            early(0)
            x_hi(0)
            early(1)
            k_hi(0, 0)
            q_hi(0, 0)
            early(2)
            k_hi(0, 1)
            early(3)
            exps(0, 0)
            q_hi(0, 1)
            exps(0, 1)
            q_hi(0, 2)
            v_hi(0, 0)
            batch(0, False)
            with act.Fori(1, NB - 1) as n:
                batch(n, False)
            batch(NB - 1, True)

            act.wait_ge(s_tab, 16 * 5)
            ternary_hi(0)
            late_layer_hi(2)
            ternary_hi(1)
            late_layer_hi(3)
            with act.Fori(2, NB) as n:
                ternary_hi(n)

            linear_x_hi(0)
            linear(0, 0, out_on=False)
            linear(1, 1, out_on=False)
            with act.Fori(1, NB // 2 - 1) as m:
                for q in range(2):
                    linear(2 * m + q, q)
            linear(NB - 2, 0)
            linear(NB - 1, 1, next_on=False)
            linear(NB, 0, qkv_on=False, next_on=False)
            linear(NB + 1, 1, qkv_on=False, next_on=False)

            for q in range(2):
                gated_x_hi(q, q)
            gated(0, False)
            with act.Fori(1, NB // 2 - 1) as m:
                gated(m, False)
            gated(NB // 2 - 1, True)

        @block.vector
        def _(dve):
            def x_tile(b, t):
                return x[:, bass.ds(ST * b + t, 1), :].rearrange("p o d -> p (o d)")

            def ln_moments(call, b):
                for t in range(ST):
                    m = dve.bn_stats(stats[:, t, :], x_tile(b, t))
                m.then_inc(s_st, 1)
                wait_apart(dve, s_st, call + 1)
                for t in range(ST):
                    m = dve.bn_aggr(moments[:, t, :], stats[:, t, :])
                m.then_inc(s_mo, 1)

            def ln_apply(call, b):
                dve.wait_ge(s_mo, call + 1)
                dve.wait_ge(s_rs, call + 1)
                for t in range(ST):
                    m = dve.tensor_scalar(xn[:, t, :], x_tile(b, t), moments[:, t, 0:1], rstd[:, t:t + 1],
                                          ALU.subtract, ALU.mult)
                return m

            def lo(out, src, hi, waits, done):
                dve.wait_ge(*waits)
                dve.tensor_tensor(out, src, f32(hi), ALU.subtract).then_inc(done, 1)

            def early(i):
                n = CHUNKS.index(EARLY[i])
                hi, low = chunk_parts(EARLY[i])[1]
                dve.wait_ge(s_raw[n], 16)
                lo(low, raw[:, n % NRAW, :], hi, (s_whi, i + 1), s_wsplit)

            def x_norm(n):
                if isinstance(n, int):
                    dve.wait_ge(s_x[n], 16)
                    if n > 0:
                        dve.wait_ge(s_xTp, n)
                else:
                    dve.wait_ge(s_xTp, n)
                ln_moments(n, n)
                ln_apply(n, n).then_inc(s_xn, 1)

            def x_lo(n):
                lo(xT[:, 1].rearrange("p k s -> p (k s)"), bM[:, :], xT[:, 0].rearrange("p k s -> p (k s)"),
                   (s_xhi, n + 1), s_xlo)

            def k_lo(n, half):
                part = [kT[:, a, 2 * half:2 * half + 2].rearrange("p g s -> p (g s)") for a in range(2)]
                lo(part[1], bM[:, :], part[0], (s_khi, 2 * n + half + 1), s_klo)

            def v_lo(n, t):
                lo(v[:, 1, t], bM[:, :], v[:, 0, t], (s_vhi, 2 * n + t + 1), s_vlo)

            def q_lo(n, j):
                part = [qT[:, a].rearrange("p h s -> p (h s)") for a in range(2)]
                lo(part[1], bQ[:, :], part[0], (s_qhi, J * n + j + 1), s_qlo)

            def pT_lo(n, j, part):
                pT, src = ((pT0, bT0[:, :]), (pT1, bT1[:, 0:2 * P]))[part]
                lo(pT[:, 1], src, pT[:, 0], (s_pThi, 2 * (J * n + j) + part + 1), s_pTlo)

            def o_lo(n, j):
                lo(oT[:, j % 2, 1], bO[:, :], oT[:, j % 2, 0], (s_ohi, J * n + j + 1), s_olo)

            def row_max(n, j):
                t = J * n + j
                for i in range(2):
                    wait_apart(dve, s_sp, 2 * t + i + 1)
                    for r, (a, b) in enumerate(((0, P), (P, 3 * P))):
                        m = dve.tensor_tensor_reduce(prob[:, j % 2, i, a:b], bS[i][:, r * S:r * S + b - a],
                                                     mask[:, (1 - r) * P:2 * P], 1.0, MASKED, ALU.add, ALU.max,
                                                     rowmax[:, 2 * i + r:2 * i + r + 1])
                    m.then_inc(s_mx, 1)
                dve.wait_ge(s_mx, 2 * t + 2)
                dve.tensor_scalar(negmax[:, :], rowmax[:, :], -SCALE, None, ALU.mult).then_inc(s_nm, 1)

            def normalise(n, j):
                t = J * n + j
                dve.wait_ge(s_ex, t + 1)
                dve.reciprocal(rowinv[:, j % 2, :], rowsum[:, :]).then_inc(s_ri, 1)
                dve.wait_ge(s_ri, t + 1)
                for r, (a, b) in enumerate(((0, P), (P, 3 * P))):
                    m = dve.tensor_scalar(prob[:, j % 2, 1, a:b], prob[:, j % 2, 1, a:b],
                                          rowinv[:, j % 2, 2 + r:3 + r], None, ALU.mult)
                m.then_inc(s_pn1, 1)

            def add_y(n):
                dve.wait_ge(s_yp, n + 1)
                xs = x[:, bass.ds(ST * n, ST), :].rearrange("p t d -> p (t d)")
                dve.tensor_tensor(xs, bY[:, :], xs, ALU.add).then_inc(s_ya, 1)

            def batch(n, last):
                for j in range(J):
                    pT_lo(n, j, 0)
                    pT_lo(n, j, 1)
                    if j == 4 and last:
                        ternary_weights()
                    if j >= 6 and last:
                        late_layer_lo(j - 6)
                    if j < J - 2 or not last:
                        row_max(*ahead(n, j, 2))
                    if j == 0:
                        v_lo(n, 1)
                    if j in (5, 6) and not last:
                        k_lo(n + 1, j - 5)
                    if j < J - 3 or not last:
                        q_lo(*ahead(n, j, 3))
                    if j == 4 and not last:
                        x_lo(n + 1)
                    if j < J - 2 or not last:
                        normalise(*ahead(n, j, 2))
                    o_lo(n, j)
                    if j == 2 and not last:
                        x_norm(n + 1)
                if not last:
                    v_lo(n + 1, 0)
                add_y(n)

            def ternary_weights():
                dve.wait_ge(s_absp, 1)
                dve.tensor_scalar(scale_eps[:, :], bM[:, 0:1], 1.0 / (D * D), EPS, ALU.mult, ALU.add).then_inc(s_half, 1)
                dve.wait_ge(s_half, 1)
                dve.tensor_scalar(half_scale[:, 0:1], scale_eps[:, :], 0.5, None, ALU.mult)
                dve.tensor_scalar(half_scale[:, 1:2], scale_eps[:, :], -0.5, None, ALU.mult).then_inc(s_half, 1)
                dve.wait_ge(s_half, 2)
                dve.tensor_scalar(ternary_pos[:, :], raw_t, half_scale[:, 0:1], None, ALU.is_gt).then_inc(s_tpos, 1)
                dve.wait_ge(s_tpos, 1)
                dve.scalar_tensor_tensor(ternary_neg[:, :], raw_t, half_scale[:, 1:2], ternary_pos[:, :], ALU.is_lt,
                                         ALU.subtract).then_inc(s_tpos, 1)
                dve.wait_ge(s_tpos, 2)
                dve.tensor_scalar(tern.rearrange("p k n -> p (k n)"), ternary_neg[:, :], -1.0, None, ALU.mult).then_inc(s_tern, 1)

            def late_layer_lo(i):
                for n in ((i,) if i < 3 else (3, 4)):
                    src, (high, low), bias, rows = LAYER_WEIGHTS[n]
                    dve.wait_ge(s_lwhi, n + 1)
                    m = dve.scalar_tensor_tensor(low, src, bias, f32(high), ALU.add, ALU.subtract)
                m.then_inc(s_lwlo, 1)

            def ternary_moments(n):
                ln_moments(NB + n, n)
                dve.wait_ge(s_mo, NB + n + 1)
                dve.tensor_scalar(variance[:, :], moments[:, :, 1], 1.0 + EPS, EPS * EPS, ALU.mult, ALU.add).then_inc(s_var, 1)

            def ternary_norm(n):
                ternary_moments(n)
                if isinstance(n, int) and n == 0:
                    dve.wait_ge(s_xTp, NB)
                else:
                    dve.wait_ge(s_fT, n)
                ln_apply(NB + n, n).then_inc(s_fn, 1)

            def ternary_lo(n):
                lo(xT[:, 1].rearrange("p k s -> p (k s)"), z, xT[:, 0].rearrange("p k s -> p (k s)"), (s_fhi, n + 1), s_flo)

            def add_bank(n, out_ready, residual_ready, done):
                dve.wait_ge(out_ready, n + 1)
                dve.wait_ge(residual_ready, n + 1)
                xs = x[:, bass.ds(ST * n, ST), :].rearrange("p t d -> p (t d)")
                dve.tensor_tensor(xs, bY[:, :], xs, ALU.add).then_inc(done, 1)

            def linear_apply(n):
                if isinstance(n, int) and n == 0:
                    dve.wait_ge(s_fT, NB)
                else:
                    dve.wait_ge(s_lT, n)
                    dve.wait_ge(s_lres1, n)
                ln_apply(2 * NB + n, n).then_inc(s_ln, 1)

            def linear_x_lo(n):
                lo(xT[:, 1].rearrange("p k s -> p (k s)"), bM[:, :], xT[:, 0].rearrange("p k s -> p (k s)"), (s_lhi, n + 1), s_llo)

            def linear_qkv(n, q, t):
                dve.wait_ge(s_lp, ST * n + t + 1)
                if t == 0 and not (isinstance(n, int) and n < 2):
                    dve.wait_ge(s_lY, n - 1)
                dve.tensor_tensor(qkv[:, q, t, 0:2 * D], bQK[t][:, :], b_in[:, 0:2 * D], ALU.add)
                dve.tensor_tensor(qkv[:, q, t, 2 * D:3 * D], bV[t][:, 0:D], b_in[:, 2 * D:3 * D], ALU.add).then_inc(s_le, 1)

            def linear_kv(n, q):
                dve.wait_ge(s_lki, n + 1)
                if not (isinstance(n, int) and n == 0):
                    dve.wait_ge(s_lA, n)
                for t in range(ST):
                    m = dve.scalar_tensor_tensor(kv[:, t, :], qkv[:, q, t, D:2 * D], k_inv[:, t:t + 1],
                                                 qkv[:, q, t, 2 * D:3 * D], ALU.mult, ALU.mult)
                m.then_inc(s_lkv, 1)

            def linear_y(n, q):
                dve.wait_ge(s_lA, n + 1)
                for t in range(ST):
                    m = dve.tensor_tensor(y[:, t, :], bQ[:, 0:D], qkv[:, q, t, 0:D], ALU.mult)
                m.then_inc(s_lY, 1)

            def linear(n, q, qkv_on=True, sum_on=True, out_on=True, next_on=True, norm_on=True):
                if sum_on:
                    linear_kv(n - 1, 1 - q)
                if qkv_on:
                    linear_qkv(n, q, 0)
                if norm_on:
                    ln_moments(2 * NB + 2 + n, n + 2)
                if out_on:
                    part = [yT[:, a].rearrange("p k s -> p (k s)") for a in range(2)]
                    lo(part[1], bO[:, :], part[0], (s_lyhi, n - 1), s_lylo)
                if qkv_on:
                    linear_qkv(n, q, 1)
                if next_on:
                    linear_x_lo(n + 1)
                if sum_on:
                    linear_y(n - 1, 1 - q)
                if norm_on:
                    linear_apply(n + 2)
                if out_on:
                    add_bank(n - 2, s_lo, s_lres, s_la)

            def gated_norm(b):
                ln_moments(3 * NB + b, b)
                if isinstance(b, int) and b == 0:
                    dve.wait_ge(s_lT, NB)
                else:
                    dve.wait_ge(s_gT, b)
                ln_apply(3 * NB + b, b).then_inc(s_gn, 1)

            def gated_x_lo(b, q):
                dve.wait_ge(s_ghi, b + 1)
                dve.tensor_tensor(xT4[:, 1, :, q * S:(q + 1) * S], bM[:, :].rearrange("p (k s) -> p k s", k=KT),
                                  f32(xT4[:, 0, :, q * S:(q + 1) * S]), ALU.subtract).then_inc(s_glo, 1)

            def hidden_tile(m, i):
                u = HT * m + i
                rows = P if i < HT - 1 else HLAST
                dve.wait_ge(s_gu_, u + 1)
                dve.wait_ge(s_gs, u + 1)
                if not (isinstance(m, int) and m == 0 and i < 2):
                    dve.wait_ge(s_ghl, u - 1)
                dve.scalar_tensor_tensor(hidden[i % 2][0:rows, :], bU[i % 2][0:rows, :], s_gu[0:rows, 1, i:i + 1],
                                         gate[0:rows, :], ALU.mult, ALU.mult).then_inc(s_gh, 1)
                dve.wait_ge(s_ghh, u + 1)
                dve.tensor_tensor(hT[0:rows, i % 2, 1], hidden[i % 2][0:rows, :], f32(hT[0:rows, i % 2, 0]),
                                  ALU.subtract).then_inc(s_ghl, 1)

            def scale_down(b, q):
                dve.wait_ge(s_gd, b + 1)
                dve.wait_ge(s_ga, b + 1)
                for t in range(ST):
                    m = dve.tensor_tensor(scaled[:, t, :], bD[q][:, t * D:(t + 1) * D], biases[:, 2, :], ALU.mult)
                m.then_inc(s_gsc, 1)

            def gated(m, first, last):
                for i in range(HT):
                    hidden_tile(m, i)
                    if i == 0 and not first:
                        for q in range(2):
                            scale_down(2 * m - 2 + q, q)
                    if i == 3 and not last:
                        gated_norm(2 * m + 2)
                if not last:
                    gated_x_lo(2 * m + 2, 0)
                    gated_norm(2 * m + 3)
                    gated_x_lo(2 * m + 3, 1)

            bQK, bV, bU, bD = (bS0, bS1), (bT0, bT1), (bS1, bT0), (bT1, bO)
            dve.wait_ge(s_const, 4)
            x_norm(0)
            early(0)
            x_lo(0)
            early(1)
            k_lo(0, 0)
            q_lo(0, 0)
            early(2)
            k_lo(0, 1)
            early(3)
            row_max(0, 0)
            normalise(0, 0)
            q_lo(0, 1)
            row_max(0, 1)
            normalise(0, 1)
            q_lo(0, 2)
            v_lo(0, 0)
            batch(0, False)
            for b in range(2, NB):
                dve.wait_ge(s_x[b], 16)
            with dve.Fori(1, NB - 1) as n:
                batch(n, False)
            batch(NB - 1, True)

            ternary_norm(0)
            ternary_lo(0)
            late_layer_lo(2)
            ternary_norm(1)
            ternary_lo(1)
            late_layer_lo(3)
            add_bank(0, s_fp, s_fb, s_fa)
            with dve.Fori(2, NB) as n:
                ternary_norm(n)
                ternary_lo(n)
                add_bank(n - 1, s_fp, s_fb, s_fa)
            add_bank(NB - 1, s_fp, s_fb, s_fa)

            dve.wait_ge(s_tab, 16 * 5)
            ln_moments(2 * NB, 0)
            linear_apply(0)
            linear_x_lo(0)
            ln_moments(2 * NB + 1, 1)
            linear_apply(1)
            linear(0, 0, sum_on=False, out_on=False)
            linear(1, 1, out_on=False)
            with dve.Fori(1, NB // 2 - 1) as m:
                for q in range(2):
                    linear(2 * m + q, q)
            linear(NB - 2, 0, norm_on=False)
            linear(NB - 1, 1, norm_on=False, next_on=False)
            linear(NB, 0, qkv_on=False, next_on=False, norm_on=False)
            linear(NB + 1, 1, qkv_on=False, sum_on=False, next_on=False, norm_on=False)

            for q in range(2):
                gated_norm(q)
                gated_x_lo(q, q)
            gated(0, True, False)
            with dve.Fori(1, NB // 2 - 1) as m:
                gated(m, False, False)
            gated(NB // 2 - 1, False, True)
            for q in range(2):
                scale_down(NB - 2 + q, q)


def kernel(**inputs):
    import concourse.bacc as bacc
    from concourse.bass_utils import run_bass_kernel_spmd

    def tiles(w):
        return w.reshape(-1, P, w.shape[1]).transpose(1, 0, 2)

    def rows(*vectors):
        return np.ascontiguousarray(np.stack([np.broadcast_to(r, (P, r.shape[-1])) for r in vectors], 1))

    w = {k: np.asarray(a) for k, a in inputs.items()}
    qkv = w["L0_attn_weight_qkv"].reshape(NG, HEADS_PER_GROUP + 2, DH, D)
    proj = w["L0_attn_weight_proj"].T.reshape(4, 4, DH, D)
    last = {k: w[k].T for k in ("L1_ffn_wq_gate", "L1_ffn_wq_up", "L1_ffn_wq_down")}
    inv_freq = np.float32(1.0) / np.float32(10000.0) ** (np.arange(0, P, 2, dtype=np.float32) / np.float32(P))
    angle = np.repeat(np.arange(S, dtype=np.float32)[:, None] * inv_freq[None, :], 2, axis=1).reshape(ST, P, P)
    sign = np.where(np.arange(P) % 2 == 0, np.float32(-1.0), np.float32(1.0))
    rope = np.stack([np.cos(angle), np.sin(angle) * sign]).astype(np.float32)
    hid = np.zeros((2, HT * P), np.float32)
    hid[0, :HID], hid[1, :HID] = w["L1_ffn_s_gate"], w["L1_ffn_s_up"]
    arrays = {
        "x": w["L0_attn_x"],
        "wk": tiles(qkv[:, HEADS_PER_GROUP].reshape(NG * DH, D).T),
        "wv": tiles(qkv[:, HEADS_PER_GROUP + 1].reshape(NG * DH, D).T),
        "wq": np.stack([tiles(qkv[g, :HEADS_PER_GROUP].reshape(-1, D).T) for g in range(NG)]),
        "wp": proj.transpose(0, 2, 1, 3),
        "wt": tiles(w["L0_ffn_weight"].T),
        "gamma_beta": np.stack([w["L0_ffn_ln_gamma"].reshape(KT, P), w["L0_ffn_ln_beta"].reshape(KT, P)]).transpose(2, 0, 1),
        "biases": rows(w["L0_ffn_bias"], w["L1_attn_b_out"], w["L1_ffn_s_down"]),
        "b_in": rows(w["L1_attn_b_in"]),
        "w_in": tiles(w["L1_attn_W_in"].T),
        "w_out": tiles(w["L1_attn_W_out"].T),
        "w_gu": np.stack([tiles(last["L1_ffn_wq_gate"]), tiles(last["L1_ffn_wq_up"])], 1),
        "s_gu": hid.reshape(2, HT, P).transpose(2, 0, 1),
        "w_down": last["L1_ffn_wq_down"],
        "rope": np.repeat(rope.transpose(2, 0, 1, 3)[:, :, :, None], 2, axis=3),
    }
    flat = {"wk", "wv", "wt", "w_in", "w_out", "w_gu", "b_in"}
    nc = bacc.Bacc("TRN2", target_bir_lowering=False, num_devices=1)
    aps = []
    for name, a in arrays.items():
        if name in flat:
            a = a.reshape(P, -1)
        if name in ("wq", "wp"):
            a = a.reshape(4, P, -1)
        arrays[name] = a = np.ascontiguousarray(a)
        aps.append(nc.dram_tensor("in_" + name, a.shape, mybir.dt.from_np(a.dtype), kind="ExternalInput").ap())
    out = nc.dram_tensor("out", (NB, S, D), F32, kind="ExternalOutput").ap()
    build(nc, *aps, out)
    return run_bass_kernel_spmd(nc, [{"in_" + k: a for k, a in arrays.items()}], core_ids=[0]).results[0]["out"]
```

```python
from contextlib import ExitStack

import numpy as np

import concourse.bass as bass
from concourse import mybir

F32 = mybir.dt.float32
F32R = mybir.dt.float32r
I32 = mybir.dt.int32
ALU = mybir.AluOpType
ACT = mybir.ActivationFunctionType
AX = mybir.AxisListType

P = 128
NB = 8
S = 256
D = 256
KT = D // P
ST = S // P
NH = 16
NG = 4
DH = 128
J = NH // 2
HEADS_PER_GROUP = NH // NG
SCALE = float(1.0 / np.sqrt(np.float32(DH)))
EPS = 1e-5
MASKED = -3.0e38
HID = 704
ZERO_POINT = 128.0
HT = -(-HID // P)
HLAST = HID - (HT - 1) * P
CH = 1024
NRAW = 7
PASSES = ((0, 0), (0, 1), (1, 0))


def build(nc, x_in, wk_in, wv_in, wq_in, wp_in, wt_in, gb_in, bias_in, bin_in, win_in, wout_in, wgu_in, sgu_in,
          wd_in, rope_in, out):
    with ExitStack() as ctx:
        def sb(name, shape, dt=F32):
            return ctx.enter_context(nc.sbuf_tensor(name, shape, dt))

        def sem(name):
            return ctx.enter_context(nc.semaphore(name))

        x = sb("x", [P, NB * ST, D])
        xn = sb("xn", [P, ST, D])
        xT = sb("xT", [P, 2, KT, S], F32R)
        big = sb("big", [P, 12 * CH], F32R)
        wk = big[:, 0:2 * CH].rearrange("p (a k n) -> p a k n", a=2, k=KT)
        wv = big[:, 2 * CH:4 * CH].rearrange("p (a k n) -> p a k n", a=2, k=KT)
        wq = big[:, 4 * CH:12 * CH].rearrange("p (c a k n) -> p c a k n", c=4, a=2, k=KT)
        wp = sb("wp", [P, 4, 2, 4, D], F32R)
        raw = sb("raw", [P, NRAW, CH])
        kT = sb("kT", [P, 2, NG, S], F32R)
        v = sb("v", [P, 2, ST, NG * DH], F32R)
        qT = sb("qT", [P, 2, 2, S], F32R)
        prob = sb("prob", [P, 2, 2, 3 * P])
        pT0 = sb("pT0", [P, 2, 2 * S], F32R)
        pT1 = sb("pT1", [P, 2, 2 * P], F32R)
        oT = sb("oT", [P, 2, 2, 2 * S], F32R)
        rowmax = sb("rowmax", [P, 4])
        negmax = sb("negmax", [P, 4])
        rowsum = sb("rowsum", [P, 4])
        rowinv = sb("rowinv", [P, 2, 4])
        stats = sb("stats", [P, ST, 6])
        moments = sb("moments", [P, ST, 2])
        rstd = sb("rstd", [P, ST])
        exponent = sb("exponent", [P, 4])
        ident = sb("ident", [P, P])
        lin_w = big[:, 0:6 * 512].rearrange("p (a k n) -> p a k n", a=2, k=KT)
        gate_up = big[:, 3072:3072 + 8 * HID].rearrange("p (a g k n) -> p a g k n", a=2, g=2, k=KT)
        down = big[:, 3072 + 8 * HID:3072 + 8 * HID + 2 * HT * D].rearrange("p (a i n) -> p a i n", a=2, i=HT)
        w1 = sb("w1", [P, 6 * D], F32R)
        tern = w1[:, 0:2 * D].rearrange("p (k n) -> p k n", k=KT)
        lin_out = w1[:, 2 * D:6 * D].rearrange("p (a k n) -> p a k n", a=2, k=KT)
        xT4 = wp[:, :, :, :, :].rearrange("p c a h n -> p (c a h n)").rearrange("p (m a k s) -> p m a k s", m=NB // 2, a=2, k=KT)
        hT = kT[:, :, :, :].rearrange("p a g s -> p (a g s)").rearrange("p (b a s) -> p b a s", b=2, a=2)
        zT = sb("zT", [P, 2, KT, S], F32R)
        yT = zT
        rawf = raw[:, :, :].rearrange("p c n -> p (c n)")
        raw_in, raw_out = rawf[:, 512:2048], rawf[:, 2048:2560]
        raw_gu, raw_d = rawf[:, 2560:2560 + 4 * HID], rawf[:, 2560 + 4 * HID:2560 + 4 * HID + HT * D]
        qkv = sb("qkv", [P, 2, ST, 3 * D])
        y = sb("y", [P, ST, D])
        residual_scale = sb("residual_scale", [P, 2, ST])
        k_norm = sb("k_norm", [P, ST])
        k_inv = sb("k_inv", [P, ST])
        raw_t, abs_w = qkv[:, 1, 1, 0:2 * D], qkv[:, 1, 0, 0:2 * D]
        ternary_pos, ternary_neg = qkv[:, 0, 0, 0:2 * D], qkv[:, 0, 1, 0:2 * D]
        txn = y
        z_parts = (qkv[:, 1, 1, 0:2 * D], rawf[:, 512:1024])
        flat_prob = prob[:, :, :, :].rearrange("p b h n -> p (b h n)")
        rot1 = rawf[:, 0:4 * P].rearrange("p (t c d) -> p t c d", t=ST, c=2)
        rot2 = flat_prob[:, 512:1024].rearrange("p (t c d) -> p t c d", t=ST, c=2)
        kv = flat_prob[:, 1024:1536].rearrange("p (t d) -> p t d", t=ST)
        gate = flat_prob[:, 0:512]
        k_square = gate.rearrange("p (t d) -> p t d", t=ST)
        hidden = [rawf[:, 512 * (i + 1):512 * (i + 2)] for i in range(2)]
        scaled = (y, qkv[:, 0, 0, 0:2 * D].rearrange("p (t d) -> p t d", t=ST))
        biases = sb("biases", [P, 3, D])
        b_in = sb("b_in", [P, 3 * D])
        rope = sb("rope", [P, 2, ST, 2, P])
        gamma_beta = sb("gamma_beta", [P, 2, KT])
        s_gu = sb("s_gu", [P, 2, HT])
        ones = sb("ones", [P, P])
        abs_sum = sb("abs_sum", [P, 1])
        scale_eps = sb("scale_eps", [P, 1])
        half_scale = sb("half_scale", [P, 2])
        t_stats = sb("ternary_stats", [P, ST, 6])
        t_moments = sb("ternary_moments", [P, ST, 2])
        t_variance = sb("ternary_variance", [P, ST])
        t_rstd = sb("ternary_rstd", [P, ST])
        variance = sb("variance", [P, ST])
        k_bound = sb("k_bound", [P, ST])
        mask = sb("mask", [P, 2 * P])

        bank = [ctx.enter_context(nc.psum_tensor(f"bank{i}", [P, 512], F32)) for i in range(8)]
        bM, bQ, bS0, bS1, bT0, bT1, bO, bY = bank
        bS = (bS0, bS1)

        s_x = [sem(f"x_landed{b}") for b in range(NB)]
        s_raw = [sem(f"raw_landed{c}") for c in range(10)]
        s_const = sem("constants_made")
        s_wsplit = sem("early_weights_split")
        s_whi = sem("early_weights_hi")
        s_wpool = sem("late_weights_split")
        s_wph = sem("late_weights_hi")
        s_st = sem("ln_stats")
        s_mo = sem("ln_moments")
        s_var = sem("ln_variance_plus_eps")
        s_rs = sem("ln_rstd")
        s_xn = sem("xn_ready")
        s_xTp = sem("xT_in_psum")
        s_xhi = sem("xT_hi")
        s_xlo = sem("xT_lo")
        s_kp = sem("k_in_psum")
        s_khi = sem("k_hi")
        s_klo = sem("k_lo")
        s_vp = sem("v_in_psum")
        s_vhi = sem("v_hi")
        s_vlo = sem("v_lo")
        s_qp = sem("q_in_psum")
        s_qhi = sem("q_hi")
        s_qlo = sem("q_lo")
        s_sp = sem("scores_in_psum")
        s_mx = sem("rowmax_taken")
        s_nm = sem("negmax_ready")
        s_ex = sem("exp_done")
        s_ri = sem("rowinv_ready")
        s_pn0 = sem("probs_ready_head0")
        s_pn1 = sem("probs_ready_head1")
        s_pTp = sem("pT_in_psum")
        s_pThi = sem("pT_hi")
        s_pTlo = sem("pT_lo")
        s_op = sem("o_in_psum")
        s_ohi = sem("o_hi")
        s_olo = sem("o_lo")
        s_yp = sem("y_in_psum")
        s_ya = sem("y_added")
        s_tab = sem("tables_landed")
        s_rawt = sem("raw_ternary_landed")
        s_rawl = [sem(f"raw_late_landed{i}") for i in range(4)]
        s_lwhi = sem("late_layers_weights_hi")
        s_lwlo = sem("late_layers_weights_split")
        s_abs = sem("abs_weights_summed")
        s_absp = sem("abs_sum_in_psum")
        s_half = sem("half_scale_ready")
        s_tpos = sem("ternary_positive")
        s_tern = sem("ternary_ready")
        s_fst = sem("ternary_ln_stats")
        s_fmo = sem("ternary_ln_moments")
        s_fvar = sem("ternary_ln_variances_joined")
        s_frs = sem("ternary_ln_rstd")
        s_fn = sem("ternary_xn_ready")
        s_fb = sem("ternary_bias_added")
        s_fT = sem("ternary_xT_in_psum")
        s_fz = sem("ternary_z_ready")
        s_fhi = sem("ternary_z_hi")
        s_flo = sem("ternary_z_lo")
        s_fp = sem("ternary_out_in_psum")
        s_fa = sem("ternary_added")
        s_ln = sem("linear_xn_ready")
        s_lres = sem("linear_residual_ready")
        s_lres1 = sem("linear_residual_half")
        s_lT = sem("linear_xT_in_psum")
        s_lhi = sem("linear_xT_hi")
        s_llo = sem("linear_xT_lo")
        s_lp = sem("linear_qkv_in_psum")
        s_le = sem("linear_qkv_ready")
        s_lc = sem("rope_cosine_products")
        s_lr1 = sem("rope_sine_products")
        s_lrs = sem("linear_residual_scale")
        s_lr = sem("rope_done")
        s_lsq = sem("k_norm_squared")
        s_lkb = sem("k_norm_bounded")
        s_lki = sem("k_inv_ready")
        s_lkv = sem("kv_ready")
        s_lA = sem("A_in_psum")
        s_lY = sem("linear_y_ready")
        s_lyT = sem("linear_yT_in_psum")
        s_lyhi = sem("linear_yT_hi")
        s_lylo = sem("linear_yT_lo")
        s_lo = sem("linear_out_in_psum")
        s_la = sem("linear_added")
        s_gn = sem("gated_xn_ready")
        s_gT = sem("gated_xT_in_psum")
        s_ghi = sem("gated_xT_hi")
        s_glo = sem("gated_xT_lo")
        s_gg = sem("gate_in_psum")
        s_gu_ = sem("up_in_psum")
        s_gs = sem("gate_ready")
        s_gh = sem("hidden_ready")
        s_ghh = sem("hidden_hi")
        s_ghl = sem("hidden_lo")
        s_gd = sem("down_in_psum")
        s_gsc = sem("down_scaled")
        s_ga = sem("gated_added")
        s_carrier = sem("wait_carrier")
        s_out = sem("out_stored")

        x_v = x_in.rearrange("b (t p) d -> b p t d", p=P)
        out_v = out.rearrange("b (t p) d -> b p t d", p=P)

        EARLY = ["k", ("q", 0), "v", ("q", 1)]
        LATE = [("p", 0), ("q", 2), ("p", 1), ("q", 3), ("p", 2), ("p", 3)]
        CHUNKS = EARLY[:3] + LATE[:1] + EARLY[3:] + LATE[1:]

        def chunk_parts(c):
            if c == "k":
                return wk_in, [big[:, a * CH:(a + 1) * CH] for a in range(2)]
            if c == "v":
                return wv_in, [big[:, (2 + a) * CH:(3 + a) * CH] for a in range(2)]
            if c[0] == "q":
                at = 4 + 2 * c[1]
                return wq_in[c[1]], [big[:, (at + a) * CH:(at + 1 + a) * CH] for a in range(2)]
            return wp_in[c[1]], [wp[:, c[1], a].rearrange("p h n -> p (h n)") for a in range(2)]

        LAYER_WEIGHTS = [
            (raw_in, [big[:, a * 1536:(a + 1) * 1536] for a in range(2)], 0.0, P),
            (raw_out, [w1[:, (2 + 2 * a) * D:(4 + 2 * a) * D] for a in range(2)], 0.0, P),
            (raw_gu.bitcast(I32), [big[:, 3072 + a * 4 * HID:3072 + (a + 1) * 4 * HID] for a in range(2)], -ZERO_POINT, P),
            (raw_d[:, 0:(HT - 1) * D].bitcast(I32),
             [down[:, a, 0:HT - 1].rearrange("p i n -> p (i n)") for a in range(2)], -ZERO_POINT, P),
            (raw_d[0:HLAST, (HT - 1) * D:HT * D].bitcast(I32), [down[0:HLAST, a, HT - 1] for a in range(2)],
             -ZERO_POINT, HLAST),
        ]

        def wait_apart(eng, semaphore, value):
            eng.wait_ge(semaphore, value)
            if not isinstance(value, int):
                eng.sem_inc(s_carrier, 1)

        def ahead(n, j, steps):
            return (n, j + steps) if j + steps < J else (n + 1, j + steps - J)

        def z_of(n):
            return z_parts[isinstance(n, int) and n == NB - 1]

        def f32(ap):
            return ap.bitcast(F32)

        block = ctx.enter_context(nc.Block())

        @block.sync
        def _(sp):
            sp.dma_start(x[:, 0:ST, :], x_v[0]).then_inc(s_x[0], 16)
            for n, c in enumerate(CHUNKS):
                if n >= NRAW:
                    old = CHUNKS[n - NRAW]
                    sp.wait_ge(*((s_wsplit, EARLY.index(old) + 1) if old in EARLY else (s_wpool, LATE.index(old) + 1)))
                sp.dma_start(raw[:, n % NRAW, :], chunk_parts(c)[0]).then_inc(s_raw[n], 16)
                if n == 3:
                    sp.dma_start(x[:, ST:2 * ST, :], x_v[1]).then_inc(s_x[1], 16)
            sp.dma_start(raw_t, wt_in).then_inc(s_rawt, 16)
            for b in range(2, NB):
                sp.dma_start(x[:, ST * b:ST * (b + 1), :], x_v[b]).then_inc(s_x[b], 16)
            for dst, src in ((biases, bias_in), (b_in, bin_in), (gamma_beta, gb_in), (s_gu, sgu_in), (rope, rope_in)):
                sp.dma_start(dst[:], src).then_inc(s_tab, 16)
            sp.wait_ge(s_wsplit, len(EARLY))
            sp.wait_ge(s_wpool, len(LATE))
            sp.dma_start(raw_in, win_in).then_inc(s_rawl[0], 16)
            sp.dma_start(raw_out, wout_in).then_inc(s_rawl[1], 16)
            sp.dma_start(raw_gu.bitcast(I32), wgu_in).then_inc(s_rawl[2], 16)
            wd = raw_d.bitcast(I32).rearrange("p (i n) -> p i n", i=HT)
            sp.dma_start(wd[:, 0:HT - 1, :], wd_in[0:(HT - 1) * P, :].rearrange("(i p) n -> p i n", p=P)).then_inc(s_rawl[3], 16)
            sp.dma_start(wd[0:HLAST, HT - 1, :], wd_in[(HT - 1) * P:HID, :]).then_inc(s_rawl[3], 16)
            for b in range(NB):
                sp.wait_ge(s_ga, b + 3)
                sp.dma_start(out_v[b], x[:, ST * b:ST * (b + 1), :]).then_inc(s_out, 16)
            sp.wait_ge(s_out, 16 * NB)

        @block.gpsimd
        def _(pool):
            pool.memset(ident[:], 0.0).then_inc(s_const, 1)
            pool.memset(mask[:], 0.0).then_inc(s_const, 1)
            pool.memset(exponent[:, :], -0.5)
            pool.memset(ones[:, :], 1.0)
            pool.wait_ge(s_const, 2)
            pool.affine_select(out=ident[:], in_=ident[:], compare_op=ALU.not_equal, fill=1.0, base=0,
                               pattern=[[-1, P]], channel_multiplier=1).then_inc(s_const, 1)
            pool.affine_select(out=mask[:, P:2 * P], in_=mask[:, P:2 * P], compare_op=ALU.is_ge, fill=MASKED,
                               base=0, pattern=[[-1, P]], channel_multiplier=1).then_inc(s_const, 1)
            def inv_std(call):
                wait_apart(pool, s_mo, call + 1)
                pool.tensor_scalar(variance[:, :], moments[:, :, 1], EPS, None, ALU.add).then_inc(s_var, 1)
                pool.wait_ge(s_var, call + 1)
                pool.tensor_tensor(rstd[:, :], variance[:, :], exponent[:, 0:ST], ALU.pow).then_inc(s_rs, 1)

            def inv_std_twice(n):
                wait_apart(pool, s_fvar, n + 1)
                pool.tensor_tensor(t_rstd[:, :], t_variance[:, :], exponent[:, 0:ST], ALU.pow).then_inc(s_frs, 1)

            def add_row(n, row):
                xs = x[:, bass.ds(ST * n, ST), :]
                return pool.tensor_tensor(xs, xs, biases[:, row:row + 1, :].to_broadcast([P, ST, D]), ALU.add)

            def ternary_bias(n):
                wait_apart(pool, s_fn, n + 1)
                add_row(n, 0).then_inc(s_fb, 1)

            def rotate(n, q, t):
                u = ST * n + t
                qk = qkv[:, q, t, 0:2 * D].rearrange("p (c d) -> p c d", c=2)[:, :, 0:P]
                pairs = qk.rearrange("p c (i e) -> p c i e", e=2)
                sin = rope[:, 1, t].rearrange("p c (i e) -> p c i e", e=2)
                turned = rot2[:, t].rearrange("p c (i e) -> p c i e", e=2)
                wait_apart(pool, s_le, u + 1)
                for e in range(2):
                    m = pool.tensor_tensor(turned[:, :, :, e], pairs[:, :, :, 1 - e], sin[:, :, :, e], ALU.mult)
                m.then_inc(s_lr1, 1)
                wait_apart(pool, s_lr1, u + 1)
                wait_apart(pool, s_lc, u + 1)
                pool.tensor_tensor(qk, rot1[:, t], rot2[:, t], ALU.add).then_inc(s_lr, 1)

            def k_inverse(n):
                wait_apart(pool, s_lsq, n + 1)
                pool.tensor_scalar(k_bound[:, :], k_norm[:, :], 1e-24, None, ALU.max).then_inc(s_lkb, 1)
                pool.wait_ge(s_lkb, n + 1)
                pool.tensor_tensor(k_inv[:, :], k_bound[:, :], exponent[:, 0:ST], ALU.pow).then_inc(s_lki, 1)

            def linear_bias(n):
                wait_apart(pool, s_lres1, n + 1)
                add_row(n, 1).then_inc(s_lres, 1)

            def normalise(n, j):
                wait_apart(pool, s_ri, J * n + j + 1)
                for r, (a, b) in enumerate(((0, P), (P, 3 * P))):
                    m = pool.tensor_scalar(prob[:, j % 2, 0, a:b], prob[:, j % 2, 0, a:b], rowinv[:, j % 2, r:r + 1], None, ALU.mult)
                m.then_inc(s_pn0, 1)

            def late_lo(i):
                n = CHUNKS.index(LATE[i])
                hi, lo = chunk_parts(LATE[i])[1]
                pool.wait_ge(s_raw[n], 16)
                pool.wait_ge(s_wph, i + 1)
                pool.tensor_tensor(lo, raw[:, n % NRAW, :], f32(hi), ALU.subtract).then_inc(s_wpool, 1)

            def batch(n, last):
                for j in range(J):
                    if j < J - 2 or not last:
                        normalise(*ahead(n, j, 2))
                    if not (isinstance(n, int) and n == 0):
                        if j == 0:
                            inv_std_twice(n - 1)
                        if j == 1:
                            ternary_bias(n - 1)
                    if j == 2 and not last:
                        inv_std(n + 1)
                    if j in (4, 5) and last:
                        inv_std(NB + j - 4)
                    if j in (6, 7) and last:
                        linear_bias(j - 6)
                    if isinstance(n, int) and n == 0 and j + 2 < len(LATE):
                        late_lo(j + 2)

            inv_std(0)
            late_lo(0)
            normalise(0, 0)
            late_lo(1)
            normalise(0, 1)
            batch(0, False)
            pool.wait_ge(s_tab, 16 * 5)
            with pool.Fori(1, NB - 1) as n:
                batch(n, False)
            batch(NB - 1, True)


            def linear(n, q, last):
                rotate(n, q, 0)
                inv_std(NB + 2 + n)
                rotate(n, q, 1)
                k_inverse(n)
                if not last:
                    linear_bias(n + 2)

            linear(0, 0, False)
            inv_std_twice(NB - 1)
            linear(1, 1, False)
            ternary_bias(NB - 1)
            with pool.Fori(1, NB // 2 - 1) as m:
                for q in range(2):
                    linear(2 * m + q, q, False)
            for q in range(2):
                linear(NB - 2 + q, q, True)

            def finish(b, q):
                xs = x[:, bass.ds(ST * b, ST), :]
                wait_apart(pool, s_gsc, b + 1)
                pool.tensor_tensor(xs, xs, scaled[q][:, :, :], ALU.add).then_inc(s_ga, 1)

            pool.sem_inc(s_ga, 2)

            def gated(m, first, last):
                if not first:
                    for q in range(2):
                        finish(2 * m - 2 + q, q)
                if not last:
                    for q in range(2):
                        inv_std(2 * NB + 2 * m + 2 + q)

            gated(0, True, False)
            with pool.Fori(1, NB // 2 - 1) as m:
                gated(m, False, False)
            gated(NB // 2 - 1, False, True)
            for q in range(2):
                finish(NB - 2 + q, q)

        def mm3(pe, out, lhs, rhs, first, last):
            for i, (a, b) in enumerate(PASSES):
                m = pe.matmul(out, lhs(a), rhs(b), start=first and i == 0, stop=last and i == 2,
                              skip_group_check=True)
            return m

        @block.tensor
        def _(pe):
            def transposes(out, src):
                for k in range(KT):
                    for t in range(ST):
                        m = pe.transpose(out[:, k * S + t * P:k * S + (t + 1) * P], src[:, t, k * P:(k + 1) * P], ident[:])
                return m

            def x_transpose(n):
                pe.wait_ge(s_xn, n + 1)
                if not (isinstance(n, int) and n == 0):
                    pe.wait_ge(*((s_half, 1) if isinstance(n, int) and n == 1 else (s_fa, n - 1)))
                transposes(bM, xn).then_inc(s_xTp, 1)

            def k_project(n, half):
                if half == 0:
                    pe.wait_ge(s_xlo, n + 1)
                else:
                    pe.wait_ge(s_klo, 2 * n + 1)
                for i in range(2):
                    g = 2 * half + i
                    for k in range(KT):
                        m = mm3(pe, bM[:, i * S:(i + 1) * S], lambda a: wk[:, a, k, g * DH:(g + 1) * DH],
                                lambda a: xT[:, a, k, :], k == 0, k == KT - 1)
                m.then_inc(s_kp, 1)

            def v_project(n, t):
                if t == 0:
                    pe.wait_ge(s_klo, 2 * n + 2)
                else:
                    pe.wait_ge(s_vlo, 2 * n + 1)
                for k in range(KT):
                    m = mm3(pe, bM[:, :], lambda a: xT[:, a, k, t * P:(t + 1) * P], lambda a: wv[:, a, k, :],
                            k == 0, k == KT - 1)
                m.then_inc(s_vp, 1)

            def q_project(n, j):
                if not (isinstance(n, int) and n == 0 and j == 0):
                    pe.wait_ge(s_qlo, J * n + j)
                for i in range(2):
                    h = 2 * j + i
                    for k in range(KT):
                        m = mm3(pe, bQ[:, i * S:(i + 1) * S],
                                lambda a: wq[:, h // 4, a, k, (h % 4) * DH:(h % 4 + 1) * DH],
                                lambda a: xT[:, a, k, :], k == 0, k == KT - 1)
                m.then_inc(s_qp, 1)

            def scores(n, j):
                t, g = J * n + j, 2 * j // HEADS_PER_GROUP
                pe.wait_ge(s_qlo, t + 1)
                pe.wait_ge(s_klo, 2 * n + 1 + g // 2)
                for i in range(2):
                    if not (isinstance(n, int) and n == 0 and j == 0):
                        pe.wait_ge(s_mx, 2 * t - 1 + i)
                    for r in range(ST):
                        m = mm3(pe, bS[i][:, r * S:(r + 1) * S], lambda a: qT[:, a, i, r * P:(r + 1) * P],
                                lambda a: kT[:, a, g, :], True, True)
                    m.then_inc(s_sp, 1)

            def p_transpose(n, j):
                t = J * n + j
                if not (isinstance(n, int) and n == 0 and j == 0):
                    pe.wait_ge(s_pTlo, 2 * t)
                for i in range(2):
                    pe.wait_ge((s_pn0, s_pn1)[i], t + 1)
                    for r in range(ST):
                        m = pe.transpose(bT0[:, i * S + r * P:i * S + (r + 1) * P], prob[:, j % 2, i, r * P:(r + 1) * P], ident[:])
                m.then_inc(s_pTp, 1)
                for i in range(2):
                    m = pe.transpose(bT1[:, i * P:(i + 1) * P], prob[:, j % 2, i, 2 * P:3 * P], ident[:])
                m.then_inc(s_pTp, 1)

            def attend(n, j):
                t, g = J * n + j, 2 * j // HEADS_PER_GROUP
                if not (isinstance(n, int) and n == 0 and j == 0):
                    pe.wait_ge(s_olo, t)
                pe.wait_ge(s_vlo, 2 * n + 1)
                pe.wait_ge(s_pTlo, 2 * t + 1)
                mm3(pe, bO[:, :], lambda a: v[:, a, 0, g * DH:(g + 1) * DH], lambda a: pT0[:, a, :], True, False)
                pe.wait_ge(s_vlo, 2 * n + 2)
                pe.wait_ge(s_pTlo, 2 * t + 2)
                late = bO[:, :].rearrange("p (h s) -> p h s", h=2)[:, :, P:2 * P]
                m = mm3(pe, late, lambda a: v[:, a, 1, g * DH:(g + 1) * DH],
                        lambda a: pT1[:, a, :].rearrange("p (h s) -> p h s", h=2), False, True)
                m.then_inc(s_op, 1)

            def out_project(n, j):
                pe.wait_ge(s_olo, J * n + j + 1)
                if j == 0 and not (isinstance(n, int) and n == 0):
                    pe.wait_ge(s_ya, n)
                for i in range(2):
                    h = 2 * j + i
                    for t in range(ST):
                        m = mm3(pe, bY[:, t * D:(t + 1) * D],
                                lambda a: oT[:, j % 2, a, i * S + t * P:i * S + (t + 1) * P],
                                lambda a: wp[:, h // 4, a, h % 4, :], h == 0 and t == 0, h == NH - 1)
                if j == J - 1:
                    m.then_inc(s_yp, 1)

            def weights(n, early=0, late=0):
                if isinstance(n, int) and n == 0:
                    if early:
                        pe.wait_ge(s_wsplit, early)
                    if late:
                        pe.wait_ge(s_wpool, late)

            def batch(n, last):
                for j in range(J):
                    p_transpose(n, j)
                    if j < J - 2 or not last:
                        scores(*ahead(n, j, 2))
                    if j == 0:
                        v_project(n, 1)
                    if isinstance(n, int) and n == 0:
                        if j == 2:
                            pe.wait_ge(s_vlo, 2)
                            pe.wait_ge(s_abs, 1)
                            pe.matmul(bM[:, 0:1], ones[:, :], abs_sum[:, 0:1], start=True, stop=True).then_inc(s_absp, 1)
                    elif j == 2:
                        pe.wait_ge(s_vlo, 2 * n + 2)
                        ternary_transpose(n - 1)
                    elif j == 3:
                        ternary(n - 1, bM)
                    if j == 6 and last:
                        linear_transpose(0)
                    if j in (5, 6) and not last:
                        k_project(n + 1, j - 5)
                    if j < J - 3 or not last:
                        weights(n, late={1: 2, 3: 4}.get(j, 0))
                        q_project(*ahead(n, j, 3))
                    if j == 4 and not last:
                        x_transpose(n + 1)
                    attend(n, j)
                    if j > 0:
                        weights(n, late={1: 1, 3: 3, 5: 5, 7: 6}.get(j, 0))
                        out_project(n, j - 1)
                if not last:
                    v_project(n + 1, 0)
                else:
                    linear_qkv(0, 0)
                    linear_qkv(0, 1)
                    linear_transpose(1)
                out_project(n, J - 1)

            def ternary_transpose(n):
                pe.wait_ge(s_fn, n + 1)
                transposes(bM, txn).then_inc(s_fT, 1)

            def ternary(n, out):
                pe.wait_ge(s_flo, n + 1)
                if isinstance(n, int) and n == 0:
                    pe.wait_ge(s_tern, 1)
                for t in range(ST):
                    for k in range(KT):
                        for a in range(2):
                            m = pe.matmul(out[:, t * D:(t + 1) * D], zT[:, a, k, t * P:(t + 1) * P], tern[:, k, :],
                                          start=k + a == 0, stop=k + a == 2, skip_group_check=True)
                m.then_inc(s_fp, 1)

            bQK, bV = (bS0, bS1), (bT0, bT1)

            def linear_transpose(n):
                pe.wait_ge(s_ln, n + 1)
                if isinstance(n, int) and n == 0:
                    pe.wait_ge(s_fa, NB - 1)
                elif isinstance(n, int) and n == 2:
                    pe.wait_ge(s_fz, NB)
                else:
                    pe.wait_ge(s_llo, n)
                transposes(bM, xn).then_inc(s_lT, 1)

            def linear_qkv(n, t):
                pe.wait_ge(s_llo, n + 1)
                if isinstance(n, int) and n == 0:
                    pe.wait_ge(s_lwlo, 1)
                    pe.wait_ge(s_pTlo, 2 * J * NB)
                else:
                    pe.wait_ge(s_lc, ST * n - ST + t + 1)
                for out, a0, a1 in ((bQK[t][:, :], 0, 2 * D), (bV[t][:, 0:D], 2 * D, 3 * D)):
                    for k in range(KT):
                        m = mm3(pe, out, lambda a: xT[:, a, k, t * P:(t + 1) * P], lambda a: lin_w[:, a, k, a0:a1],
                                k == 0, k == KT - 1)
                m.then_inc(s_lp, 1)

            def linear_sum(n):
                pe.wait_ge(s_lkv, n + 1)
                if not (isinstance(n, int) and n == 0):
                    pe.wait_ge(s_lY, n)
                for t in range(ST):
                    m = pe.matmul(bQ[:, 0:D], ones[:, :], kv[:, t, :], start=t == 0, stop=t == ST - 1)
                m.then_inc(s_lA, 1)

            def linear_y_transpose(n):
                pe.wait_ge(s_lY, n + 1)
                if not (isinstance(n, int) and n == 0):
                    pe.wait_ge(s_lylo, n)
                transposes(bO, y).then_inc(s_lyT, 1)

            def linear_out(n):
                pe.wait_ge(s_lylo, n + 1)
                if isinstance(n, int) and n == 0:
                    pe.wait_ge(s_lwlo, 2)
                    pe.wait_ge(s_fa, NB)
                else:
                    pe.wait_ge(s_la, n)
                for t in range(ST):
                    for k in range(KT):
                        m = mm3(pe, bY[:, t * D:(t + 1) * D], lambda a: yT[:, a, k, t * P:(t + 1) * P],
                                lambda a: lin_out[:, a, k, :], k == 0, k == KT - 1)
                m.then_inc(s_lo, 1)

            def linear(n, qkv_on=True, sum_on=True, out_on=True, next_on=True):
                if qkv_on:
                    linear_qkv(n, 0)
                if out_on:
                    linear_y_transpose(n - 2)
                if qkv_on:
                    linear_qkv(n, 1)
                if isinstance(n, int) and n == 1:
                    pe.wait_ge(s_llo, 2)
                    ternary_transpose(NB - 1)
                if next_on:
                    linear_transpose(n + 1)
                elif n <= NB:
                    gated_transpose(n - NB + 1)
                if sum_on:
                    linear_sum(n - 1)
                if isinstance(n, int) and n == 1:
                    ternary(NB - 1, bY)
                if isinstance(n, int) and n > NB:
                    gate_and_up(0, 1)
                if out_on:
                    linear_out(n - 2)
                if isinstance(n, int) and n == NB:
                    gate_and_up(0, 0)

            bG, bU, bD = (bS0, bS1), (bT0, bT1), (bQ, bO)

            def gated_transpose(b):
                pe.wait_ge(s_gn, b + 1)
                if isinstance(b, int) and b == 0:
                    pe.wait_ge(s_llo, NB)
                else:
                    pe.wait_ge(s_glo, b)
                transposes(bM, xn).then_inc(s_gT, 1)

            def gate_and_up(m, i):
                u = HT * m + i
                rows = P if i < HT - 1 else HLAST
                if i == 0:
                    pe.wait_ge(s_glo, 2 * m + 2)
                if isinstance(m, int) and m == 0 and i == 0:
                    pe.wait_ge(s_lwlo, 3)
                    pe.wait_ge(s_lc, ST * NB)
                for g, (bank_of, done) in enumerate(((bG, s_gg), (bU, s_gu_))):
                    if not (isinstance(m, int) and m == 0 and i < 2):
                        wait_apart(pe, s_gh, u - 1)
                    for k in range(KT):
                        mm = mm3(pe, bank_of[i % 2][0:rows, :], lambda a: gate_up[:, a, g, k, i * P:i * P + rows],
                                 lambda a: xT4[:, m, a, k, :], k == 0, k == KT - 1)
                    mm.then_inc(done, 1)

            def down_project(m, i):
                u = HT * m + i
                rows = P if i < HT - 1 else HLAST
                pe.wait_ge(s_ghl, u + 1)
                if i == 0:
                    if isinstance(m, int) and m == 0:
                        pe.wait_ge(s_lwlo, 4)
                        pe.wait_ge(s_lylo, NB)
                    else:
                        pe.wait_ge(s_gsc, 2 * m)
                for b in range(2):
                    for t in range(ST):
                        at = b * S + t * P
                        mm = mm3(pe, bD[b][:, t * D:(t + 1) * D], lambda a: hT[0:rows, i % 2, a, at:at + P],
                                 lambda a: down[0:rows, a, i, :], i == 0 and t == 0, i == HT - 1)
                    if i == HT - 1:
                        mm.then_inc(s_gd, 1)

            def gated(m, first, last):
                for i in range(HT):
                    if not (first and i < 2):
                        gate_and_up(m, i)
                    if i > 0:
                        down_project(m, i - 1)
                    elif not first:
                        down_project(m - 1, HT - 1)
                    if i in (3, 4) and not last:
                        gated_transpose(2 * m - 1 + i)

            pe.wait_ge(s_const, 4)
            x_transpose(0)
            weights(0, early=1)
            k_project(0, 0)
            weights(0, early=2)
            q_project(0, 0)
            k_project(0, 1)
            scores(0, 0)
            q_project(0, 1)
            scores(0, 1)
            weights(0, early=4)
            q_project(0, 2)
            weights(0, early=3)
            v_project(0, 0)
            batch(0, False)
            with pe.Fori(1, NB - 1) as n:
                batch(n, False)
            batch(NB - 1, True)

            linear(1, out_on=False)
            linear(2)
            with pe.Fori(3, NB - 1) as n:
                linear(n)
            linear(NB - 1, next_on=False)
            linear(NB, qkv_on=False, next_on=False)
            linear(NB + 1, qkv_on=False, sum_on=False, next_on=False)

            gated(0, True, False)
            with pe.Fori(1, NB // 2 - 1) as m:
                gated(m, False, False)
            gated(NB // 2 - 1, False, True)
            down_project(NB // 2 - 1, HT - 1)

        @block.scalar
        def _(act):
            def hi(out, src, waits, done):
                act.wait_ge(*waits)
                act.activation(out, src, ACT.Copy).then_inc(done, 1)

            def early(i):
                n = CHUNKS.index(EARLY[i])
                act.wait_ge(s_raw[n], 16)
                act.activation(chunk_parts(EARLY[i])[1][0], raw[:, n % NRAW, :], ACT.Copy).then_inc(s_whi, 1)

            def late_hi(i):
                n = CHUNKS.index(LATE[i])
                act.wait_ge(s_raw[n], 16)
                act.activation(chunk_parts(LATE[i])[1][0], raw[:, n % NRAW, :], ACT.Copy).then_inc(s_wph, 1)

            def x_hi(n):
                hi(xT[:, 0].rearrange("p k s -> p (k s)"), bM[:, :], (s_xTp, n + 1), s_xhi)

            def k_hi(n, half):
                hi(kT[:, 0, 2 * half:2 * half + 2].rearrange("p g s -> p (g s)"), bM[:, :], (s_kp, 2 * n + half + 1), s_khi)

            def v_hi(n, t):
                hi(v[:, 0, t], bM[:, :], (s_vp, 2 * n + t + 1), s_vhi)

            def q_hi(n, j):
                hi(qT[:, 0].rearrange("p h s -> p (h s)"), bQ[:, :], (s_qp, J * n + j + 1), s_qhi)

            def pT_hi(n, j):
                t = J * n + j
                hi(pT0[:, 0], bT0[:, :], (s_pTp, 2 * t + 1), s_pThi)
                hi(pT1[:, 0], bT1[:, 0:2 * P], (s_pTp, 2 * t + 2), s_pThi)

            def o_hi(n, j):
                hi(oT[:, j % 2, 0], bO[:, :], (s_op, J * n + j + 1), s_ohi)

            def exps(n, j):
                t = J * n + j
                act.wait_ge(s_nm, t + 1)
                for i in range(2):
                    for r, (a, b) in enumerate(((0, P), (P, 3 * P))):
                        m = act.activation(prob[:, j % 2, i, a:b], prob[:, j % 2, i, a:b], ACT.Exp, scale=SCALE,
                                           bias=negmax[:, 2 * i + r:2 * i + r + 1],
                                           accum_out=rowsum[:, 2 * i + r:2 * i + r + 1])
                m.then_inc(s_ex, 1)

            def batch(n, last):
                for j in range(J):
                    pT_hi(n, j)
                    if isinstance(n, int) and n == 0 and j + 2 < len(LATE):
                        late_hi(j + 2)
                    if j == 0 and isinstance(n, int) and n == 0:
                        act.wait_ge(s_rawt, 16)
                        act.activation(abs_w, raw_t, ACT.Abs, accum_out=abs_sum[:, 0:1]).then_inc(s_abs, 1)
                    if j == 2 and not (isinstance(n, int) and n == 0):
                        ternary_hi(n - 1)
                    if j == 6 and last:
                        linear_x_hi(0)
                    if j == 0:
                        v_hi(n, 1)
                    if j in (5, 6) and not last:
                        k_hi(n + 1, j - 5)
                    if j < J - 3 or not last:
                        q_hi(*ahead(n, j, 3))
                    if j == 4 and not last:
                        x_hi(n + 1)
                    if j == J - 1:
                        o_hi(n, j)
                    if j < J - 2 or not last:
                        exps(*ahead(n, j, 2))
                    if j < J - 1:
                        o_hi(n, j)
                    if j >= 5 and last:
                        late_layer_hi(j - 5)
                    if j in (5, 7) and last:
                        linear_residual((j - 5) // 2)
                if not last:
                    v_hi(n + 1, 0)

            def late_layer_hi(i):
                src, (high, _), bias, _ = LAYER_WEIGHTS[i]
                act.wait_ge(s_rawl[i], 16 if i < 3 else 32)
                if i == 0:
                    act.wait_ge(s_qp, J * NB)
                act.activation(high, src, ACT.Copy, bias=bias).then_inc(s_lwhi, 1)
                if i == 3:
                    src, (high, _), bias, _ = LAYER_WEIGHTS[4]
                    act.activation(high, src, ACT.Copy, bias=bias).then_inc(s_lwhi, 1)

            def ternary_hi(n):
                act.wait_ge(s_fT, n + 1)
                z = z_of(n)
                for k in range(KT):
                    m = act.activation(z[:, k * S:(k + 1) * S], bM[:, k * S:(k + 1) * S], ACT.Identity,
                                       bias=gamma_beta[:, 1, k:k + 1], scale=gamma_beta[:, 0, k:k + 1])
                m.then_inc(s_fz, 1)
                act.wait_ge(s_fz, n + 1)
                act.activation(zT[:, 0].rearrange("p k s -> p (k s)"), z, ACT.Copy).then_inc(s_fhi, 1)

            def linear_x_hi(n):
                hi(xT[:, 0].rearrange("p k s -> p (k s)"), bM[:, :], (s_lT, n + 1), s_lhi)

            def gated_x_hi(b, m=0, q=None):
                q = b if q is None else q
                act.wait_ge(s_gT, b + 1)
                act.activation(xT4[:, m, 0, :, q * S:(q + 1) * S], bM[:, :].rearrange("p (k s) -> p k s", k=KT),
                               ACT.Copy).then_inc(s_ghi, 1)

            def linear_residual(n):
                act.wait_ge(s_lrs, n + 1)
                for t in range(ST):
                    xs = x[:, bass.ds(ST * n + t, 1), :].rearrange("p o d -> p (o d)")
                    m = act.activation(xs, xs, ACT.Identity, bias=residual_scale[:, 1, t:t + 1],
                                       scale=residual_scale[:, 0, t:t + 1])
                m.then_inc(s_lres1, 1)

            def linear(n, q, qkv_on=True, out_on=True, next_on=True, norm_on=True):
                if out_on:
                    hi(yT[:, 0].rearrange("p k s -> p (k s)"), bO[:, :], (s_lyT, n - 1), s_lyhi)
                if isinstance(n, int) and n == 1:
                    ternary_hi(NB - 1)
                if next_on:
                    linear_x_hi(n + 1)
                elif n <= NB:
                    gated_x_hi(n - NB + 1)
                if qkv_on:
                    act.wait_ge(s_lr, ST * n + ST)
                    for t in range(ST):
                        m = act.activation(k_square[:, t, :], qkv[:, q, t, D:2 * D], ACT.Square, accum_out=k_norm[:, t:t + 1])
                    m.then_inc(s_lsq, 1)
                if norm_on:
                    linear_residual(n + 2)

            bG = (bS0, bS1)

            def gated_tile(m, i):
                u = HT * m + i
                rows = P if i < HT - 1 else HLAST
                act.wait_ge(s_gg, u + 1)
                if not (isinstance(m, int) and m == 0 and i == 0):
                    act.wait_ge(s_gh, u)
                act.activation(gate[0:rows, :], bG[i % 2][0:rows, :], ACT.Silu, scale=s_gu[0:rows, 0, i:i + 1]).then_inc(s_gs, 1)
                act.wait_ge(s_gh, u + 1)
                act.activation(hT[0:rows, i % 2, 0], hidden[i % 2][0:rows, :], ACT.Copy).then_inc(s_ghh, 1)

            def gated(m, first, last):
                for i in range(HT):
                    if not (first and i == 0):
                        gated_tile(m, i)
                    if i in (3, 4) and not last:
                        gated_x_hi(2 * m - 1 + i, m + 1, i - 3)

            early(0)
            x_hi(0)
            early(1)
            k_hi(0, 0)
            q_hi(0, 0)
            early(2)
            k_hi(0, 1)
            early(3)
            q_hi(0, 1)
            late_hi(0)
            exps(0, 0)
            late_hi(1)
            q_hi(0, 2)
            exps(0, 1)
            v_hi(0, 0)
            batch(0, False)
            act.wait_ge(s_tab, 16 * 5)
            with act.Fori(1, NB - 1) as n:
                batch(n, False)
            batch(NB - 1, True)

            linear(0, 0, out_on=False)
            late_layer_hi(3)
            linear(1, 1, out_on=False)
            with act.Fori(1, NB // 2 - 1) as m:
                for q in range(2):
                    linear(2 * m + q, q)
            linear(NB - 2, 0, norm_on=False)
            linear(NB - 1, 1, next_on=False, norm_on=False)
            linear(NB, 0, qkv_on=False, next_on=False, norm_on=False)
            gated_tile(0, 0)
            linear(NB + 1, 1, qkv_on=False, next_on=False, norm_on=False)

            gated(0, True, False)
            with act.Fori(1, NB // 2 - 1) as m:
                gated(m, False, False)
            gated(NB // 2 - 1, False, True)

        @block.vector
        def _(dve):
            def x_tile(b, t):
                return x[:, bass.ds(ST * b + t, 1), :].rearrange("p o d -> p (o d)")

            def ln_moments(call, b):
                for t in range(ST):
                    m = dve.bn_stats(stats[:, t, :], x_tile(b, t))
                m.then_inc(s_st, 1)
                wait_apart(dve, s_st, call + 1)
                for t in range(ST):
                    m = dve.bn_aggr(moments[:, t, :], stats[:, t, :])
                m.then_inc(s_mo, 1)

            def ln_apply(call, b):
                dve.wait_ge(s_mo, call + 1)
                dve.wait_ge(s_rs, call + 1)
                for t in range(ST):
                    m = dve.tensor_scalar(xn[:, t, :], x_tile(b, t), moments[:, t, 0:1], rstd[:, t:t + 1],
                                          ALU.subtract, ALU.mult)
                return m

            def lo(out, src, hi, waits, done):
                dve.wait_ge(*waits)
                dve.tensor_tensor(out, src, f32(hi), ALU.subtract).then_inc(done, 1)

            def early(i):
                n = CHUNKS.index(EARLY[i])
                hi, low = chunk_parts(EARLY[i])[1]
                dve.wait_ge(s_raw[n], 16)
                lo(low, raw[:, n % NRAW, :], hi, (s_whi, i + 1), s_wsplit)

            def x_apply(n):
                if not (isinstance(n, int) and n == 0):
                    dve.wait_ge(s_xTp, n)
                ln_apply(n, n).then_inc(s_xn, 1)

            def x_lo(n):
                lo(xT[:, 1].rearrange("p k s -> p (k s)"), bM[:, :], xT[:, 0].rearrange("p k s -> p (k s)"),
                   (s_xhi, n + 1), s_xlo)

            def k_lo(n, half):
                part = [kT[:, a, 2 * half:2 * half + 2].rearrange("p g s -> p (g s)") for a in range(2)]
                lo(part[1], bM[:, :], part[0], (s_khi, 2 * n + half + 1), s_klo)

            def v_lo(n, t):
                lo(v[:, 1, t], bM[:, :], v[:, 0, t], (s_vhi, 2 * n + t + 1), s_vlo)

            def q_lo(n, j):
                part = [qT[:, a].rearrange("p h s -> p (h s)") for a in range(2)]
                lo(part[1], bQ[:, :], part[0], (s_qhi, J * n + j + 1), s_qlo)

            def pT_lo(n, j, part):
                pT, src = ((pT0, bT0[:, :]), (pT1, bT1[:, 0:2 * P]))[part]
                lo(pT[:, 1], src, pT[:, 0], (s_pThi, 2 * (J * n + j) + part + 1), s_pTlo)

            def o_lo(n, j):
                lo(oT[:, j % 2, 1], bO[:, :], oT[:, j % 2, 0], (s_ohi, J * n + j + 1), s_olo)

            def row_max(n, j):
                t = J * n + j
                for i in range(2):
                    wait_apart(dve, s_sp, 2 * t + i + 1)
                    for r, (a, b) in enumerate(((0, P), (P, 3 * P))):
                        m = dve.tensor_tensor_reduce(prob[:, j % 2, i, a:b], bS[i][:, r * S:r * S + b - a],
                                                     mask[:, (1 - r) * P:2 * P], 1.0, MASKED, ALU.add, ALU.max,
                                                     rowmax[:, 2 * i + r:2 * i + r + 1])
                    m.then_inc(s_mx, 1)
                dve.wait_ge(s_mx, 2 * t + 2)
                dve.tensor_scalar(negmax[:, :], rowmax[:, :], -SCALE, None, ALU.mult).then_inc(s_nm, 1)

            def normalise(n, j):
                t = J * n + j
                dve.wait_ge(s_ex, t + 1)
                dve.reciprocal(rowinv[:, j % 2, :], rowsum[:, :]).then_inc(s_ri, 1)
                dve.wait_ge(s_ri, t + 1)
                for r, (a, b) in enumerate(((0, P), (P, 3 * P))):
                    m = dve.tensor_scalar(prob[:, j % 2, 1, a:b], prob[:, j % 2, 1, a:b],
                                          rowinv[:, j % 2, 2 + r:3 + r], None, ALU.mult)
                m.then_inc(s_pn1, 1)

            def add_y(n):
                dve.wait_ge(s_yp, n + 1)
                xs = x[:, bass.ds(ST * n, ST), :].rearrange("p t d -> p (t d)")
                dve.tensor_tensor(xs, bY[:, :], xs, ALU.add).then_inc(s_ya, 1)

            def batch(n, last):
                for j in range(J):
                    pT_lo(n, j, 0)
                    pT_lo(n, j, 1)
                    if j == 6 and last:
                        linear_x_lo(0)
                    if j < J - 2 or not last:
                        row_max(*ahead(n, j, 2))
                    if j == 0:
                        v_lo(n, 1)
                    if not (isinstance(n, int) and n == 0):
                        if j == 1:
                            ternary_apply(n - 1)
                        if j == 2:
                            ternary_lo(n - 1)
                        if j == 3:
                            add_bank(n - 1, bM, s_fp, s_fb, s_fa)
                    if j in (5, 6) and not last:
                        k_lo(n + 1, j - 5)
                    if j < J - 3 or not last:
                        q_lo(*ahead(n, j, 3))
                    if j == 4 and not last:
                        x_lo(n + 1)
                    if j == 0 and not (isinstance(n, int) and n == 0):
                        ternary_moments(n - 1)
                    if j == 2 and not last:
                        if isinstance(n, int):
                            dve.wait_ge(s_x[n + 1], 16)
                        ln_moments(n + 1, n + 1)
                    if j == 3 and not last:
                        x_apply(n + 1)
                    if j == J - 1:
                        o_lo(n, j)
                    if j < J - 2 or not last:
                        normalise(*ahead(n, j, 2))
                    if j < J - 1:
                        o_lo(n, j)
                    if j == 3 and isinstance(n, int) and n == 0:
                        ternary_weights()
                    if j == 4 and last:
                        ln_moments(NB, 0)
                    if j == 5 and last:
                        linear_apply(0)
                        dve.wait_ge(s_lrs, 1)
                        ln_moments(NB + 1, 1)
                    if j == 7 and last:
                        linear_apply(1)
                    if j >= 5 and last:
                        late_layer_lo(j - 5)
                if not last:
                    v_lo(n + 1, 0)
                    add_y(n)

            def ternary_weights():
                dve.wait_ge(s_absp, 1)
                dve.tensor_scalar(scale_eps[:, :], bM[:, 0:1], 1.0 / (D * D), EPS, ALU.mult, ALU.add).then_inc(s_half, 1)
                dve.wait_ge(s_half, 1)
                dve.tensor_scalar(half_scale[:, 0:1], scale_eps[:, :], 0.5, None, ALU.mult)
                dve.tensor_scalar(half_scale[:, 1:2], scale_eps[:, :], -0.5, None, ALU.mult).then_inc(s_half, 1)
                dve.wait_ge(s_half, 2)
                dve.tensor_scalar(ternary_pos[:, :], raw_t, half_scale[:, 0:1], None, ALU.is_gt).then_inc(s_tpos, 1)
                dve.wait_ge(s_tpos, 1)
                dve.scalar_tensor_tensor(ternary_neg[:, :], raw_t, half_scale[:, 1:2], ternary_pos[:, :], ALU.is_lt,
                                         ALU.subtract).then_inc(s_tpos, 1)
                dve.wait_ge(s_tpos, 2)
                dve.tensor_scalar(tern.rearrange("p k n -> p (k n)"), ternary_neg[:, :], -1.0, None, ALU.mult).then_inc(s_tern, 1)

            def late_layer_lo(i):
                for n in ((i,) if i < 3 else (3, 4)):
                    src, (high, low), bias, rows = LAYER_WEIGHTS[n]
                    dve.wait_ge(s_lwhi, n + 1)
                    m = dve.scalar_tensor_tensor(low, src, bias, f32(high), ALU.add, ALU.subtract)
                m.then_inc(s_lwlo, 1)

            def ternary_moments(n):
                wait_apart(dve, s_ya, n + 1)
                for t in range(ST):
                    m = dve.bn_stats(t_stats[:, t, :], x_tile(n, t))
                m.then_inc(s_fst, 1)
                wait_apart(dve, s_fst, n + 1)
                for t in range(ST):
                    m = dve.bn_aggr(t_moments[:, t, :], t_stats[:, t, :])
                m.then_inc(s_fmo, 1)
                dve.wait_ge(s_fmo, n + 1)
                dve.tensor_scalar(t_variance[:, :], t_moments[:, :, 1], 1.0 + EPS, EPS * EPS, ALU.mult, ALU.add).then_inc(s_fvar, 1)

            def ternary_apply(n):
                dve.wait_ge(s_frs, n + 1)
                for t in range(ST):
                    m = dve.tensor_scalar(txn[:, t, :], x_tile(n, t), t_moments[:, t, 0:1], t_rstd[:, t:t + 1],
                                          ALU.subtract, ALU.mult)
                m.then_inc(s_fn, 1)

            def ternary_lo(n):
                lo(zT[:, 1].rearrange("p k s -> p (k s)"), z_of(n), zT[:, 0].rearrange("p k s -> p (k s)"), (s_fhi, n + 1), s_flo)

            def add_bank(n, out_bank, out_ready, residual_ready, done):
                dve.wait_ge(out_ready, n + 1)
                dve.wait_ge(residual_ready, n + 1)
                xs = x[:, bass.ds(ST * n, ST), :].rearrange("p t d -> p (t d)")
                dve.tensor_tensor(xs, out_bank[:, :], xs, ALU.add).then_inc(done, 1)

            def linear_apply(n):
                if isinstance(n, int) and n == 0:
                    dve.wait_ge(s_xTp, NB)
                else:
                    dve.wait_ge(s_lT, n)
                    dve.wait_ge(s_lres1, n)
                ln_apply(NB + n, n).then_inc(s_ln, 1)
                dve.tensor_scalar(residual_scale[:, 0, :], rstd[:, :], 1.0, None, ALU.add)
                dve.scalar_tensor_tensor(residual_scale[:, 1, :], moments[:, :, 0], -1.0, rstd[:, :], ALU.mult,
                                         ALU.mult).then_inc(s_lrs, 1)

            def linear_x_lo(n):
                lo(xT[:, 1].rearrange("p k s -> p (k s)"), bM[:, :], xT[:, 0].rearrange("p k s -> p (k s)"), (s_lhi, n + 1), s_llo)

            def linear_qkv(n, q, t):
                dve.wait_ge(s_lp, ST * n + t + 1)
                if t == 0 and not (isinstance(n, int) and n < 2):
                    dve.wait_ge(s_lY, n - 1)
                u = ST * n + t
                dve.tensor_tensor(qkv[:, q, t, 0:2 * D], bQK[t][:, :], b_in[:, 0:2 * D], ALU.add).then_inc(s_le, 1)
                dve.tensor_tensor(qkv[:, q, t, 2 * D:3 * D], bV[t][:, 0:D], b_in[:, 2 * D:3 * D], ALU.add)
                dve.wait_ge(s_le, u + 1)
                if not (isinstance(n, int) and n == 0):
                    dve.wait_ge(s_lr, u - 1)
                qk = qkv[:, q, t, 0:2 * D].rearrange("p (c d) -> p c d", c=2)[:, :, 0:P]
                dve.tensor_tensor(rot1[:, t], qk, rope[:, 0, t], ALU.mult).then_inc(s_lc, 1)

            def linear_kv(n, q):
                dve.wait_ge(s_lki, n + 1)
                if not (isinstance(n, int) and n == 0):
                    dve.wait_ge(s_lA, n)
                for t in range(ST):
                    m = dve.scalar_tensor_tensor(kv[:, t, :], qkv[:, q, t, D:2 * D], k_inv[:, t:t + 1],
                                                 qkv[:, q, t, 2 * D:3 * D], ALU.mult, ALU.mult)
                m.then_inc(s_lkv, 1)

            def linear_y(n, q):
                dve.wait_ge(s_lA, n + 1)
                for t in range(ST):
                    m = dve.tensor_tensor(y[:, t, :], bQ[:, 0:D], qkv[:, q, t, 0:D], ALU.mult)
                m.then_inc(s_lY, 1)

            def linear(n, q, qkv_on=True, sum_on=True, out_on=True, next_on=True, norm_on=True):
                if sum_on:
                    linear_kv(n - 1, 1 - q)
                if qkv_on:
                    linear_qkv(n, q, 0)
                if norm_on:
                    ln_moments(NB + 2 + n, n + 2)
                elif n < NB:
                    ln_moments(NB + 2 + n, n + 2 - NB)
                if out_on:
                    part = [yT[:, a].rearrange("p k s -> p (k s)") for a in range(2)]
                    lo(part[1], bO[:, :], part[0], (s_lyhi, n - 1), s_lylo)
                if qkv_on:
                    linear_qkv(n, q, 1)
                if isinstance(n, int) and n == 1:
                    ternary_apply(NB - 1)
                if next_on:
                    linear_x_lo(n + 1)
                elif n <= NB:
                    gated_x_lo(n - NB + 1)
                if sum_on:
                    linear_y(n - 1, 1 - q)
                if norm_on:
                    linear_apply(n + 2)
                elif n < NB:
                    gated_apply(n + 2 - NB)
                if out_on:
                    add_bank(n - 2, bY, s_lo, s_lres, s_la)

            def gated_apply(b):
                if isinstance(b, int) and b == 0:
                    dve.wait_ge(s_lT, NB)
                else:
                    dve.wait_ge(s_gT, b)
                ln_apply(2 * NB + b, b).then_inc(s_gn, 1)

            def gated_x_lo(b, m=0, q=None):
                q = b if q is None else q
                dve.wait_ge(s_ghi, b + 1)
                dve.tensor_tensor(xT4[:, m, 1, :, q * S:(q + 1) * S], bM[:, :].rearrange("p (k s) -> p k s", k=KT),
                                  f32(xT4[:, m, 0, :, q * S:(q + 1) * S]), ALU.subtract).then_inc(s_glo, 1)

            def hidden_tile(m, i):
                u = HT * m + i
                rows = P if i < HT - 1 else HLAST
                dve.wait_ge(s_gu_, u + 1)
                dve.wait_ge(s_gs, u + 1)
                if not (isinstance(m, int) and m == 0 and i < 2):
                    dve.wait_ge(s_ghl, u - 1)
                dve.scalar_tensor_tensor(hidden[i % 2][0:rows, :], bU[i % 2][0:rows, :], s_gu[0:rows, 1, i:i + 1],
                                         gate[0:rows, :], ALU.mult, ALU.mult).then_inc(s_gh, 1)
                dve.wait_ge(s_ghh, u + 1)
                dve.tensor_tensor(hT[0:rows, i % 2, 1], hidden[i % 2][0:rows, :], f32(hT[0:rows, i % 2, 0]),
                                  ALU.subtract).then_inc(s_ghl, 1)

            def scale_down(b, q):
                dve.wait_ge(s_gd, b + 1)
                dve.wait_ge(s_ga, b + 1)
                for t in range(ST):
                    m = dve.tensor_tensor(scaled[q][:, t, :], bD[q][:, t * D:(t + 1) * D], biases[:, 2, :], ALU.mult)
                m.then_inc(s_gsc, 1)

            def gated(m, first, last):
                for i in range(HT):
                    if not (first and i == 0):
                        hidden_tile(m, i)
                    if i == 0 and not first:
                        for q in range(2):
                            scale_down(2 * m - 2 + q, q)
                    if not last:
                        if i in (3, 4):
                            gated_x_lo(2 * m - 1 + i, m + 1, i - 3)
                        if i in (2, 3):
                            gated_apply(2 * m + i)
                        if i == 2:
                            dve.wait_ge(s_gn, 2 * m + 3)
                        if i in (1, 2):
                            ln_moments(2 * NB + 2 * m + 1 + i, 2 * m + 1 + i)

            bQK, bV, bU, bD = (bS0, bS1), (bT0, bT1), (bT0, bT1), (bQ, bO)
            dve.wait_ge(s_const, 4)
            dve.wait_ge(s_x[0], 16)
            ln_moments(0, 0)
            x_apply(0)
            early(0)
            x_lo(0)
            early(1)
            k_lo(0, 0)
            q_lo(0, 0)
            early(2)
            k_lo(0, 1)
            row_max(0, 0)
            q_lo(0, 1)
            early(3)
            normalise(0, 0)
            row_max(0, 1)
            q_lo(0, 2)
            normalise(0, 1)
            v_lo(0, 0)
            batch(0, False)
            dve.wait_ge(s_tab, 16 * 5)
            for b in range(2, NB):
                dve.wait_ge(s_x[b], 16)
            with dve.Fori(1, NB - 1) as n:
                batch(n, False)
            batch(NB - 1, True)

            linear(0, 0, sum_on=False, out_on=False)
            add_y(NB - 1)
            ternary_moments(NB - 1)
            linear(1, 1, out_on=False)
            ternary_lo(NB - 1)
            late_layer_lo(3)
            add_bank(NB - 1, bY, s_fp, s_fb, s_fa)
            with dve.Fori(1, NB // 2 - 1) as m:
                for q in range(2):
                    linear(2 * m + q, q)
            linear(NB - 2, 0, norm_on=False)
            linear(NB - 1, 1, norm_on=False, next_on=False)
            linear(NB, 0, qkv_on=False, next_on=False, norm_on=False)
            hidden_tile(0, 0)
            linear(NB + 1, 1, qkv_on=False, sum_on=False, next_on=False, norm_on=False)

            gated(0, True, False)
            with dve.Fori(1, NB // 2 - 1) as m:
                gated(m, False, False)
            gated(NB // 2 - 1, False, True)
            for q in range(2):
                scale_down(NB - 2 + q, q)


def kernel(**inputs):
    import concourse.bacc as bacc
    from concourse.bass_utils import run_bass_kernel_spmd

    def tiles(w):
        return w.reshape(-1, P, w.shape[1]).transpose(1, 0, 2)

    def rows(*vectors):
        return np.ascontiguousarray(np.stack([np.broadcast_to(r, (P, r.shape[-1])) for r in vectors], 1))

    w = {k: np.asarray(a) for k, a in inputs.items()}
    qkv = w["L0_attn_weight_qkv"].reshape(NG, HEADS_PER_GROUP + 2, DH, D)
    proj = w["L0_attn_weight_proj"].T.reshape(4, 4, DH, D)
    last = {k: w[k].T for k in ("L1_ffn_wq_gate", "L1_ffn_wq_up", "L1_ffn_wq_down")}
    inv_freq = np.float32(1.0) / np.float32(10000.0) ** (np.arange(0, P, 2, dtype=np.float32) / np.float32(P))
    angle = np.repeat(np.arange(S, dtype=np.float32)[:, None] * inv_freq[None, :], 2, axis=1).reshape(ST, P, P)
    sign = np.where(np.arange(P) % 2 == 0, np.float32(-1.0), np.float32(1.0))
    rope = np.stack([np.cos(angle), np.sin(angle) * sign]).astype(np.float32)
    hid = np.zeros((2, HT * P), np.float32)
    hid[0, :HID], hid[1, :HID] = w["L1_ffn_s_gate"], w["L1_ffn_s_up"]
    arrays = {
        "x": w["L0_attn_x"],
        "wk": tiles(qkv[:, HEADS_PER_GROUP].reshape(NG * DH, D).T),
        "wv": tiles(qkv[:, HEADS_PER_GROUP + 1].reshape(NG * DH, D).T),
        "wq": np.stack([tiles(qkv[g, :HEADS_PER_GROUP].reshape(-1, D).T) for g in range(NG)]),
        "wp": proj.transpose(0, 2, 1, 3),
        "wt": tiles(w["L0_ffn_weight"].T),
        "gamma_beta": np.stack([w["L0_ffn_ln_gamma"].reshape(KT, P), w["L0_ffn_ln_beta"].reshape(KT, P)]).transpose(2, 0, 1),
        "biases": rows(w["L0_ffn_bias"], w["L1_attn_b_out"], w["L1_ffn_s_down"]),
        "b_in": rows(w["L1_attn_b_in"]),
        "w_in": tiles(w["L1_attn_W_in"].T),
        "w_out": tiles(w["L1_attn_W_out"].T),
        "w_gu": np.stack([tiles(last["L1_ffn_wq_gate"]), tiles(last["L1_ffn_wq_up"])], 1),
        "s_gu": hid.reshape(2, HT, P).transpose(2, 0, 1),
        "w_down": last["L1_ffn_wq_down"],
        "rope": np.repeat(rope.transpose(2, 0, 1, 3)[:, :, :, None], 2, axis=3),
    }
    flat = {"wk", "wv", "wt", "w_in", "w_out", "w_gu", "b_in"}
    nc = bacc.Bacc("TRN2", target_bir_lowering=False, num_devices=1)
    aps = []
    for name, a in arrays.items():
        if name in flat:
            a = a.reshape(P, -1)
        if name in ("wq", "wp"):
            a = a.reshape(4, P, -1)
        arrays[name] = a = np.ascontiguousarray(a)
        aps.append(nc.dram_tensor("in_" + name, a.shape, mybir.dt.from_np(a.dtype), kind="ExternalInput").ap())
    out = nc.dram_tensor("out", (NB, S, D), F32, kind="ExternalOutput").ap()
    build(nc, *aps, out)
    return run_bass_kernel_spmd(nc, [{"in_" + k: a for k, a in arrays.items()}], core_ids=[0]).results[0]["out"]
```

```python
from contextlib import ExitStack

import numpy as np

import concourse.bass as bass
from concourse import mybir

F32 = mybir.dt.float32
F32R = mybir.dt.float32r
I32 = mybir.dt.int32
ALU = mybir.AluOpType
ACT = mybir.ActivationFunctionType
AX = mybir.AxisListType

P = 128
NB = 8
S = 256
D = 256
KT = D // P
ST = S // P
NH = 16
NG = 4
DH = 128
J = NH // 2
HEADS_PER_GROUP = NH // NG
SCALE = float(1.0 / np.sqrt(np.float32(DH)))
EPS = 1e-5
MASKED = -3.0e38
HID = 704
ZERO_POINT = 128.0
HT = -(-HID // P)
HLAST = HID - (HT - 1) * P
CH = 1024
NRAW = 7
PASSES = ((0, 0), (0, 1), (1, 0))


def build(nc, x_in, wk_in, wv_in, wq_in, wp_in, wt_in, gb_in, bias_in, bin_in, win_in, wout_in, wgu_in, sgu_in,
          wd_in, rope_in, out):
    with ExitStack() as ctx:
        def sb(name, shape, dt=F32):
            return ctx.enter_context(nc.sbuf_tensor(name, shape, dt))

        def sem(name):
            return ctx.enter_context(nc.semaphore(name))

        x = sb("x", [P, NB * ST, D])
        xn = sb("xn", [P, ST, D])
        xT = sb("xT", [P, 2, KT, S], F32R)
        big = sb("big", [P, 12 * CH], F32R)
        wk = big[:, 0:2 * CH].rearrange("p (a k n) -> p a k n", a=2, k=KT)
        wv = big[:, 2 * CH:4 * CH].rearrange("p (a k n) -> p a k n", a=2, k=KT)
        wq = big[:, 4 * CH:12 * CH].rearrange("p (c a k n) -> p c a k n", c=4, a=2, k=KT)
        wp = sb("wp", [P, 4, 2, 4, D], F32R)
        raw = sb("raw", [P, NRAW, CH])
        kT = sb("kT", [P, 2, NG, S], F32R)
        v = sb("v", [P, 2, ST, NG * DH], F32R)
        qT = sb("qT", [P, 2, 2, S], F32R)
        prob = sb("prob", [P, 2, 2, 3 * P])
        pT0 = sb("pT0", [P, 2, 2 * S], F32R)
        pT1 = sb("pT1", [P, 2, 2 * P], F32R)
        oT = sb("oT", [P, 2, 2, 2 * S], F32R)
        rowmax = sb("rowmax", [P, 4])
        negmax = sb("negmax", [P, 4])
        rowsum = sb("rowsum", [P, 4])
        rowinv = sb("rowinv", [P, 2, 4])
        stats = sb("stats", [P, ST, 6])
        moments = sb("moments", [P, ST, 2])
        rstd = sb("rstd", [P, ST])
        exponent = sb("exponent", [P, 4])
        ident = sb("ident", [P, P])
        lin_w = big[:, 0:6 * 512].rearrange("p (a k n) -> p a k n", a=2, k=KT)
        gate_up = big[:, 3072:3072 + 8 * HID].rearrange("p (a g k n) -> p a g k n", a=2, g=2, k=KT)
        down = big[:, 3072 + 8 * HID:3072 + 8 * HID + 2 * HT * D].rearrange("p (a i n) -> p a i n", a=2, i=HT)
        w1 = sb("w1", [P, 6 * D], F32R)
        tern = w1[:, 0:2 * D].rearrange("p (k n) -> p k n", k=KT)
        lin_out = w1[:, 2 * D:6 * D].rearrange("p (a k n) -> p a k n", a=2, k=KT)
        xT4 = wp[:, :, :, :, :].rearrange("p c a h n -> p (c a h n)").rearrange("p (m a k s) -> p m a k s", m=NB // 2, a=2, k=KT)
        hT = [room.rearrange("p (a s) -> p a s", a=2) for room in
              (kT[:, 0].rearrange("p g s -> p (g s)"), kT[:, 1].rearrange("p g s -> p (g s)"),
               v[:, 0].rearrange("p t n -> p (t n)"))]
        xTs = (xT, qT[:, :, :, :])
        k_room = kT[:, :, :, :].rearrange("p a g s -> p (a g s)")
        v_bias = k_room[:, 0:2 * D].rearrange("p (a n) -> p a n", a=2)
        mean_rows = k_room[:, 2 * D:2 * D + P]
        zT = sb("zT", [P, 2, KT, S], F32R)
        yT = zT
        rawf = raw[:, :, :].rearrange("p c n -> p (c n)")
        raw_in, raw_out = rawf[:, 512:2048], rawf[:, 2048:2560]
        raw_gu, raw_d = rawf[:, 2560:2560 + 4 * HID], rawf[:, 2560 + 4 * HID:2560 + 4 * HID + HT * D]
        qkv = sb("qkv", [P, 2, ST, 3 * D])
        y = sb("y", [P, ST, D])
        residual_scale = sb("residual_scale", [P, 2, ST])
        k_norm = sb("k_norm", [P, ST])
        k_inv = sb("k_inv", [P, ST])
        raw_t, abs_w = qkv[:, 1, 1, 0:2 * D], qkv[:, 1, 0, 0:2 * D]
        ternary_pos, ternary_neg = qkv[:, 0, 0, 0:2 * D], qkv[:, 0, 1, 0:2 * D]
        txn = y
        z_parts = (qkv[:, 1, 1, 0:2 * D], rawf[:, 512:1024])
        flat_prob = prob[:, :, :, :].rearrange("p b h n -> p (b h n)")
        rot1 = rawf[:, 0:4 * P].rearrange("p (t c d) -> p t c d", t=ST, c=2)
        rot2 = flat_prob[:, 512:1024].rearrange("p (t c d) -> p t c d", t=ST, c=2)
        kv = flat_prob[:, 1024:1536].rearrange("p (t d) -> p t d", t=ST)
        gate = flat_prob[:, 0:512]
        k_square = gate.rearrange("p (t d) -> p t d", t=ST)
        hidden = [rawf[:, 512 * (i + 1):512 * (i + 2)] for i in range(2)]
        scaled = (y, qkv[:, 0, 0, 0:2 * D].rearrange("p (t d) -> p t d", t=ST))
        biases = sb("biases", [P, 3, D])
        b_in = sb("b_in", [P, 3 * D])
        rope = sb("rope", [P, 2, ST, 2, P])
        gamma_beta = sb("gamma_beta", [P, 2, KT])
        s_gu = sb("s_gu", [P, 2, HT])
        ones = sb("ones", [P, P])
        abs_sum = sb("abs_sum", [P, 1])
        lo_sums = sb("lo_sums", [P, 4])
        lo_sum = sb("lo_sum", [P, 1])
        lo_flag = sb("lo_flag", [P, 1], I32)
        scale_eps = sb("scale_eps", [P, 1])
        half_scale = sb("half_scale", [P, 2])
        t_stats = sb("ternary_stats", [P, ST, 6])
        t_moments = sb("ternary_moments", [P, ST, 2])
        t_variance = sb("ternary_variance", [P, ST])
        t_rstd = sb("ternary_rstd", [P, ST])
        variance = sb("variance", [P, ST])
        k_bound = sb("k_bound", [P, ST])
        mask = sb("mask", [P, 2 * P])

        bank = [ctx.enter_context(nc.psum_tensor(f"bank{i}", [P, 512], F32)) for i in range(8)]
        bM, bQ, bS0, bS1, bT0, bT1, bO, bY = bank
        bS = (bS0, bS1)

        s_x = [sem(f"x_landed{b}") for b in range(NB)]
        s_raw = [sem(f"raw_landed{c}") for c in range(10)]
        s_const = sem("constants_made")
        s_wsplit = sem("early_weights_split")
        s_whi = sem("early_weights_hi")
        s_wpool = sem("late_weights_split")
        s_wph = sem("late_weights_hi")
        s_st = sem("ln_stats")
        s_mo = sem("ln_moments")
        s_var = sem("ln_variance_plus_eps")
        s_rs = sem("ln_rstd")
        s_xn = sem("xn_ready")
        s_xTp = sem("xT_in_psum")
        s_xhi = sem("xT_hi")
        s_xlo = sem("xT_lo")
        s_kp = sem("k_in_psum")
        s_khi = sem("k_hi")
        s_klo = sem("k_lo")
        s_vp = sem("v_in_psum")
        s_vhi = sem("v_hi")
        s_vlo = sem("v_lo")
        s_qp = sem("q_in_psum")
        s_qhi = sem("q_hi")
        s_qlo = sem("q_lo")
        s_sp = sem("scores_in_psum")
        s_sc = sem("scores_rows0_masked")
        s_mx = sem("rowmax_taken")
        s_nm = sem("negmax_ready")
        s_ex = sem("exp_done")
        s_ri = sem("rowinv_ready")
        s_pn0 = sem("probs_ready_head0")
        s_pn1 = sem("probs_ready_head1")
        s_pTp = sem("pT_in_psum")
        s_pThi = sem("pT_hi")
        s_pTlo = sem("pT_lo")
        s_op = sem("o_in_psum")
        s_ohi = sem("o_hi")
        s_olo = sem("o_lo")
        s_yp = sem("y_in_psum")
        s_ya = sem("y_added")
        s_tab = sem("tables_landed")
        s_rawt = sem("raw_ternary_landed")
        s_rawl = [sem(f"raw_late_landed{i}") for i in range(4)]
        s_zero = sem("zero_point_subtracted")
        s_lwhi = sem("late_layers_weights_hi")
        s_lwlo = sem("linear_weights_split")
        s_gwlo = sem("gated_weights_split")
        s_dwlo = sem("down_weights_split")
        s_los = sem("lo_parts_summed")
        s_lop = sem("lo_sums_in_psum")
        s_lor = sem("lo_sum_ready")
        s_flag = sem("lo_flag_ready")
        s_abs = sem("abs_weights_summed")
        s_absp = sem("abs_sum_in_psum")
        s_half = sem("half_scale_ready")
        s_tpos = sem("ternary_positive")
        s_tern = sem("ternary_ready")
        s_fst = sem("ternary_ln_stats")
        s_fmo = sem("ternary_ln_moments")
        s_fvar = sem("ternary_ln_variances_joined")
        s_frs = sem("ternary_ln_rstd")
        s_fn = sem("ternary_xn_ready")
        s_fb = sem("ternary_bias_added")
        s_fT = sem("ternary_xT_in_psum")
        s_fz = sem("ternary_z_ready")
        s_fhi = sem("ternary_z_hi")
        s_flo = sem("ternary_z_lo")
        s_fp = sem("ternary_out_in_psum")
        s_fa = sem("ternary_added")
        s_ln = sem("linear_xn_ready")
        s_lres = sem("linear_residual_ready")
        s_lres1 = sem("linear_residual_half")
        s_lT = sem("linear_xT_in_psum")
        s_lhi = sem("linear_xT_hi")
        s_llo = sem("linear_xT_lo")
        s_lp = sem("linear_qkv_in_psum")
        s_le = sem("linear_qkv_ready")
        s_lc = sem("rope_cosine_products")
        s_lv = sem("linear_v_ready")
        s_bhi = sem("v_bias_hi")
        s_blo = sem("v_bias_split")
        s_lr1 = sem("rope_sine_products")
        s_lrs = sem("linear_residual_scale")
        s_lr = sem("rope_done")
        s_lsq = sem("k_norm_squared")
        s_lkb = sem("k_norm_bounded")
        s_lki = sem("k_inv_ready")
        s_lkv = sem("kv_ready")
        s_lA = sem("A_in_psum")
        s_lY = sem("linear_y_ready")
        s_lyT = sem("linear_yT_in_psum")
        s_lyhi = sem("linear_yT_hi")
        s_lylo = sem("linear_yT_lo")
        s_lo = sem("linear_out_in_psum")
        s_la = sem("linear_added")
        s_gn = sem("gated_xn_ready")
        s_gT = sem("gated_xT_in_psum")
        s_ghi = sem("gated_xT_hi")
        s_glo = sem("gated_xT_lo")
        s_gg = sem("gate_in_psum")
        s_gu_ = sem("up_in_psum")
        s_gs = sem("gate_ready")
        s_gh = sem("hidden_ready")
        s_ghh = sem("hidden_hi")
        s_ghl = sem("hidden_lo")
        s_gd = sem("down_in_psum")
        s_gsc = sem("down_scaled")
        s_ga = sem("gated_added")
        s_gl = sem("gated_last_pair_added")
        s_carrier = sem("wait_carrier")
        s_out = sem("out_stored")

        x_v = x_in.rearrange("b (t p) d -> b p t d", p=P)
        out_v = out.rearrange("b (t p) d -> b p t d", p=P)

        EARLY = ["k", ("q", 0), "v", ("q", 1)]
        LATE = [("p", 0), ("q", 2), ("p", 1), ("q", 3), ("p", 2), ("p", 3)]
        CHUNKS = EARLY[:3] + LATE[:1] + EARLY[3:] + LATE[1:]

        def chunk_parts(c):
            if c == "k":
                return wk_in, [big[:, a * CH:(a + 1) * CH] for a in range(2)]
            if c == "v":
                return wv_in, [big[:, (2 + a) * CH:(3 + a) * CH] for a in range(2)]
            if c[0] == "q":
                at = 4 + 2 * c[1]
                return wq_in[c[1]], [big[:, (at + a) * CH:(at + 1 + a) * CH] for a in range(2)]
            return wp_in[c[1]], [wp[:, c[1], a].rearrange("p h n -> p (h n)") for a in range(2)]

        def piece(src, room, first, last, rows=P):
            return src[0:rows, first:last], [part[0:rows, first:last] for part in room], rows

        in_room = [big[:, a * 1536:(a + 1) * 1536] for a in range(2)]
        gu_room = [big[:, 3072 + a * 4 * HID:3072 + (a + 1) * 4 * HID] for a in range(2)]
        out_room = [w1[:, (2 + 2 * a) * D:(4 + 2 * a) * D] for a in range(2)]
        down_room = [down[:, a].rearrange("p i n -> p (i n)") for a in range(2)]
        LAYER_WEIGHTS = [
            piece(raw_in, in_room, 0, 768), piece(raw_in, in_room, 768, 1536),
            piece(raw_gu, gu_room, 0, 2 * HID), piece(raw_gu, gu_room, 2 * HID, 4 * HID),
            piece(raw_out, out_room, 0, 512),
            piece(raw_d, down_room, 0, (HT - 1) * D), piece(raw_d, down_room, (HT - 1) * D, HT * D, HLAST),
        ]
        IN0, IN1, GU0, GU1, OUT, DOWN0, DOWN1 = range(7)
        LANDED = {IN0: (0, 16), IN1: (0, 16), OUT: (1, 16), GU0: (2, 16), GU1: (2, 16), DOWN0: (3, 32), DOWN1: (3, 32)}
        INTS = (GU0, GU1, DOWN0, DOWN1)

        def wait_apart(eng, semaphore, value):
            eng.wait_ge(semaphore, value)
            if not isinstance(value, int):
                eng.sem_inc(s_carrier, 1)

        def ahead(n, j, steps):
            return (n, j + steps) if j + steps < J else (n + 1, j + steps - J)

        def ternary_bank(n):
            return bO if isinstance(n, int) and n == NB - 1 else bM

        def v_bank(n, t):
            return ((bQ, bM) if isinstance(n, int) and n == 0 else (bT0, bT1))[t][:, 0:D]

        def z_of(n):
            return z_parts[isinstance(n, int) and n == NB - 1]

        def f32(ap):
            return ap.bitcast(F32)

        block = ctx.enter_context(nc.Block())

        @block.sync
        def _(sp):
            sp.dma_start(x[:, 0:ST, :], x_v[0]).then_inc(s_x[0], 16)
            for n, c in enumerate(CHUNKS):
                if n >= NRAW:
                    old = CHUNKS[n - NRAW]
                    sp.wait_ge(*((s_wsplit, EARLY.index(old) + 1) if old in EARLY else (s_wpool, LATE.index(old) + 1)))
                sp.dma_start(raw[:, n % NRAW, :], chunk_parts(c)[0]).then_inc(s_raw[n], 16)
                if n == 3:
                    sp.dma_start(x[:, ST:2 * ST, :], x_v[1]).then_inc(s_x[1], 16)
            sp.dma_start(raw_t, wt_in).then_inc(s_rawt, 16)
            for b in range(2, NB):
                sp.dma_start(x[:, ST * b:ST * (b + 1), :], x_v[b]).then_inc(s_x[b], 16)
            for dst, src in ((biases, bias_in), (b_in, bin_in), (gamma_beta, gb_in), (s_gu, sgu_in), (rope, rope_in)):
                sp.dma_start(dst[:], src).then_inc(s_tab, 16)
            sp.wait_ge(s_wsplit, len(EARLY))
            sp.wait_ge(s_wpool, len(LATE))
            sp.dma_start(raw_in, win_in).then_inc(s_rawl[0], 16)
            sp.dma_start(raw_out, wout_in).then_inc(s_rawl[1], 16)
            sp.dma_start(raw_gu.bitcast(I32), wgu_in).then_inc(s_rawl[2], 16)
            wd = raw_d.bitcast(I32).rearrange("p (i n) -> p i n", i=HT)
            sp.dma_start(wd[:, 0:HT - 1, :], wd_in[0:(HT - 1) * P, :].rearrange("(i p) n -> p i n", p=P)).then_inc(s_rawl[3], 16)
            sp.dma_start(wd[0:HLAST, HT - 1, :], wd_in[(HT - 1) * P:HID, :]).then_inc(s_rawl[3], 16)
            for b in range(NB):
                sp.wait_ge(*((s_ga, b + 3) if b < NB - 2 else (s_gl, b - NB + 3)))
                sp.dma_start(out_v[b], x[:, ST * b:ST * (b + 1), :]).then_inc(s_out, 16)
            sp.wait_ge(s_out, 16 * NB)

        @block.gpsimd
        def _(pool):
            pool.memset(ident[:], 0.0).then_inc(s_const, 1)
            pool.memset(mask[:], 0.0).then_inc(s_const, 1)
            pool.memset(exponent[:, :], -0.5)
            pool.memset(ones[:, :], 1.0)
            pool.memset(lo_sums[:, :], 0.0)
            pool.wait_ge(s_const, 2)
            pool.affine_select(out=ident[:], in_=ident[:], compare_op=ALU.not_equal, fill=1.0, base=0,
                               pattern=[[-1, P]], channel_multiplier=1).then_inc(s_const, 1)
            pool.affine_select(out=mask[:, P:2 * P], in_=mask[:, P:2 * P], compare_op=ALU.is_ge, fill=MASKED,
                               base=0, pattern=[[-1, P]], channel_multiplier=1).then_inc(s_const, 1)
            def inv_std(call):
                wait_apart(pool, s_mo, call + 1)
                pool.tensor_scalar(variance[:, :], moments[:, :, 1], EPS, None, ALU.add).then_inc(s_var, 1)
                pool.wait_ge(s_var, call + 1)
                pool.tensor_tensor(rstd[:, :], variance[:, :], exponent[:, 0:ST], ALU.pow).then_inc(s_rs, 1)

            def inv_std_twice(n):
                wait_apart(pool, s_fvar, n + 1)
                pool.tensor_tensor(t_rstd[:, :], t_variance[:, :], exponent[:, 0:ST], ALU.pow).then_inc(s_frs, 1)

            def add_row(n, row):
                xs = x[:, bass.ds(ST * n, ST), :]
                return pool.tensor_tensor(xs, xs, biases[:, row:row + 1, :].to_broadcast([P, ST, D]), ALU.add)

            def ternary_bias(n):
                wait_apart(pool, s_fn, n + 1)
                add_row(n, 0).then_inc(s_fb, 1)

            def rotate(n, q, t):
                u = ST * n + t
                qk = qkv[:, q, t, 0:2 * D].rearrange("p (c d) -> p c d", c=2)[:, :, 0:P]
                pairs = qk.rearrange("p c (i e) -> p c i e", e=2)
                sin = rope[:, 1, t].rearrange("p c (i e) -> p c i e", e=2)
                turned = rot2[:, t].rearrange("p c (i e) -> p c i e", e=2)
                wait_apart(pool, s_le, u + 1)
                for e in range(2):
                    m = pool.tensor_tensor(turned[:, :, :, e], pairs[:, :, :, 1 - e], sin[:, :, :, e], ALU.mult)
                m.then_inc(s_lr1, 1)
                wait_apart(pool, s_lr1, u + 1)
                wait_apart(pool, s_lc, u + 1)
                pool.tensor_tensor(qk, rot1[:, t], rot2[:, t], ALU.add).then_inc(s_lr, 1)

            def k_inverse(n):
                wait_apart(pool, s_lsq, n + 1)
                pool.tensor_scalar(k_bound[:, :], k_norm[:, :], 1e-24, None, ALU.max).then_inc(s_lkb, 1)
                pool.wait_ge(s_lkb, n + 1)
                pool.tensor_tensor(k_inv[:, :], k_bound[:, :], exponent[:, 0:ST], ALU.pow).then_inc(s_lki, 1)

            def linear_bias(n):
                wait_apart(pool, s_lres1, n + 1)
                add_row(n, 1).then_inc(s_lres, 1)

            def normalise(n, j):
                wait_apart(pool, s_ri, J * n + j + 1)
                for r, (a, b) in enumerate(((0, P), (P, 3 * P))):
                    m = pool.tensor_scalar(prob[:, j % 2, 0, a:b], prob[:, j % 2, 0, a:b], rowinv[:, j % 2, r:r + 1], None, ALU.mult)
                m.then_inc(s_pn0, 1)

            def late_lo(i):
                n = CHUNKS.index(LATE[i])
                hi, lo = chunk_parts(LATE[i])[1]
                pool.wait_ge(s_raw[n], 16)
                pool.wait_ge(s_wph, i + 1)
                pool.tensor_tensor(lo, raw[:, n % NRAW, :], f32(hi), ALU.subtract).then_inc(s_wpool, 1)

            def gated_weights_lo(n, count):
                src, (high, low), _ = LAYER_WEIGHTS[n]
                pool.wait_ge(s_lwhi, n + 1)
                m = pool.tensor_tensor(low, src, f32(high), ALU.subtract)
                if count:
                    m.then_inc(s_gwlo, 1)

            def batch(n, last):
                for j in range(J):
                    if j < J - 2 or not last:
                        normalise(*ahead(n, j, 2))
                    if not (isinstance(n, int) and n == 0):
                        if j == 0:
                            inv_std_twice(n - 1)
                        if j == 1:
                            ternary_bias(n - 1)
                    if j == 2:
                        inv_std(n + 1)
                    if j == 5 and last:
                        inv_std(NB + 1)
                    if j == 5 and last:
                        linear_bias(0)
                        gated_weights_lo(GU0, False)
                    if j == 6 and last:
                        gated_weights_lo(GU1, True)
                        linear_bias(1)
                    if isinstance(n, int) and n == 0 and j + 2 < len(LATE):
                        late_lo(j + 2)

            inv_std(0)
            late_lo(0)
            normalise(0, 0)
            late_lo(1)
            normalise(0, 1)
            batch(0, False)
            pool.wait_ge(s_tab, 16 * 5)
            with pool.Fori(1, NB - 1) as n:
                batch(n, False)
            batch(NB - 1, True)


            def linear(n, q, last):
                rotate(n, q, 0)
                inv_std(NB + 2 + n)
                rotate(n, q, 1)
                if isinstance(n, int) and n == 1:
                    ternary_bias(NB - 1)
                k_inverse(n)
                if not last:
                    linear_bias(n + 2)

            linear(0, 0, False)
            inv_std_twice(NB - 1)
            linear(1, 1, False)
            with pool.Fori(1, NB // 2 - 1) as m:
                for q in range(2):
                    linear(2 * m + q, q, False)
            for q in range(2):
                linear(NB - 2 + q, q, True)

            def finish(b, q):
                xs = x[:, bass.ds(ST * b, ST), :]
                wait_apart(pool, s_gsc, b + 1)
                pool.tensor_tensor(xs, xs, scaled[q][:, :, :], ALU.add).then_inc(s_ga, 1)

            pool.sem_inc(s_ga, 2)

            def gated(m, first, last):
                if not last:
                    inv_std(2 * NB + 2 * m + 2)
                if not first:
                    for q in range(2):
                        finish(2 * m - 2 + q, q)
                if not last:
                    inv_std(2 * NB + 2 * m + 3)

            gated(0, True, False)
            with pool.Fori(1, NB // 2 - 1) as m:
                gated(m, False, False)
            gated(NB // 2 - 1, False, True)

        def mm3(pe, out, lhs, rhs, first, last, passes=PASSES):
            for i, (a, b) in enumerate(passes):
                m = pe.matmul(out, lhs(a), rhs(b), start=first and i == 0, stop=last and i == len(passes) - 1,
                              skip_group_check=True)
            return m

        @block.tensor
        def _(pe):
            def transposes(out, src):
                for k in range(KT):
                    for t in range(ST):
                        m = pe.transpose(out[:, k * S + t * P:k * S + (t + 1) * P], src[:, t, k * P:(k + 1) * P], ident[:])
                return m

            def x_transpose(n):
                pe.wait_ge(s_xn, n + 1)
                if not (isinstance(n, int) and n == 0):
                    pe.wait_ge(*((s_half, 1) if isinstance(n, int) and n == 1 else (s_fa, n - 1)))
                transposes(bM, xn).then_inc(s_xTp, 1)

            def k_project(n, half):
                if half == 0:
                    pe.wait_ge(s_xlo, n + 1)
                else:
                    pe.wait_ge(s_klo, 2 * n + 1)
                for i in range(2):
                    g = 2 * half + i
                    for k in range(KT):
                        m = mm3(pe, bM[:, i * S:(i + 1) * S], lambda a: wk[:, a, k, g * DH:(g + 1) * DH],
                                lambda a: xT[:, a, k, :], k == 0, k == KT - 1)
                m.then_inc(s_kp, 1)

            def v_project(n, t):
                if t == 0:
                    pe.wait_ge(s_klo, 2 * n + 2)
                else:
                    pe.wait_ge(s_vlo, 2 * n + 1)
                for k in range(KT):
                    m = mm3(pe, bM[:, :], lambda a: xT[:, a, k, t * P:(t + 1) * P], lambda a: wv[:, a, k, :],
                            k == 0, k == KT - 1)
                m.then_inc(s_vp, 1)

            def q_project(n, j):
                if not (isinstance(n, int) and n == 0 and j == 0):
                    pe.wait_ge(s_qlo, J * n + j)
                for i in range(2):
                    h = 2 * j + i
                    for k in range(KT):
                        m = mm3(pe, bQ[:, i * S:(i + 1) * S],
                                lambda a: wq[:, h // 4, a, k, (h % 4) * DH:(h % 4 + 1) * DH],
                                lambda a: xT[:, a, k, :], k == 0, k == KT - 1)
                m.then_inc(s_qp, 1)

            def scores(n, j):
                t, g = J * n + j, 2 * j // HEADS_PER_GROUP
                pe.wait_ge(s_qlo, t + 1)
                pe.wait_ge(s_klo, 2 * n + 1 + g // 2)
                first = isinstance(n, int) and n == 0 and j == 0
                if not first:
                    pe.wait_ge(s_mx, 2 * t)
                for i in range(2):
                    for a in range(2):
                        m = pe.matmul(bS0[:, i * S:(i + 1) * S], qT[:, a, i, 0:P], kT[:, :, g, 0:P], start=a == 0,
                                      stop=a == 1, skip_group_check=True)
                m.then_inc(s_sp, 1)
                for i in range(2):
                    m = mm3(pe, bS1[:, i * S:(i + 1) * S], lambda a: qT[:, a, i, P:2 * P], lambda a: kT[:, a, g, :], True, True)
                m.then_inc(s_sp, 1)

            def p_transpose(n, j):
                t = J * n + j
                if not (isinstance(n, int) and n == 0 and j == 0):
                    pe.wait_ge(s_pTlo, 2 * t)
                for i in range(2):
                    pe.wait_ge((s_pn0, s_pn1)[i], t + 1)
                    for r in range(ST):
                        m = pe.transpose(bT0[:, i * S + r * P:i * S + (r + 1) * P], prob[:, j % 2, i, r * P:(r + 1) * P], ident[:])
                m.then_inc(s_pTp, 1)
                for i in range(2):
                    m = pe.transpose(bT1[:, i * P:(i + 1) * P], prob[:, j % 2, i, 2 * P:3 * P], ident[:])
                m.then_inc(s_pTp, 1)

            def attend(n, j):
                t, g = J * n + j, 2 * j // HEADS_PER_GROUP
                if not (isinstance(n, int) and n == 0 and j == 0):
                    pe.wait_ge(s_olo, t)
                pe.wait_ge(s_vlo, 2 * n + 1)
                pe.wait_ge(s_pTlo, 2 * t + 1)
                mm3(pe, bO[:, :], lambda a: v[:, a, 0, g * DH:(g + 1) * DH], lambda a: pT0[:, a, :], True, False)
                pe.wait_ge(s_vlo, 2 * n + 2)
                pe.wait_ge(s_pTlo, 2 * t + 2)
                late = bO[:, :].rearrange("p (h s) -> p h s", h=2)[:, :, P:2 * P]
                m = mm3(pe, late, lambda a: v[:, a, 1, g * DH:(g + 1) * DH],
                        lambda a: pT1[:, a, :].rearrange("p (h s) -> p h s", h=2), False, True)
                m.then_inc(s_op, 1)

            def out_project(n, j):
                pe.wait_ge(s_olo, J * n + j + 1)
                if j == 0 and not (isinstance(n, int) and n == 0):
                    pe.wait_ge(s_ya, n)
                for i in range(2):
                    h = 2 * j + i
                    for t in range(ST):
                        m = mm3(pe, bY[:, t * D:(t + 1) * D],
                                lambda a: oT[:, j % 2, a, i * S + t * P:i * S + (t + 1) * P],
                                lambda a: wp[:, h // 4, a, h % 4, :], h == 0 and t == 0, h == NH - 1)
                if j == J - 1:
                    m.then_inc(s_yp, 1)

            def weights(n, early=0, late=0):
                if isinstance(n, int) and n == 0:
                    if early:
                        pe.wait_ge(s_wsplit, early)
                    if late:
                        pe.wait_ge(s_wpool, late)

            def batch(n, last):
                for j in range(J):
                    p_transpose(n, j)
                    if j < J - 2 or not last:
                        scores(*ahead(n, j, 2))
                    if j == 0:
                        v_project(n, 1)
                    if isinstance(n, int) and n == 0:
                        if j == 2:
                            pe.wait_ge(s_vlo, 2)
                            pe.wait_ge(s_abs, 1)
                            pe.matmul(bM[:, 0:1], ones[:, :], abs_sum[:, 0:1], start=True, stop=True).then_inc(s_absp, 1)
                    elif j == 3:
                        ternary(n - 1, bM)
                    if j in (5, 6) and not last:
                        k_project(n + 1, j - 5)
                    if j < J - 3 or not last:
                        weights(n, late={1: 2, 3: 4}.get(j, 0))
                        q_project(*ahead(n, j, 3))
                    if j == 2 and not (isinstance(n, int) and n == 0):
                        pe.wait_ge(s_vlo, 2 * n + 2)
                        ternary_transpose(n - 1)
                    if j == 4:
                        linear_transpose(0) if last else x_transpose(n + 1)
                    attend(n, j)
                    if j >= 6 and last:
                        linear_qkv(0, 0, j - 6)
                    if j > 0:
                        weights(n, late={1: 1, 3: 3, 5: 5, 7: 6}.get(j, 0))
                        out_project(n, j - 1)
                if not last:
                    v_project(n + 1, 0)
                else:
                    linear_transpose(1)
                out_project(n, J - 1)

            def ternary_transpose(n):
                pe.wait_ge(s_fn, n + 1)
                transposes(ternary_bank(n), txn).then_inc(s_fT, 1)

            def ternary(n, out):
                pe.wait_ge(s_flo, n + 1)
                if isinstance(n, int) and n == 0:
                    pe.wait_ge(s_tern, 1)
                for t in range(ST):
                    for k in range(KT):
                        for a in range(2):
                            m = pe.matmul(out[:, t * D:(t + 1) * D], zT[:, a, k, t * P:(t + 1) * P], tern[:, k, :],
                                          start=k + a == 0, stop=k + a == 2, skip_group_check=True)
                m.then_inc(s_fp, 1)

            bQK = (bS0, bS1)

            def linear_transpose(n):
                pe.wait_ge(s_ln, n + 1)
                if isinstance(n, int) and n == 0:
                    pe.wait_ge(s_fa, NB - 1)
                else:
                    pe.wait_ge(s_llo, n)
                if isinstance(n, int) and n == 1:
                    pe.wait_ge(s_lv, ST)
                transposes(bM, xn).then_inc(s_lT, 1)

            def linear_qkv(n, q, t):
                pe.wait_ge(s_llo, n + 1)
                if isinstance(n, int) and n == 0:
                    pe.wait_ge(s_blo, 1)
                    pe.wait_ge(s_lwlo, 2)
                    pe.wait_ge(s_mx, 2 * J * NB)
                    pe.wait_ge(s_qlo, J * NB)
                else:
                    pe.wait_ge(s_le, ST * n - ST + t + 1)
                    pe.wait_ge(s_lv, ST * n - ST + t + 1)
                for out, a0, a1 in ((bQK[t][:, :], 0, 2 * D), (v_bank(n, t), 2 * D, 3 * D)):
                    for k in range(KT):
                        m = mm3(pe, out, lambda a: xTs[q][:, a, k, t * P:(t + 1) * P], lambda a: lin_w[:, a, k, a0:a1],
                                k == 0, k == KT - 1 and a0 == 0)
                for a in range(2):
                    m = pe.matmul(v_bank(n, t), mean_rows, v_bias[:, a, :], start=False, stop=a == 1, skip_group_check=True)
                m.then_inc(s_lp, 1)

            def linear_sum(n):
                pe.wait_ge(s_lkv, n + 1)
                if not (isinstance(n, int) and n == 0):
                    pe.wait_ge(s_lY, n)
                for t in range(ST):
                    m = pe.matmul(bQ[:, 0:D], ones[:, :], kv[:, t, :], start=t == 0, stop=t == ST - 1)
                m.then_inc(s_lA, 1)

            def linear_y_transpose(n):
                pe.wait_ge(s_lY, n + 1)
                if not (isinstance(n, int) and n == 0):
                    pe.wait_ge(s_lylo, n)
                transposes(bO, y).then_inc(s_lyT, 1)

            def linear_out(n):
                pe.wait_ge(s_lylo, n + 1)
                if isinstance(n, int) and n == 0:
                    pe.wait_ge(s_lwlo, 3)
                    pe.wait_ge(s_fa, NB)
                else:
                    pe.wait_ge(s_la, n)
                for t in range(ST):
                    for k in range(KT):
                        m = mm3(pe, bY[:, t * D:(t + 1) * D], lambda a: yT[:, a, k, t * P:(t + 1) * P],
                                lambda a: lin_out[:, a, k, :], k == 0, k == KT - 1)
                m.then_inc(s_lo, 1)

            def linear(n, q, qkv_on=True, sum_on=True, out_on=True, next_on=True, weight_parts=2):
                if qkv_on:
                    linear_qkv(n, q, 0)
                if isinstance(n, int) and n == 2:
                    ternary(NB - 1, bY)
                if out_on:
                    linear_y_transpose(n - 2)
                if next_on:
                    linear_transpose(n + 1)
                elif n <= NB:
                    gated_transpose(n - NB + 1)
                if qkv_on:
                    linear_qkv(n, q, 1)
                if isinstance(n, int) and n == NB:
                    gate_and_up(0, 0, weight_parts)
                if sum_on:
                    linear_sum(n - 1)
                if isinstance(n, int) and n == 1:
                    pe.wait_ge(s_olo, J * NB)
                    ternary_transpose(NB - 1)
                if isinstance(n, int) and n > NB:
                    gate_and_up(0, 1, weight_parts)
                if out_on:
                    linear_out(n - 2)

            bG, bU, bD = (bS0, bS1), (bT0, bT1), (bQ, bO)

            def gated_transpose(b):
                pe.wait_ge(s_gn, b + 1)
                if isinstance(b, int) and b == 0:
                    pe.wait_ge(s_flag, 1)
                else:
                    pe.wait_ge(s_glo, b)
                transposes(bM, xn).then_inc(s_gT, 1)

            def gate_and_up(m, i, weight_parts):
                u = HT * m + i
                rows = P if i < HT - 1 else HLAST
                if i == 0:
                    pe.wait_ge(s_glo, 2 * m + 2)
                if isinstance(m, int) and m == 0 and i == 0:
                    pe.wait_ge(s_gwlo, 1)
                    pe.wait_ge(s_le, ST * NB)
                    pe.wait_ge(s_lv, ST * NB)
                for g, (bank_of, done) in enumerate(((bG, s_gg), (bU, s_gu_))):
                    if not (isinstance(m, int) and m == 0 and i < 2):
                        wait_apart(pe, s_gh, u - 1)
                    for k in range(KT):
                        mm = mm3(pe, bank_of[i % 2][0:rows, :], lambda a: gate_up[:, a, g, k, i * P:i * P + rows],
                                 lambda a: xT4[:, m, a, k, :], k == 0, k == KT - 1, PASSES[:1 + weight_parts])
                    mm.then_inc(done, 1)

            def down_project(m, i, weight_parts):
                u = HT * m + i
                rows = P if i < HT - 1 else HLAST
                pe.wait_ge(s_ghl, u + 1)
                if i == 0:
                    if isinstance(m, int) and m == 0:
                        pe.wait_ge(s_dwlo, 1)
                        pe.wait_ge(s_lylo, NB)
                for b in range(2):
                    if i == 0 and not (isinstance(m, int) and m == 0):
                        pe.wait_ge(s_gsc, 2 * m - 1 + b)
                    for t in range(ST):
                        at = b * S + t * P
                        mm = mm3(pe, bD[b][:, t * D:(t + 1) * D], lambda a: hT[i % 3][0:rows, a, at:at + P],
                                 lambda a: down[0:rows, a, i, :], i == 0 and t == 0, i == HT - 1,
                                 PASSES if weight_parts == 2 else PASSES[::2])
                    if i == HT - 1:
                        mm.then_inc(s_gd, 1)

            def gated(m, first, last, weight_parts):
                for i in range(HT):
                    if not (first and i < 2):
                        gate_and_up(m, i, weight_parts)
                    if i > 1:
                        down_project(m, i - 2, weight_parts)
                    elif not first:
                        down_project(m - 1, HT - 2 + i, weight_parts)
                    if i in (2, 4) and not last:
                        gated_transpose(2 * m + 1 + i // 2)

            def keep_busy(count):
                for _ in range(count):
                    pe.transpose(bY[:, 0:P], ident[:], ident[:])

            pe.wait_ge(s_const, 4)
            keep_busy(20)
            x_transpose(0)
            keep_busy(8)
            weights(0, early=1)
            k_project(0, 0)
            weights(0, early=2)
            q_project(0, 0)
            k_project(0, 1)
            scores(0, 0)
            q_project(0, 1)
            scores(0, 1)
            weights(0, early=4)
            q_project(0, 2)
            weights(0, early=3)
            v_project(0, 0)
            batch(0, False)
            with pe.Fori(1, NB - 1) as n:
                batch(n, False)
            batch(NB - 1, True)

            linear(1, 1, out_on=False)
            linear(2, 0)
            with pe.Fori(0, NB // 2 - 2) as m:
                for q in range(2):
                    linear(2 * m + 3 + q, 1 - q)
            pe.wait_ge(s_llo, NB)
            pe.wait_ge(s_los, 4)
            pe.matmul(bM[:, 0:4], ones[:, :], lo_sums[:, :], start=True, stop=True).then_inc(s_lop, 1)
            linear(NB - 1, 1, next_on=False)

            def rest(weight_parts):
                linear(NB, 0, qkv_on=False, next_on=False, weight_parts=weight_parts)
                linear(NB + 1, 1, qkv_on=False, sum_on=False, next_on=False, weight_parts=weight_parts)
                gated(0, True, False, weight_parts)
                with pe.Fori(1, NB // 2 - 1) as m:
                    gated(m, False, False, weight_parts)
                gated(NB // 2 - 1, False, True, weight_parts)
                for i in (HT - 2, HT - 1):
                    down_project(NB // 2 - 1, i, weight_parts)

            pe.wait_ge(s_flag, 1)
            flag = pe.value_load(lo_flag[0:1, 0:1])
            with pe.If(flag != 0):
                rest(2)
            with pe.Else():
                rest(1)

        @block.scalar
        def _(act):
            def hi(out, src, waits, done):
                act.wait_ge(*waits)
                act.activation(out, src, ACT.Copy).then_inc(done, 1)

            def early(i):
                n = CHUNKS.index(EARLY[i])
                act.wait_ge(s_raw[n], 16)
                act.activation(chunk_parts(EARLY[i])[1][0], raw[:, n % NRAW, :], ACT.Copy).then_inc(s_whi, 1)

            def late_hi(i):
                n = CHUNKS.index(LATE[i])
                act.wait_ge(s_raw[n], 16)
                act.activation(chunk_parts(LATE[i])[1][0], raw[:, n % NRAW, :], ACT.Copy).then_inc(s_wph, 1)

            def x_hi(n):
                hi(xT[:, 0].rearrange("p k s -> p (k s)"), bM[:, :], (s_xTp, n + 1), s_xhi)

            def k_hi(n, half):
                hi(kT[:, 0, 2 * half:2 * half + 2].rearrange("p g s -> p (g s)"), bM[:, :], (s_kp, 2 * n + half + 1), s_khi)

            def v_hi(n, t):
                hi(v[:, 0, t], bM[:, :], (s_vp, 2 * n + t + 1), s_vhi)

            def q_hi(n, j):
                hi(qT[:, 0].rearrange("p h s -> p (h s)"), bQ[:, :], (s_qp, J * n + j + 1), s_qhi)

            def pT_hi(n, j):
                t = J * n + j
                hi(pT0[:, 0], bT0[:, :], (s_pTp, 2 * t + 1), s_pThi)
                hi(pT1[:, 0], bT1[:, 0:2 * P], (s_pTp, 2 * t + 2), s_pThi)

            def o_hi(n, j):
                hi(oT[:, j % 2, 0], bO[:, :], (s_op, J * n + j + 1), s_ohi)

            def exps(n, j):
                t = J * n + j
                act.wait_ge(s_nm, t + 1)
                for i in range(2):
                    for r, (a, b) in enumerate(((0, P), (P, 3 * P))):
                        m = act.activation(prob[:, j % 2, i, a:b], prob[:, j % 2, i, a:b], ACT.Exp, scale=SCALE,
                                           bias=negmax[:, 2 * i + r:2 * i + r + 1],
                                           accum_out=rowsum[:, 2 * i + r:2 * i + r + 1])
                m.then_inc(s_ex, 1)

            def batch(n, last):
                for j in range(J):
                    pT_hi(n, j)
                    if isinstance(n, int) and n == 0 and j + 2 < len(LATE):
                        late_hi(j + 2)
                    if j == 0 and isinstance(n, int) and n == 0:
                        act.wait_ge(s_rawt, 16)
                        act.activation(abs_w, raw_t, ACT.Abs, accum_out=abs_sum[:, 0:1]).then_inc(s_abs, 1)
                    if j == 0:
                        v_hi(n, 1)
                    if j in (5, 6) and not last:
                        k_hi(n + 1, j - 5)
                    if j < J - 3 or not last:
                        q_hi(*ahead(n, j, 3))
                    if j == 2 and not (isinstance(n, int) and n == 0):
                        ternary_hi(n - 1)
                    if j == 4:
                        linear_x_hi(0, 0) if last else x_hi(n + 1)
                    if last:
                        if j in (0, 3):
                            subtract_zero_point(GU0 if j == 0 else GU1)
                        if j in (1, 2):
                            if j == 1:
                                act.wait_ge(s_vp, 2 * NB)
                            late_layer_hi(IN0 if j == 1 else IN1)
                        if j == 4:
                            act.wait_ge(s_qp, J * NB - 2)
                            late_layer_hi(GU0)
                        if j == 7:
                            for i in (DOWN0, DOWN1):
                                late_layer_hi(i)
                        if j == 5:
                            linear_residual(0)
                            act.wait_ge(s_sp, 2 * J * NB)
                            act.activation(mean_rows, ones[:, :], ACT.Copy, scale=1.0 / P)
                            act.activation(v_bias[:, 0, :], b_in[:, 2 * D:3 * D], ACT.Copy).then_inc(s_bhi, 1)
                    if j == J - 1:
                        o_hi(n, j)
                    if j < J - 2 or not last:
                        exps(*ahead(n, j, 2))
                    if j < J - 1:
                        o_hi(n, j)
                    if j == 6 and last:
                        late_layer_hi(GU1)
                        linear_residual(1)
                        late_layer_hi(OUT)
                if not last:
                    v_hi(n + 1, 0)

            def late_layer_hi(n):
                src, (high, _), _ = LAYER_WEIGHTS[n]
                if n in (GU0, GU1):
                    act.wait_ge(s_zero, INTS.index(n) + 1)
                else:
                    act.wait_ge(s_rawl[LANDED[n][0]], LANDED[n][1])
                if n in (DOWN0, DOWN1):
                    act.activation(high, src.bitcast(I32), ACT.Copy, bias=-ZERO_POINT).then_inc(s_lwhi, 1)
                else:
                    act.activation(high, src, ACT.Copy).then_inc(s_lwhi, 1)

            def sum_lo(n):
                src, (_, low), rows = LAYER_WEIGHTS[n]
                i = INTS.index(n)
                act.activation(src, f32(low), ACT.Abs, accum_out=lo_sums[0:rows, i:i + 1]).then_inc(s_los, 1)

            def subtract_zero_point(n):
                src = LAYER_WEIGHTS[n][0]
                act.wait_ge(s_rawl[LANDED[n][0]], LANDED[n][1])
                act.activation(src, src.bitcast(I32), ACT.Copy, bias=-ZERO_POINT).then_inc(s_zero, 1)

            def ternary_hi(n):
                act.wait_ge(s_fT, n + 1)
                z = z_of(n)
                for k in range(KT):
                    m = act.activation(z[:, k * S:(k + 1) * S], ternary_bank(n)[:, k * S:(k + 1) * S], ACT.Identity,
                                       bias=gamma_beta[:, 1, k:k + 1], scale=gamma_beta[:, 0, k:k + 1])
                m.then_inc(s_fz, 1)
                act.wait_ge(s_fz, n + 1)
                act.activation(zT[:, 0].rearrange("p k s -> p (k s)"), z, ACT.Copy).then_inc(s_fhi, 1)

            def linear_x_hi(n, q):
                hi(xTs[q][:, 0].rearrange("p k s -> p (k s)"), bM[:, :], (s_lT, n + 1), s_lhi)

            def gated_x_hi(b, m=0, q=None):
                q = b if q is None else q
                act.wait_ge(s_gT, b + 1)
                act.activation(xT4[:, m, 0, :, q * S:(q + 1) * S], bM[:, :].rearrange("p (k s) -> p k s", k=KT),
                               ACT.Copy).then_inc(s_ghi, 1)

            def linear_residual(n):
                act.wait_ge(s_lrs, n + 1)
                for t in range(ST):
                    xs = x[:, bass.ds(ST * n + t, 1), :].rearrange("p o d -> p (o d)")
                    m = act.activation(xs, xs, ACT.Identity, bias=residual_scale[:, 1, t:t + 1],
                                       scale=residual_scale[:, 0, t:t + 1])
                m.then_inc(s_lres1, 1)

            def linear_squares(n, q):
                act.wait_ge(s_lr, ST * n + ST)
                for t in range(ST):
                    m = act.activation(k_square[:, t, :], qkv[:, q, t, D:2 * D], ACT.Square, accum_out=k_norm[:, t:t + 1])
                m.then_inc(s_lsq, 1)

            def linear_v(n, q, t):
                act.wait_ge(s_lp, ST * n + t + 1)
                if t == 0 and not (isinstance(n, int) and n < 2):
                    act.wait_ge(s_lkv, n - 1)
                act.activation(qkv[:, q, t, 2 * D:3 * D], v_bank(n, t), ACT.Copy).then_inc(s_lv, 1)

            def linear(n, q, qkv_on=True, out_on=True, next_on=True, norm_on=True):
                if qkv_on:
                    linear_v(n, q, 0)
                if isinstance(n, int) and n == NB:
                    gated_x_hi(1)
                if out_on:
                    hi(yT[:, 0].rearrange("p k s -> p (k s)"), bO[:, :], (s_lyT, n - 1), s_lyhi)
                if next_on:
                    linear_x_hi(n + 1, 1 - q)
                elif n < NB:
                    gated_x_hi(0)
                if qkv_on:
                    linear_v(n, q, 1)
                if isinstance(n, int) and n == 1:
                    act.wait_ge(s_gwlo, 1)
                    sum_lo(GU0)
                    sum_lo(GU1)
                    ternary_hi(NB - 1)
                if isinstance(n, int) and n == NB - 2:
                    act.wait_ge(s_dwlo, 1)
                    sum_lo(DOWN0)
                    sum_lo(DOWN1)
                if qkv_on:
                    linear_squares(n, q)
                if norm_on:
                    linear_residual(n + 2)

            bG = (bS0, bS1)

            def gated_tile(m, i):
                u = HT * m + i
                rows = P if i < HT - 1 else HLAST
                act.wait_ge(s_gg, u + 1)
                if not (isinstance(m, int) and m == 0 and i == 0):
                    act.wait_ge(s_gh, u)
                act.activation(gate[0:rows, :], bG[i % 2][0:rows, :], ACT.Silu, scale=s_gu[0:rows, 0, i:i + 1]).then_inc(s_gs, 1)
                act.wait_ge(s_gh, u + 1)
                act.activation(hT[i % 3][0:rows, 0], hidden[i % 2][0:rows, :], ACT.Copy).then_inc(s_ghh, 1)

            def gated(m, first, last):
                for i in range(HT):
                    if not (first and i == 0):
                        gated_tile(m, i)
                    if i in (2, 4) and not last:
                        gated_x_hi(2 * m + 1 + i // 2, m + 1, i // 2 - 1)

            early(0)
            x_hi(0)
            early(1)
            k_hi(0, 0)
            q_hi(0, 0)
            early(2)
            k_hi(0, 1)
            early(3)
            q_hi(0, 1)
            late_hi(0)
            exps(0, 0)
            late_hi(1)
            q_hi(0, 2)
            exps(0, 1)
            v_hi(0, 0)
            batch(0, False)
            act.wait_ge(s_tab, 16 * 5)
            with act.Fori(1, NB - 1) as n:
                batch(n, False)
            batch(NB - 1, True)

            linear_v(0, 0, 0)
            linear_v(0, 0, 1)
            linear_x_hi(1, 1)
            linear_squares(0, 0)
            linear_residual(2)
            linear(1, 1, out_on=False)
            with act.Fori(1, NB // 2 - 1) as m:
                for q in range(2):
                    linear(2 * m + q, q)
            linear(NB - 2, 0, norm_on=False)
            linear(NB - 1, 1, next_on=False, norm_on=False)
            linear(NB, 0, qkv_on=False, next_on=False, norm_on=False)
            gated_tile(0, 0)
            linear(NB + 1, 1, qkv_on=False, next_on=False, norm_on=False)

            gated(0, True, False)
            with act.Fori(1, NB // 2 - 1) as m:
                gated(m, False, False)
            gated(NB // 2 - 1, False, True)

        @block.vector
        def _(dve):
            def x_tile(b, t):
                return x[:, bass.ds(ST * b + t, 1), :].rearrange("p o d -> p (o d)")

            def ln_moments(call, b):
                for t in range(ST):
                    m = dve.bn_stats(stats[:, t, :], x_tile(b, t))
                m.then_inc(s_st, 1)
                wait_apart(dve, s_st, call + 1)
                for t in range(ST):
                    m = dve.bn_aggr(moments[:, t, :], stats[:, t, :])
                m.then_inc(s_mo, 1)

            def ln_apply(call, b):
                dve.wait_ge(s_mo, call + 1)
                dve.wait_ge(s_rs, call + 1)
                for t in range(ST):
                    m = dve.tensor_scalar(xn[:, t, :], x_tile(b, t), moments[:, t, 0:1], rstd[:, t:t + 1],
                                          ALU.subtract, ALU.mult)
                return m

            def lo(out, src, hi, waits, done):
                dve.wait_ge(*waits)
                dve.tensor_tensor(out, src, f32(hi), ALU.subtract).then_inc(done, 1)

            def early(i):
                n = CHUNKS.index(EARLY[i])
                hi, low = chunk_parts(EARLY[i])[1]
                dve.wait_ge(s_raw[n], 16)
                lo(low, raw[:, n % NRAW, :], hi, (s_whi, i + 1), s_wsplit)

            def x_apply(n):
                if not (isinstance(n, int) and n == 0):
                    dve.wait_ge(s_xTp, n)
                ln_apply(n, n).then_inc(s_xn, 1)

            def x_lo(n):
                lo(xT[:, 1].rearrange("p k s -> p (k s)"), bM[:, :], xT[:, 0].rearrange("p k s -> p (k s)"),
                   (s_xhi, n + 1), s_xlo)

            def k_lo(n, half):
                part = [kT[:, a, 2 * half:2 * half + 2].rearrange("p g s -> p (g s)") for a in range(2)]
                lo(part[1], bM[:, :], part[0], (s_khi, 2 * n + half + 1), s_klo)

            def v_lo(n, t):
                lo(v[:, 1, t], bM[:, :], v[:, 0, t], (s_vhi, 2 * n + t + 1), s_vlo)

            def q_lo(n, j):
                part = [qT[:, a].rearrange("p h s -> p (h s)") for a in range(2)]
                lo(part[1], bQ[:, :], part[0], (s_qhi, J * n + j + 1), s_qlo)

            def pT_lo(n, j, part):
                pT, src = ((pT0, bT0[:, :]), (pT1, bT1[:, 0:2 * P]))[part]
                lo(pT[:, 1], src, pT[:, 0], (s_pThi, 2 * (J * n + j) + part + 1), s_pTlo)

            def o_lo(n, j):
                lo(oT[:, j % 2, 1], bO[:, :], oT[:, j % 2, 0], (s_ohi, J * n + j + 1), s_olo)

            def row_max(n, j):
                t = J * n + j
                halves = bS0[:, :].rearrange("p (i b n) -> p i b n", i=2, b=2)
                wait_apart(dve, s_sp, 2 * t + 1)
                diagonal = mask[:, P:2 * P].rearrange("p (o n) -> p o n", o=1).to_broadcast([P, 2, P])
                dve.tensor_tensor(prob[:, j % 2, :, 0:P], halves[:, :, 0], diagonal, ALU.add).then_inc(s_sc, 1)

                def sum_and_max(i, r, src, other):
                    a, b = ((0, P), (P, 3 * P))[r]
                    return dve.tensor_tensor_reduce(prob[:, j % 2, i, a:b], src, other, 1.0, MASKED,
                                                    ALU.add, ALU.max, rowmax[:, 2 * i + r:2 * i + r + 1])

                wait_apart(dve, s_sp, 2 * t + 2)
                for i in range(2):
                    m = sum_and_max(i, 1, bS1[:, i * S:(i + 1) * S], mask[:, :])
                m.then_inc(s_mx, 1)
                wait_apart(dve, s_sc, t + 1)
                for i in range(2):
                    m = sum_and_max(i, 0, halves[:, i, 1], prob[:, j % 2, i, 0:P])
                m.then_inc(s_mx, 1)
                dve.wait_ge(s_mx, 2 * t + 2)
                dve.tensor_scalar(negmax[:, :], rowmax[:, :], -SCALE, None, ALU.mult).then_inc(s_nm, 1)

            def normalise(n, j):
                t = J * n + j
                dve.wait_ge(s_ex, t + 1)
                dve.reciprocal(rowinv[:, j % 2, :], rowsum[:, :]).then_inc(s_ri, 1)
                dve.wait_ge(s_ri, t + 1)
                for r, (a, b) in enumerate(((0, P), (P, 3 * P))):
                    m = dve.tensor_scalar(prob[:, j % 2, 1, a:b], prob[:, j % 2, 1, a:b],
                                          rowinv[:, j % 2, 2 + r:3 + r], None, ALU.mult)
                m.then_inc(s_pn1, 1)

            def add_y(n):
                dve.wait_ge(s_yp, n + 1)
                xs = x[:, bass.ds(ST * n, ST), :].rearrange("p t d -> p (t d)")
                dve.tensor_tensor(xs, bY[:, :], xs, ALU.add).then_inc(s_ya, 1)

            def batch(n, last):
                for j in range(J):
                    pT_lo(n, j, 0)
                    pT_lo(n, j, 1)
                    if j < J - 2 or not last:
                        row_max(*ahead(n, j, 2))
                    if j == 0:
                        v_lo(n, 1)
                    if j in (5, 6) and not last:
                        k_lo(n + 1, j - 5)
                    if j < J - 3 or not last:
                        q_lo(*ahead(n, j, 3))
                    if not (isinstance(n, int) and n == 0):
                        if j == 1:
                            ternary_apply(n - 1)
                        if j == 2:
                            ternary_lo(n - 1)
                        if j == 3:
                            add_bank(n - 1, bM, s_fp, s_fb, s_fa)
                    if j == 4:
                        linear_x_lo(0, 0) if last else x_lo(n + 1)
                    if j == 0 and not (isinstance(n, int) and n == 0):
                        ternary_moments(n - 1)
                    if j == 2 and not last:
                        if isinstance(n, int):
                            dve.wait_ge(s_x[n + 1], 16)
                        ln_moments(n + 1, n + 1)
                    if j == 3 and not last:
                        x_apply(n + 1)
                    if isinstance(n, int) and n == 0 and j >= 3:
                        ternary_weights(j - 3)
                    if last:
                        if j == 2:
                            ln_moments(NB, 0)
                        if j == 3:
                            linear_apply(0)
                        if j == 4:
                            late_layer_lo(IN0)
                        if j == 5:
                            dve.wait_ge(s_lrs, 1)
                            ln_moments(NB + 1, 1)
                            late_layer_lo(IN1)
                        if j == 6:
                            lo(v_bias[:, 1, :], b_in[:, 2 * D:3 * D], v_bias[:, 0, :], (s_bhi, 1), s_blo)
                            linear_apply(1)
                        if j == 7:
                            linear_qkv(0, 0, 0)
                    if j == J - 1:
                        o_lo(n, j)
                    if j < J - 2 or not last:
                        normalise(*ahead(n, j, 2))
                    if j < J - 1:
                        o_lo(n, j)
                    if j == 6 and last:
                        late_layer_lo(OUT)
                if not last:
                    v_lo(n + 1, 0)
                    add_y(n)

            def ternary_weights(part):
                if part == 0:
                    dve.wait_ge(s_absp, 1)
                    dve.tensor_scalar(scale_eps[:, :], bM[:, 0:1], 1.0 / (D * D), EPS, ALU.mult, ALU.add).then_inc(s_half, 1)
                    dve.wait_ge(s_half, 1)
                    dve.tensor_scalar(half_scale[:, 0:1], scale_eps[:, :], 0.5, None, ALU.mult)
                    dve.tensor_scalar(half_scale[:, 1:2], scale_eps[:, :], -0.5, None, ALU.mult).then_inc(s_half, 1)
                if part == 1:
                    dve.wait_ge(s_half, 2)
                    dve.tensor_scalar(ternary_pos[:, :], raw_t, half_scale[:, 0:1], None, ALU.is_gt).then_inc(s_tpos, 1)
                if part == 2:
                    dve.wait_ge(s_tpos, 1)
                    dve.scalar_tensor_tensor(ternary_neg[:, :], raw_t, half_scale[:, 1:2], ternary_pos[:, :], ALU.is_lt,
                                             ALU.subtract).then_inc(s_tpos, 1)
                if part == 3:
                    dve.wait_ge(s_tpos, 2)
                    dve.tensor_scalar(tern.rearrange("p k n -> p (k n)"), ternary_neg[:, :], -1.0, None, ALU.mult).then_inc(s_tern, 1)

            def late_layer_lo(n):
                src, (high, low), _ = LAYER_WEIGHTS[n]
                lo(low, src, high, (s_lwhi, n + 1), s_lwlo)

            def ternary_moments(n):
                wait_apart(dve, s_ya, n + 1)
                for t in range(ST):
                    m = dve.bn_stats(t_stats[:, t, :], x_tile(n, t))
                m.then_inc(s_fst, 1)
                wait_apart(dve, s_fst, n + 1)
                for t in range(ST):
                    m = dve.bn_aggr(t_moments[:, t, :], t_stats[:, t, :])
                m.then_inc(s_fmo, 1)
                dve.wait_ge(s_fmo, n + 1)
                dve.tensor_scalar(t_variance[:, :], t_moments[:, :, 1], 1.0 + EPS, EPS * EPS, ALU.mult, ALU.add).then_inc(s_fvar, 1)

            def ternary_apply(n):
                dve.wait_ge(s_frs, n + 1)
                for t in range(ST):
                    m = dve.tensor_scalar(txn[:, t, :], x_tile(n, t), t_moments[:, t, 0:1], t_rstd[:, t:t + 1],
                                          ALU.subtract, ALU.mult)
                m.then_inc(s_fn, 1)

            def ternary_lo(n):
                lo(zT[:, 1].rearrange("p k s -> p (k s)"), z_of(n), zT[:, 0].rearrange("p k s -> p (k s)"), (s_fhi, n + 1), s_flo)

            def add_bank(n, out_bank, out_ready, residual_ready, done):
                dve.wait_ge(out_ready, n + 1)
                dve.wait_ge(residual_ready, n + 1)
                xs = x[:, bass.ds(ST * n, ST), :].rearrange("p t d -> p (t d)")
                dve.tensor_tensor(xs, out_bank[:, :], xs, ALU.add).then_inc(done, 1)

            def linear_apply(n):
                if isinstance(n, int) and n == 0:
                    dve.wait_ge(s_xTp, NB)
                else:
                    dve.wait_ge(s_lT, n)
                    dve.wait_ge(s_lres1, n)
                ln_apply(NB + n, n).then_inc(s_ln, 1)
                dve.tensor_scalar(residual_scale[:, 0, :], rstd[:, :], 1.0, None, ALU.add)
                dve.scalar_tensor_tensor(residual_scale[:, 1, :], moments[:, :, 0], -1.0, rstd[:, :], ALU.mult,
                                         ALU.mult).then_inc(s_lrs, 1)

            def linear_x_lo(n, q):
                lo(xTs[q][:, 1].rearrange("p k s -> p (k s)"), bM[:, :], xTs[q][:, 0].rearrange("p k s -> p (k s)"), (s_lhi, n + 1), s_llo)

            def linear_qkv(n, q, t):
                dve.wait_ge(s_lp, ST * n + t + 1)
                if t == 0 and not (isinstance(n, int) and n < 2):
                    dve.wait_ge(s_lY, n - 1)
                u = ST * n + t
                dve.tensor_tensor(qkv[:, q, t, 0:2 * D], bQK[t][:, :], b_in[:, 0:2 * D], ALU.add).then_inc(s_le, 1)
                dve.wait_ge(s_le, u + 1)
                if not (isinstance(n, int) and n == 0):
                    dve.wait_ge(s_lr, u - 1)
                qk = qkv[:, q, t, 0:2 * D].rearrange("p (c d) -> p c d", c=2)[:, :, 0:P]
                dve.tensor_tensor(rot1[:, t], qk, rope[:, 0, t], ALU.mult).then_inc(s_lc, 1)

            def linear_kv(n, q):
                dve.wait_ge(s_lki, n + 1)
                if not (isinstance(n, int) and n == 0):
                    dve.wait_ge(s_lA, n)
                for t in range(ST):
                    m = dve.scalar_tensor_tensor(kv[:, t, :], qkv[:, q, t, D:2 * D], k_inv[:, t:t + 1],
                                                 qkv[:, q, t, 2 * D:3 * D], ALU.mult, ALU.mult)
                m.then_inc(s_lkv, 1)

            def linear_y(n, q):
                dve.wait_ge(s_lA, n + 1)
                if isinstance(n, int) and n == 0:
                    dve.wait_ge(s_fT, NB)
                for t in range(ST):
                    m = dve.tensor_tensor(y[:, t, :], bQ[:, 0:D], qkv[:, q, t, 0:D], ALU.mult)
                m.then_inc(s_lY, 1)

            def linear(n, q, qkv_on=True, sum_on=True, out_on=True, next_on=True, norm_on=True):
                if qkv_on:
                    linear_qkv(n, q, 0)
                if isinstance(n, int) and n == NB:
                    gated_x_lo(1)
                if sum_on:
                    linear_kv(n - 1, 1 - q)
                if isinstance(n, int) and n == NB:
                    dve.wait_ge(s_gn, 2)
                    ln_moments(2 * NB + 2, 2)
                if out_on:
                    part = [yT[:, a].rearrange("p k s -> p (k s)") for a in range(2)]
                    lo(part[1], bO[:, :], part[0], (s_lyhi, n - 1), s_lylo)
                if norm_on:
                    ln_moments(NB + 2 + n, n + 2)
                elif n < NB:
                    ln_moments(NB + 2 + n, n + 2 - NB)
                if next_on:
                    linear_x_lo(n + 1, 1 - q)
                elif n < NB:
                    gated_x_lo(0)
                if qkv_on:
                    linear_qkv(n, q, 1)
                if isinstance(n, int) and n == 1:
                    ternary_apply(NB - 1)
                if sum_on and not (isinstance(n, int) and n == 1):
                    linear_y(n - 1, 1 - q)
                if norm_on:
                    linear_apply(n + 2)
                elif n < NB:
                    gated_apply(n + 2 - NB)
                if isinstance(n, int) and n == 1:
                    linear_y(0, 0)
                if isinstance(n, int) and n >= NB:
                    hidden_tile(0, n - NB)
                    if n > NB:
                        gated_apply(2)
                if isinstance(n, int) and n > NB:
                    hidden_lo(0, 0)
                if out_on:
                    add_bank(n - 2, bY, s_lo, s_lres, s_la)

            def gated_apply(b):
                if isinstance(b, int) and b == 0:
                    dve.wait_ge(s_lT, NB)
                else:
                    dve.wait_ge(s_gT, b)
                ln_apply(2 * NB + b, b).then_inc(s_gn, 1)

            def gated_x_lo(b, m=0, q=None):
                q = b if q is None else q
                dve.wait_ge(s_ghi, b + 1)
                dve.tensor_tensor(xT4[:, m, 1, :, q * S:(q + 1) * S], bM[:, :].rearrange("p (k s) -> p k s", k=KT),
                                  f32(xT4[:, m, 0, :, q * S:(q + 1) * S]), ALU.subtract).then_inc(s_glo, 1)

            def hidden_tile(m, i):
                u = HT * m + i
                rows = P if i < HT - 1 else HLAST
                dve.wait_ge(s_gu_, u + 1)
                dve.wait_ge(s_gs, u + 1)
                if not (isinstance(m, int) and m == 0 and i < 2):
                    dve.wait_ge(s_ghl, u - 1)
                dve.scalar_tensor_tensor(hidden[i % 2][0:rows, :], bU[i % 2][0:rows, :], s_gu[0:rows, 1, i:i + 1],
                                         gate[0:rows, :], ALU.mult, ALU.mult).then_inc(s_gh, 1)

            def hidden_lo(m, i):
                rows = P if i < HT - 1 else HLAST
                dve.wait_ge(s_ghh, HT * m + i + 1)
                dve.tensor_tensor(hT[i % 3][0:rows, 1], hidden[i % 2][0:rows, :], f32(hT[i % 3][0:rows, 0]),
                                  ALU.subtract).then_inc(s_ghl, 1)

            def scale_down(b, q):
                dve.wait_ge(s_gd, b + 1)
                dve.wait_ge(s_ga, b + 1)
                for t in range(ST):
                    m = dve.tensor_tensor(scaled[q][:, t, :], bD[q][:, t * D:(t + 1) * D], biases[:, 2, :], ALU.mult)
                m.then_inc(s_gsc, 1)

            def gated(m, first, last):
                for i in range(HT):
                    if not (first and i < 2):
                        hidden_tile(m, i)
                    if i == 1 and not first:
                        scale_down(2 * m - 2, 0)
                    if i == 3 and not last:
                        gated_x_lo(2 * m + 2, m + 1, 0)
                    if i > 0:
                        if not (first and i == 1):
                            hidden_lo(m, i - 1)
                    elif not first:
                        hidden_lo(m - 1, HT - 1)
                    if i == 1 and not first:
                        scale_down(2 * m - 1, 1)
                    if not last:
                        if i == 4:
                            gated_x_lo(2 * m + 3, m + 1, 1)
                        if i in (1, 3) and not (first and i == 1):
                            gated_apply(2 * m + 2 + i // 2)
                        if i == 2:
                            dve.wait_ge(s_gn, 2 * m + 3)
                        if i in (0, 2) and not (first and i == 0):
                            ln_moments(2 * NB + 2 * m + 2 + i // 2, 2 * m + 2 + i // 2)

            bQK, bU, bD = (bS0, bS1), (bT0, bT1), (bQ, bO)
            dve.wait_ge(s_const, 4)
            dve.wait_ge(s_x[0], 16)
            ln_moments(0, 0)
            x_apply(0)
            early(0)
            x_lo(0)
            early(1)
            k_lo(0, 0)
            q_lo(0, 0)
            early(2)
            k_lo(0, 1)
            row_max(0, 0)
            q_lo(0, 1)
            early(3)
            normalise(0, 0)
            row_max(0, 1)
            q_lo(0, 2)
            normalise(0, 1)
            v_lo(0, 0)
            batch(0, False)
            dve.wait_ge(s_tab, 16 * 5)
            for b in range(2, NB):
                dve.wait_ge(s_x[b], 16)
            with dve.Fori(1, NB - 1) as n:
                batch(n, False)
            batch(NB - 1, True)

            dve.wait_ge(s_lrs, 2)
            ln_moments(NB + 2, 2)
            linear_qkv(0, 0, 1)
            linear_x_lo(1, 1)
            add_y(NB - 1)
            ternary_moments(NB - 1)
            linear_apply(2)
            linear(1, 1, out_on=False)
            ternary_lo(NB - 1)
            for n in (DOWN0, DOWN1):
                src, (high, low), _ = LAYER_WEIGHTS[n]
                dve.wait_ge(s_lwhi, n + 1)
                m = dve.scalar_tensor_tensor(low, src.bitcast(I32), -ZERO_POINT, f32(high), ALU.add, ALU.subtract)
            m.then_inc(s_dwlo, 1)
            add_bank(NB - 1, bY, s_fp, s_fb, s_fa)
            with dve.Fori(1, NB // 2 - 1) as m:
                for q in range(2):
                    linear(2 * m + q, q)
            linear(NB - 2, 0, norm_on=False)
            dve.wait_ge(s_lop, 1)
            dve.tensor_reduce(lo_sum[:, :], bM[:, 0:4], AX.X, ALU.add).then_inc(s_lor, 1)
            dve.wait_ge(s_lor, 1)
            dve.tensor_scalar(lo_flag[:, :], lo_sum[:, :], 0.0, None, ALU.is_gt).then_inc(s_flag, 1)
            linear(NB - 1, 1, norm_on=False, next_on=False)
            linear(NB, 0, qkv_on=False, next_on=False, norm_on=False)
            linear(NB + 1, 1, qkv_on=False, sum_on=False, next_on=False, norm_on=False)

            gated(0, True, False)
            with dve.Fori(1, NB // 2 - 1) as m:
                gated(m, False, False)
            gated(NB // 2 - 1, False, True)
            hidden_lo(NB // 2 - 1, HT - 1)
            for q in range(2):
                b = NB - 2 + q
                scale_down(b, q)
                dve.wait_ge(s_gsc, b + 1)
                xs = x[:, ST * b:ST * (b + 1), :]
                dve.tensor_tensor(xs, xs, scaled[q][:, :, :], ALU.add).then_inc(s_gl, 1)


def kernel(**inputs):
    import concourse.bacc as bacc
    from concourse.bass_utils import run_bass_kernel_spmd

    def tiles(w):
        return w.reshape(-1, P, w.shape[1]).transpose(1, 0, 2)

    def rows(*vectors):
        return np.ascontiguousarray(np.stack([np.broadcast_to(r, (P, r.shape[-1])) for r in vectors], 1))

    w = {k: np.asarray(a) for k, a in inputs.items()}
    qkv = w["L0_attn_weight_qkv"].reshape(NG, HEADS_PER_GROUP + 2, DH, D)
    proj = w["L0_attn_weight_proj"].T.reshape(4, 4, DH, D)
    last = {k: w[k].T for k in ("L1_ffn_wq_gate", "L1_ffn_wq_up", "L1_ffn_wq_down")}
    inv_freq = np.float32(1.0) / np.float32(10000.0) ** (np.arange(0, P, 2, dtype=np.float32) / np.float32(P))
    angle = np.repeat(np.arange(S, dtype=np.float32)[:, None] * inv_freq[None, :], 2, axis=1).reshape(ST, P, P)
    sign = np.where(np.arange(P) % 2 == 0, np.float32(-1.0), np.float32(1.0))
    rope = np.stack([np.cos(angle), np.sin(angle) * sign]).astype(np.float32)
    hid = np.zeros((2, HT * P), np.float32)
    hid[0, :HID], hid[1, :HID] = w["L1_ffn_s_gate"], w["L1_ffn_s_up"]
    arrays = {
        "x": w["L0_attn_x"],
        "wk": tiles(qkv[:, HEADS_PER_GROUP].reshape(NG * DH, D).T),
        "wv": tiles(qkv[:, HEADS_PER_GROUP + 1].reshape(NG * DH, D).T),
        "wq": np.stack([tiles(qkv[g, :HEADS_PER_GROUP].reshape(-1, D).T) for g in range(NG)]),
        "wp": proj.transpose(0, 2, 1, 3),
        "wt": tiles(w["L0_ffn_weight"].T),
        "gamma_beta": np.stack([w["L0_ffn_ln_gamma"].reshape(KT, P), w["L0_ffn_ln_beta"].reshape(KT, P)]).transpose(2, 0, 1),
        "biases": rows(w["L0_ffn_bias"], w["L1_attn_b_out"], w["L1_ffn_s_down"]),
        "b_in": rows(w["L1_attn_b_in"]),
        "w_in": tiles(w["L1_attn_W_in"].T),
        "w_out": tiles(w["L1_attn_W_out"].T),
        "w_gu": np.stack([tiles(last["L1_ffn_wq_gate"]), tiles(last["L1_ffn_wq_up"])], 1),
        "s_gu": hid.reshape(2, HT, P).transpose(2, 0, 1),
        "w_down": last["L1_ffn_wq_down"],
        "rope": np.repeat(rope.transpose(2, 0, 1, 3)[:, :, :, None], 2, axis=3),
    }
    flat = {"wk", "wv", "wt", "w_in", "w_out", "w_gu", "b_in"}
    nc = bacc.Bacc("TRN2", target_bir_lowering=False, num_devices=1)
    aps = []
    for name, a in arrays.items():
        if name in flat:
            a = a.reshape(P, -1)
        if name in ("wq", "wp"):
            a = a.reshape(4, P, -1)
        arrays[name] = a = np.ascontiguousarray(a)
        aps.append(nc.dram_tensor("in_" + name, a.shape, mybir.dt.from_np(a.dtype), kind="ExternalInput").ap())
    out = nc.dram_tensor("out", (NB, S, D), F32, kind="ExternalOutput").ap()
    build(nc, *aps, out)
    return run_bass_kernel_spmd(nc, [{"in_" + k: a for k, a in arrays.items()}], core_ids=[0]).results[0]["out"]
```
